# Optimizing a Trainium2 kernel written in Bass

```python
import numpy as np
import jax
import jax.numpy as jnp

def _softmax(x, axis=-1):
    return jax.nn.softmax(x, axis=axis)

def _gelu(x):
    return jax.nn.gelu(x, approximate=True)

def _silu(x):
    return jax.nn.silu(x)

def _sigmoid(x):
    return jax.nn.sigmoid(x)

def _layernorm(x, axis=-1, eps=1e-05):
    m = jnp.mean(x, axis=axis, keepdims=True)
    v = jnp.var(x, axis=axis, keepdims=True)
    return (x - m) / jnp.sqrt(v + eps)

def _scatter_add(tgt, idx, src, axis=0):
    return tgt.at[idx].add(src)

def _segment_sum(src, seg, n):
    return jax.ops.segment_sum(src, seg, n)
kernel_name = 'mk_seq_preln_d2_jaxref_r8_2e0dbc'

def setup_inputs(seed: int=0):
    np.random.seed(seed)
    _w = jnp.asarray

    def _L0_attn_setup():
        import jax, jax.numpy as jnp
        import numpy as np
        B, S, D, H = (2, 256, 128, 16)
        HD = D // H
        MAX_BIAS = 8.0

        def _alibi_bias(T, Sk, dtype):
            slopes = (2.0 ** (-MAX_BIAS / H)) ** jnp.arange(1, H + 1, dtype=dtype)
            qpos = jnp.arange(T)[:, None]
            kpos = jnp.arange(Sk)[None, :]
            rel = -jnp.abs(kpos - qpos).astype(dtype)
            return slopes[:, None, None] * rel[None]
        key = jax.random.key(seed)
        ks = jax.random.split(key, 5)
        sc = 1.0 / np.sqrt(D)
        return {'x': jax.random.normal(ks[0], (B, S, D), jnp.float32), 'Wq': jax.random.normal(ks[1], (D, D), jnp.float32) * sc, 'bq': jnp.zeros((D,), jnp.float32), 'Wk': jax.random.normal(ks[2], (D, D), jnp.float32) * sc, 'bk': jnp.zeros((D,), jnp.float32), 'Wv': jax.random.normal(ks[3], (D, D), jnp.float32) * sc, 'bv': jnp.zeros((D,), jnp.float32), 'Wo': jax.random.normal(ks[4], (D, D), jnp.float32) * sc, 'bo': jnp.zeros((D,), jnp.float32)}
    _L0_attn_in = _L0_attn_setup()

    def _L0_ffn_setup():
        import jax, jax.numpy as jnp
        import numpy as np
        key = jax.random.key(seed)
        ks = jax.random.split(key, 5)
        B, T, D, E = (4, 256, 128, 8)
        inputs = jax.random.normal(ks[0], (B, T, D), dtype=jnp.float32)
        Wr = jax.random.normal(ks[1], (D, E), dtype=jnp.float32) * 0.02
        br = jnp.zeros((E,), dtype=jnp.float32)
        W1 = jax.random.normal(ks[2], (E, D, D), dtype=jnp.float32) * 0.02
        b1 = jnp.zeros((E, D), dtype=jnp.float32)
        W2 = jax.random.normal(ks[3], (E, D, D), dtype=jnp.float32) * 0.02
        b2 = jnp.zeros((E, D), dtype=jnp.float32)
        return {'inputs': inputs, 'Wr': Wr, 'br': br, 'W1': W1, 'b1': b1, 'W2': W2, 'b2': b2}
    _L0_ffn_in = _L0_ffn_setup()

    def _L1_attn_setup():
        import jax, jax.numpy as jnp
        import numpy as np
        SEQ, BATCH, DIM = (256, 8, 128)
        key = jax.random.key(seed)
        k1, k2, k3 = jax.random.split(key, 3)
        x = jax.random.normal(k1, (SEQ, BATCH, DIM), dtype=jnp.float32)
        Wq = jax.random.normal(k2, (DIM, DIM), dtype=jnp.float32) * DIM ** (-0.5)
        Wk = jax.random.normal(k3, (DIM, DIM), dtype=jnp.float32) * DIM ** (-0.5)
        return {'x': x, 'Wq': Wq, 'Wk': Wk}
    _L1_attn_in = _L1_attn_setup()

    def _L1_ffn_setup():
        import jax, jax.numpy as jnp
        import numpy as np
        R = 64
        key = jax.random.key(seed)
        k1, k2, k3 = jax.random.split(key, 3)
        B, S, D_IN, D_OUT = (8, 512, 128, 128)
        x = jax.random.normal(k1, (B, S, D_IN), dtype=jnp.float32)
        weight = jax.random.normal(k2, (D_OUT, D_IN), dtype=jnp.float32) * (1.0 / np.sqrt(D_IN))
        disha = jax.random.normal(k3, (R, D_OUT), dtype=jnp.float32) * 0.01
        return {'x': x, 'weight': weight, 'disha': disha}
    _L1_ffn_in = _L1_ffn_setup()
    _d = {'L0_attn_x': _L0_attn_in['x'], 'L0_attn_Wq': _L0_attn_in['Wq'], 'L0_attn_bq': _L0_attn_in['bq'], 'L0_attn_Wk': _L0_attn_in['Wk'], 'L0_attn_bk': _L0_attn_in['bk'], 'L0_attn_Wv': _L0_attn_in['Wv'], 'L0_attn_bv': _L0_attn_in['bv'], 'L0_attn_Wo': _L0_attn_in['Wo'], 'L0_attn_bo': _L0_attn_in['bo'], 'L0_ffn_Wr': _L0_ffn_in['Wr'], 'L0_ffn_br': _L0_ffn_in['br'], 'L0_ffn_W1': _L0_ffn_in['W1'], 'L0_ffn_b1': _L0_ffn_in['b1'], 'L0_ffn_W2': _L0_ffn_in['W2'], 'L0_ffn_b2': _L0_ffn_in['b2'], 'L1_attn_Wq': _L1_attn_in['Wq'], 'L1_attn_Wk': _L1_attn_in['Wk'], 'L1_ffn_weight': _L1_ffn_in['weight'], 'L1_ffn_disha': _L1_ffn_in['disha']}
    _x0 = _d['L0_attn_x']
    _d['L0_attn_x'] = jax.random.normal(jax.random.fold_in(jax.random.key(seed), 1), (4, 1024, 128), dtype=_x0.dtype)
    del _x0
    return _d

def reference(L0_attn_x, L0_attn_Wq, L0_attn_bq, L0_attn_Wk, L0_attn_bk, L0_attn_Wv, L0_attn_bv, L0_attn_Wo, L0_attn_bo, L0_ffn_Wr, L0_ffn_br, L0_ffn_W1, L0_ffn_b1, L0_ffn_W2, L0_ffn_b2, L1_attn_Wq, L1_attn_Wk, L1_ffn_weight, L1_ffn_disha):

    def _L0_attn_ref(x, Wq, bq, Wk, bk, Wv, bv, Wo, bo):
        import jax, jax.numpy as jnp
        import numpy as np
        B, S, D, H = (2, 256, 128, 16)
        HD = D // H
        MAX_BIAS = 8.0

        def _alibi_bias(T, Sk, dtype):
            slopes = (2.0 ** (-MAX_BIAS / H)) ** jnp.arange(1, H + 1, dtype=dtype)
            qpos = jnp.arange(T)[:, None]
            kpos = jnp.arange(Sk)[None, :]
            rel = -jnp.abs(kpos - qpos).astype(dtype)
            return slopes[:, None, None] * rel[None]
        Bb, Ss, Dd = x.shape
        q = (x @ Wq + bq).reshape(Bb, Ss, H, HD)
        k = (x @ Wk + bk).reshape(Bb, Ss, H, HD)
        v = (x @ Wv + bv).reshape(Bb, Ss, H, HD)
        scores = jnp.einsum('bthd,bshd->bhts', q, k) / jnp.sqrt(jnp.asarray(HD, x.dtype))
        alibi = _alibi_bias(Ss, Ss, x.dtype)
        causal = jnp.triu(jnp.ones((Ss, Ss), bool), 1)
        scores = scores + alibi[None]
        scores = jnp.where(causal[None, None], -jnp.inf, scores)
        attn = jax.nn.softmax(scores, axis=-1)
        out = jnp.einsum('bhts,bshd->bthd', attn, v).reshape(Bb, Ss, Dd)
        return out @ Wo + bo

    def _L0_ffn_ref(inputs, Wr, br, W1, b1, W2, b2):
        import jax, jax.numpy as jnp
        import numpy as np
        B, T, D = inputs.shape
        E = Wr.shape[1]
        x = inputs.reshape(B * T, D)
        N = x.shape[0]
        C = N // E
        logits = x @ Wr + br
        probs = jax.nn.softmax(logits, axis=-1)
        gate = jnp.max(probs, axis=-1, keepdims=True)
        idx = jnp.argmax(probs, axis=-1)
        mask = jax.nn.one_hot(idx, E, dtype=jnp.float32)
        pos = (jnp.cumsum(mask, axis=0) * mask).astype(jnp.int32)
        mask = mask * (pos < C).astype(jnp.float32)
        mask_flat = jnp.sum(mask, axis=-1, keepdims=True)
        gate = gate * mask_flat
        combine = (gate * mask_flat * jax.nn.one_hot(idx, E, dtype=jnp.float32))[..., None] * jax.nn.one_hot(pos, C, dtype=jnp.float32)
        dispatch = combine
        expert_in = jnp.einsum('nd,nec->ecd', x, dispatch)
        h = jax.nn.relu(jnp.einsum('ecd,edf->ecf', expert_in, W1) + b1[:, None, :])
        eo = jnp.einsum('ecf,efd->ecd', h, W2) + b2[:, None, :]
        out = jnp.einsum('ecd,nec->nd', eo, combine)
        return out.reshape(B, T, D)

    def _L1_attn_ref(x, Wq, Wk):
        import jax, jax.numpy as jnp
        import numpy as np
        SEQ, BATCH, DIM = (256, 8, 128)
        q = jnp.einsum('sbd,ed->sbe', x, Wq)
        k = jnp.einsum('sbd,ed->sbe', x, Wk)
        scale = jnp.asarray(x.shape[2], x.dtype) ** 0.5
        scores = jnp.einsum('sbd,tbd->bst', q, k) / scale
        align = jax.nn.softmax(jnp.tanh(scores), axis=2)
        out = jnp.einsum('bst,tbd->sbd', align, x)
        return out

    def _L1_ffn_ref(x, weight, disha):
        import jax, jax.numpy as jnp
        import numpy as np
        R = 64
        result = jnp.einsum('bsd,od->bso', x, weight)
        r = disha.shape[0]
        pooled = x.reshape(*x.shape[:-1], x.shape[-1] // r, r).sum(axis=-2)
        return result + pooled @ disha
    x = L0_attn_x
    x = x + _L0_attn_ref(_layernorm(x, axis=-1), L0_attn_Wq, L0_attn_bq, L0_attn_Wk, L0_attn_bk, L0_attn_Wv, L0_attn_bv, L0_attn_Wo, L0_attn_bo)
    x = x + _L0_ffn_ref(_layernorm(x, axis=-1), L0_ffn_Wr, L0_ffn_br, L0_ffn_W1, L0_ffn_b1, L0_ffn_W2, L0_ffn_b2)
    x = x + _L1_attn_ref(_layernorm(x, axis=-1), L1_attn_Wq, L1_attn_Wk)
    x = x + _L1_ffn_ref(_layernorm(x, axis=-1), L1_ffn_weight, L1_ffn_disha)
    return x

_drawn_inputs = setup_inputs


def setup_inputs(seed=0):
    import zlib

    import numpy as np

    out = dict(_drawn_inputs(seed))
    spreads = {'L0_attn_bq': (0.0, 0.356),
     'L0_attn_bk': (0.0, 0.8),
     'L0_attn_bv': (0.0, 0.1),
     'L0_attn_bo': (0.0, 0.1),
     'L0_ffn_br': (0.0, 0.572),
     'L0_ffn_b1': (0.0, 0.8),
     'L0_ffn_b2': (0.0, 0.621)}
    factors = {'L0_ffn_Wr': 4.663, 'L0_ffn_W1': 8.0, 'L0_ffn_W2': 8.0}
    for name, (base, spread) in spreads.items():
        noise = np.random.default_rng([zlib.crc32(name.encode()), seed]).standard_normal(out[name].shape)
        drawn = base * np.exp(spread * noise) if base else spread * noise
        out[name] = jnp.asarray(drawn.astype(out[name].dtype))
    for name, factor in factors.items():
        out[name] = (out[name] * factor).astype(out[name].dtype)
    return out
```

```python
from contextlib import ExitStack

import numpy as np
import concourse.bass as bass
from concourse import mybir

F32 = mybir.dt.float32
BF16 = mybir.dt.bfloat16
ALU = mybir.AluOpType
ACT = mybir.ActivationFunctionType
AX = mybir.AxisListType

P = 128
B, S, D = 4, 1024, 128
H, HD = 16, 8
E, CAP = 8, B * S // 8
TILES = B * S // P
CH = 4
CW = CH * P
CHUNKS = TILES // CH
EPS = 1e-5
GH = 4
NG = B * H // GH
KB = S // P
QC = S // CW

MAXROWS, BIASROWS = 3, 6
Q_PART = (0, 0, 1, 0, 2, 1)
K_PART = (0, 1, 0, 2, 0, 1)
NPROD = len(Q_PART)
CROWS = MAXROWS + BIASROWS
ROWS = CROWS + NPROD * HD
FILL = -3.0e38
BIG = -1.0e30


def bf16_bits(a):
    return (np.ascontiguousarray(a, np.float32).view(np.uint32) >> 16).astype(np.uint16)


def top(a):
    return (np.ascontiguousarray(a, np.float32).view(np.uint32) & np.uint32(0xFFFF0000)).view(np.float32)


def constants():
    pos = np.arange(S)
    slopes = np.power(np.float32(2.0 ** (-8.0 / H)), np.arange(1, H + 1, dtype=np.float32)).astype(np.float32)
    s0 = top(slopes)
    s1 = top(slopes - s0)
    s2 = top(slopes - s0 - s1)
    krows = np.zeros((CROWS, S), np.float32)
    krows[:MAXROWS] = 1.0
    qrows = np.zeros((H, CROWS, S), np.float32)
    for part, s in enumerate((s0, s1, s2)):
        krows[MAXROWS + 2 * part] = pos // P * P
        krows[MAXROWS + 2 * part + 1] = pos % P
        qrows[:, MAXROWS + 2 * part] = s[:, None]
        qrows[:, MAXROWS + 2 * part + 1] = s[:, None]
    q, k = np.arange(P)[:, None], np.arange(P)[None, :]
    cmask = np.zeros((P, S), np.float32)
    cmask[:, S - P:] = np.where(k <= q, 0.0, FILL)
    seq, at = np.arange(P) // 32, np.arange(P) % 32
    same = seq[:, None] == seq[None, :]
    sel = np.zeros((H, P), np.float32)
    sel[np.arange(P) % H, np.arange(P)] = 1.0
    big = np.zeros((E, E, P), np.float32)
    big[np.arange(E), np.arange(E)] = BIG
    return {
        "c_qrows": bf16_bits(qrows),
        "c_krows": bf16_bits(krows),
        "c_cmask": bf16_bits(cmask),
        "c_identb": bf16_bits(np.eye(P)),
        "c_guard": bf16_bits(np.where(q > k, FILL, 0.0)),
        "c_ident": np.eye(P, dtype=np.float32),
        "c_sel": sel,
        "c_incl": bf16_bits(same & (at[:, None] <= at[None, :])),
        "c_same": bf16_bits(same),
        "c_less": bf16_bits(seq[:, None] < seq[None, :]),
        "c_big": bf16_bits(big.reshape(E, E * P)),
        "c_samet": (at[:, None] == at[None, :]).astype(np.float32),
        "c_rank": np.tile((E - np.arange(E)).astype(np.float32), (P, 1)),
        "c_half": np.full((P, CH), -0.5, np.float32),
    }


def attention_units():
    out = []
    for slot, c in enumerate(range(QC - 1, -1, -1)):
        for kb in range(CH * (c + 1)):
            d = kb - CH * c
            q0 = P * max(d, 0)
            out.append((slot, c, kb, q0, CW - q0, d >= 0))
    return out


def steep(par, i):
    return any(2.0 ** (-8.0 / H * (GH * g + i + 1)) * (P - 1) > 40 for g in range(par, H // GH, 2))


UNITS = attention_units()
NU = len(UNITS)
MAXUNITS = [(slot, t, i) for slot, c in enumerate(range(QC - 1, -1, -1))
            for t in range(CH * c, CH * c + CH) for i in range(GH)]
NM = len(MAXUNITS)
FIRST = [min(u for u in range(NU) if UNITS[u][0] == s) for s in range(QC)]
LAST = [max(u for u in range(NU) if UNITS[u][0] == s) for s in range(QC)]
DIAG = [u for u in range(NU) if UNITS[u][5]]


def step_order(with_b, with_a):
    b, a = [], []
    if with_b:
        for u in range(NU + 1):
            if u < NU:
                w = UNITS[u][4]
                b += [(("S", u, 0), w), (("S", u, 1), w)]
            if u > 0:
                b.append((("V", u - 1), 4 * UNITS[u - 1][4]))
                if u - 1 in LAST:
                    b.append((("O", LAST.index(u - 1)), 0))
            if u < NU:
                b += [(("S", u, 2), w), (("S", u, 3), w)]
            if u == 1:
                b.append((("L", QC - 1), 100))
    if with_a:
        for k, (slot, t, i) in enumerate(MAXUNITS):
            a.append((("A", k), P * (t + 1)))
            if k + 1 == NM // 2:
                a.append((("F", 0), 0))
            if k == NM // 2 + 4:
                a.append((("T", 0), 100))
        a.append((("F", 1), 0))
    out, done_a, done_b = [], 0.0, 0.0
    tot_a = sum(w for _, w in a) or 1
    tot_b = sum(w for _, w in b) or 1
    while a or b:
        if b and (not a or done_b / tot_b <= done_a / tot_a):
            item, w = b.pop(0)
            done_b += w
        else:
            item, w = a.pop(0)
            done_a += w
        out.append(item)
    return out


def build(nc, x, Wq, bq, Wk, bk, Wv, bv, Wo, bo, Wr, br, W1, b1, W2, b2, W1q, W1k, Wf, disha, consts, out):
    ctx = ExitStack()
    with ctx:
        def sb(name, shape, dt=F32):
            return ctx.enter_context(nc.sbuf_tensor(name, shape, dt))

        def sem(name):
            return ctx.enter_context(nc.semaphore(name))

        bank2 = [ctx.enter_context(nc.psum_tensor(f"bank2_{i}", [P, 2 * CW], F32)) for i in range(2)]
        bank = [ctx.enter_context(nc.psum_tensor(f"bank{i}", [P, CW], F32)) for i in range(4)]
        half = [bank2[0][:, 0:CW], bank2[0][:, CW:2 * CW], bank2[1][:, 0:CW], bank2[1][:, CW:2 * CW]]
        b0, b1_, b2_, b3 = (t[:, :] for t in bank)

        q_dram = nc.dram_tensor("q_rows", (NG, GH, ROWS, S), BF16).ap()
        k_dram = nc.dram_tensor("k_rows", (NG, GH, NPROD * HD, S), BF16).ap()
        m_dram = nc.dram_tensor("max_rows", (QC, CH * GH * 3, P), BF16).ap()
        o_dram = nc.dram_tensor("weighted_sums", (NG, GH, HD + 1, S), F32).ap()

        ident = sb("ident", [P, P])
        identb = sb("identb", [P, P], BF16)
        cmask = sb("cmask", [P, S], BF16)
        guards = sb("guards", [P, P], BF16)
        half_pow = sb("half_pow", [P, CH])
        wq, wk, wv = sb("wq", [P, D]), sb("wk", [P, D]), sb("wv", [P, D])
        bqc, bkc = sb("bqc", [P, 1]), sb("bkc", [P, 1])
        bvb = sb("bvb", [P, D])
        v_all = sb("v_all", [P, NG, KB, GH, 32])
        x_res = sb("x_res", [P, TILES, D])

        const_in = sem("const_in")
        w_in = sem("w_in")
        x_in = [sem(f"x_in{b}") for b in range(B)]
        xres_in = sem("xres_in")
        rows_in = sem("rows_in")

        scale = 1.0 / float(np.sqrt(np.float32(HD)))

        att = ExitStack()
        ctx.enter_context(att)

        def asb(name, shape, dt=F32):
            return att.enter_context(nc.sbuf_tensor(name, shape, dt))

        qa, ka = asb("q_for_max", [P, 2, GH, S], BF16), asb("k_for_max", [P, 2, GH, S], BF16)
        qb, kb_ = asb("q_for_exp", [P, 2, GH, S], BF16), asb("k_for_exp", [P, 2, GH, S], BF16)
        pad_zero, krows_in = sem("pad_zero"), sem("krows_in")

        pre = ExitStack()
        with pre:
            def tsb(name, shape, dt=F32):
                return pre.enter_context(nc.sbuf_tensor(name, shape, dt))

            xn = tsb("xn", [P, 2 * KB, D])
            stats = tsb("stats0", [P, 2, CH, 6])
            mv = tsb("mv0", [P, 2, CH, 2])
            ve = tsb("ve0", [P, 2, CH])
            rs = tsb("rs0", [P, 2, CH])
            nt = tsb("nt0", [P, 3, CH])
            xt = tsb("xt0", [P, 2, CW])
            full = tsb("qk_full", [P, 2, 2, CW])
            rest = tsb("qk_rest", [P, 2, 2, CW])
            parts = tsb("qk_parts", [P, 2, 2, 3, S], BF16)
            bsc = tsb("bsc", [P, 2])

            norm_in, var_ready, pow_ready, xn_ready = sem("norm_chain"), sem("var_ready"), sem("pow_ready"), sem("xn_ready")
            xt_psum, xt_ready, qk_psum, v_psum = sem("xt_psum"), sem("xt_ready"), sem("qk_psum"), sem("v_psum")
            bias_ready, hi_ready, rest_ready, parts_ready = sem("bias_ready"), sem("hi_ready"), sem("rest_ready"), sem("parts_ready")
            mid_ready, v_ready, v_zero = sem("mid_ready"), sem("v_ready"), sem("v_zero")
            parts_out = [sem(f"parts_out{i}") for i in range(2)]
            NCONST = 5
            NW = 6

            psT = [half[0], half[1]]
            psQ = [b0, b1_]
            psK = [b2_, b3]
            psV = [half[2], half[3]]
            block = pre.enter_context(nc.Block())

            @block.sync
            def _(sp):
                for b in range(2):
                    sp.dma_start(xn[:, b * KB:(b + 1) * KB, :],
                                 x[b].rearrange("(u p) d -> p u d", p=P)).then_inc(x_in[b], 16)
                    if b == 0:
                        sp.dma_start(ident[:, :], consts["c_ident"]).then_inc(const_in, 16)
                        sp.dma_start(half_pow[:, :], consts["c_half"]).then_inc(const_in, 16)
                        sp.dma_start(wq[:, :], Wq).then_inc(w_in, 16)
                        sp.dma_start(wk[:, :], Wk).then_inc(w_in, 16)
                        sp.dma_start(wv[:, :], Wv).then_inc(w_in, 16)
                        sp.dma_start(bqc[:, :], bq.rearrange("(p o) -> p o", o=1)).then_inc(w_in, 16)
                        sp.dma_start(bkc[:, :], bk.rearrange("(p o) -> p o", o=1)).then_inc(w_in, 16)
                        sp.dma_start(bvb[:, :], bv.partition_broadcast(P)).then_inc(w_in, 16)
                sp.dma_start(cmask[:, :], consts["c_cmask"].bitcast(BF16)).then_inc(const_in, 16)
                sp.dma_start(identb[:, :], consts["c_identb"].bitcast(BF16)).then_inc(const_in, 16)
                sp.dma_start(guards[:, :], consts["c_guard"].bitcast(BF16)).then_inc(const_in, 16)
                for b in range(2, B):
                    sp.wait_ge(xt_psum, 2 * (b - 1))
                    sp.dma_start(xn[:, b % 2 * KB:(b % 2 + 1) * KB, :],
                                 x[b].rearrange("(u p) d -> p u d", p=P)).then_inc(x_in[b], 16)
                for b in range(B):
                    g = slice(b * H // GH, (b + 1) * H // GH)
                    sp.dma_start(q_dram[g, :, 0:CROWS, :].rearrange("g i c s -> (g i) c s"),
                                 consts["c_qrows"].bitcast(BF16)).then_inc(rows_in, 16)
                for s in range(B):
                    sp.dma_start(x_res[32 * s:32 * s + 32, :, :],
                                 x[s].rearrange("(u t) d -> t u d", t=32)).then_inc(xres_in, 16)
                for b in range(B):
                    sp.wait_ge(parts_ready, 2 * 2 * (b + 1))
                    sp.wait_ge(mid_ready, 2 * 2 * (b + 1))
                    sp.wait_ge(hi_ready, 2 * 2 * (b + 1))
                    if b == B - 1:
                        sp.wait_ge(pad_zero, 1)
                        for t in (ka, kb_):
                            for par in range(2):
                                for i in range(GH):
                                    sp.dma_start(t[0:CROWS, par, i, :],
                                                 consts["c_krows"].bitcast(BF16)).then_inc(krows_in, 16)
                    for c in range(NPROD):
                        dst = q_dram[4 * b:4 * b + 4, :, CROWS + HD * c:CROWS + HD * (c + 1), :]
                        sp.dma_start(dst.rearrange("g i d s -> (g i) d s"),
                                     parts[:, b % 2, 0, Q_PART[c], :]).then_inc(parts_out[b % 2], 16)

            @block.gpsimd
            def _(pool):
                nc.gpsimd.memset(v_all[:, :, :, :, :], 0.0).then_inc(v_zero, 1)
                pool.wait_ge(v_zero, 1)
                nc.gpsimd.memset(v_all[:, :, :, :, HD:HD + 1], 1.0).then_inc(v_zero, 1)
                pool.wait_ge(const_in, 16 * NCONST)
                pads = [qa, ka, qb, kb_]
                for k in range(CHUNKS):
                    if k >= 2 and pads:
                        last = nc.gpsimd.memset(pads.pop()[:, :, :, :].bitcast(F32), 0.0)
                        if not pads:
                            last.then_inc(pad_zero, 1)
                    pool.wait_ge(var_ready, k + 1)
                    nc.gpsimd.tensor_tensor(rs[:, k % 2, :], ve[:, k % 2, :], half_pow[:, :], ALU.pow).then_inc(pow_ready, 1)
                    for z in range(2):
                        if k == 0:
                            break
                        pool.wait_ge(mid_ready, 2 * (k - 1) + z + 1)
                        kk = k - 1
                        nc.gpsimd.tensor_tensor(parts[:, kk // 2 % 2, z, 2, CW * (kk % 2):CW * (kk % 2) + CW],
                                                rest[:, kk % 2, z, :],
                                                parts[:, kk // 2 % 2, z, 1, CW * (kk % 2):CW * (kk % 2) + CW],
                                                ALU.subtract).then_inc(parts_ready, 1)
                kk = CHUNKS - 1
                for z in range(2):
                    pool.wait_ge(mid_ready, 2 * kk + z + 1)
                    nc.gpsimd.tensor_tensor(parts[:, kk // 2 % 2, z, 2, CW * (kk % 2):CW * (kk % 2) + CW],
                                            rest[:, kk % 2, z, :],
                                            parts[:, kk // 2 % 2, z, 1, CW * (kk % 2):CW * (kk % 2) + CW],
                                            ALU.subtract).then_inc(parts_ready, 1)

            @block.vector
            def _(dve):
                chain = [0]

                def link(ins):
                    chain[0] += 1
                    ins.then_inc(norm_in, 1)
                    dve.wait_ge(norm_in, chain[0])

                def norm(k):
                    if k % 2 == 0:
                        dve.wait_ge(x_in[k // 2], 16)
                    for i in range(CH):
                        last = nc.vector.bn_stats(stats[:, k % 2, i, :], xn[:, (CH * k + i) % (2 * KB), :])
                    link(last)
                    for i in range(CH):
                        last = nc.vector.bn_aggr(mv[:, k % 2, i, :], stats[:, k % 2, i, :])
                    link(last)
                    nc.vector.tensor_scalar_add(ve[:, k % 2, :], mv[:, k % 2, :, 1], EPS).then_inc(var_ready, 1)
                    dve.wait_ge(pow_ready, k + 1)
                    link(nc.vector.tensor_tensor(nt[:, 0, :], ve[:, k % 2, :], rs[:, k % 2, :], ALU.mult))
                    link(nc.vector.tensor_tensor(nt[:, 1, :], nt[:, 0, :], rs[:, k % 2, :], ALU.mult))
                    link(nc.vector.tensor_scalar(nt[:, 2, :], nt[:, 1, :], -0.5, 1.5, ALU.mult, ALU.add))
                    link(nc.vector.tensor_tensor(rs[:, k % 2, :], rs[:, k % 2, :], nt[:, 2, :], ALU.mult))
                    for i in range(CH):
                        last = nc.vector.tensor_scalar(xn[:, (CH * k + i) % (2 * KB), :], xn[:, (CH * k + i) % (2 * KB), :], mv[:, k % 2, i, 0:1],
                                                       rs[:, k % 2, i:i + 1], ALU.subtract, ALU.mult)
                    last.then_inc(xn_ready, 1)

                def cut(k):
                    for z in range(2):
                        dve.wait_ge(hi_ready, 2 * k + z + 1)
                        if k >= 2:
                            dve.wait_ge(parts_ready, 2 * (k - 2) + z + 1)
                        if k >= 4:
                            dve.wait_ge(parts_out[k // 2 % 2], 16 * NPROD * 2 * (k // 4))
                        to = slice(CW * (k % 2), CW * (k % 2) + CW)
                        link(nc.vector.tensor_tensor(rest[:, k % 2, z, :], full[:, k % 2, z, :],
                                                     parts[:, k // 2 % 2, z, 0, to], ALU.subtract))
                        nc.vector.tensor_copy(parts[:, k // 2 % 2, z, 1, to], rest[:, k % 2, z, :]).then_inc(mid_ready, 1)
                    dve.wait_ge(v_psum, k + 1)
                    dve.wait_ge(v_zero, 2)
                    for i in range(CH):
                        t = CH * k + i
                        dst = v_all[:, 4 * (t // KB):4 * (t // KB) + 4, t % KB, :, 0:HD]
                        last = nc.vector.tensor_tensor(
                            dst, psV[k % 2][:, P * i:P * i + P].rearrange("p (g i d) -> p g i d", g=4, i=GH),
                            bvb[:, :].rearrange("p (g i d) -> p g i d", g=4, i=GH), ALU.add)
                    last.then_inc(v_ready, 1)

                dve.wait_ge(w_in, 16 * NW)
                norm(0)
                for k in range(CHUNKS):
                    if k + 1 < CHUNKS:
                        norm(k + 1)
                    cut(k)

            @block.tensor
            def _(pe):
                pe.wait_ge(const_in, 16 * NCONST)
                pe.wait_ge(w_in, 16 * NW)

                def turn(k):
                    pe.wait_ge(xn_ready, k + 1)
                    if k >= 2:
                        pe.wait_ge(xt_ready, k - 1)
                    for i in range(CH):
                        last = nc.tensor.transpose(psT[k % 2][:, P * i:P * i + P], xn[:, (CH * k + i) % (2 * KB), :], ident[:, :])
                    last.then_inc(xt_psum, 1)

                def project(k):
                    pe.wait_ge(xt_ready, k + 1)
                    if k >= 2:
                        pe.wait_ge(hi_ready, 2 * (k - 1))
                        pe.wait_ge(v_ready, k - 1)
                    nc.tensor.matmul(psQ[k % 2], wq[:, :], xt[:, k % 2, :], start=True, stop=True).then_inc(qk_psum, 1)
                    nc.tensor.matmul(psK[k % 2], wk[:, :], xt[:, k % 2, :], start=True, stop=True).then_inc(qk_psum, 1)
                    for i in range(CH):
                        last = nc.tensor.matmul(psV[k % 2][:, P * i:P * i + P], xt[:, k % 2, P * i:P * i + P], wv[:, :],
                                                start=True, stop=True)
                    last.then_inc(v_psum, 1)

                turn(0)
                for k in range(CHUNKS):
                    if k + 1 < CHUNKS:
                        turn(k + 1)
                    project(k)

            @block.scalar
            def _(act):
                act.wait_ge(w_in, 16 * NW)
                nc.scalar.mul(bsc[:, 0:1], bqc[:, :], scale).then_inc(bias_ready, 1)
                nc.scalar.copy(bsc[:, 1:2], bkc[:, :]).then_inc(bias_ready, 1)
                act.wait_ge(bias_ready, 2)

                def take(k):
                    act.wait_ge(xt_psum, k + 1)
                    if k >= 2:
                        act.wait_ge(v_psum, k - 1)
                    nc.scalar.copy(xt[:, k % 2, :], psT[k % 2]).then_inc(xt_ready, 1)

                take(0)
                for k in range(CHUNKS):
                    if k + 1 < CHUNKS:
                        take(k + 1)
                    for z, ps in enumerate((psQ, psK)):
                        act.wait_ge(qk_psum, 2 * k + z + 1)
                        if k >= 2:
                            act.wait_ge(mid_ready, 2 * (k - 2) + z + 1)
                        if k >= 4:
                            act.wait_ge(parts_out[k // 2 % 2], 16 * NPROD * 2 * (k // 4))
                        to = slice(CW * (k % 2), CW * (k % 2) + CW)
                        sc = scale if z == 0 else 1.0
                        nc.scalar.activation(full[:, k % 2, z, :], ps[k % 2], ACT.Identity, bias=bsc[:, z:z + 1], scale=sc)
                        nc.scalar.activation(parts[:, k // 2 % 2, z, 0, to], ps[k % 2], ACT.Identity,
                                             bias=bsc[:, z:z + 1], scale=sc).then_inc(hi_ready, 1)
                    if k % 2 == 1:
                        b = k // 2
                        act.wait_ge(parts_ready, 2 * 2 * (b + 1))
                        act.wait_ge(mid_ready, 2 * 2 * (b + 1))
                        act.wait_ge(hi_ready, 2 * 2 * (b + 1))
                        for c in range(NPROD):
                            dst = k_dram[4 * b:4 * b + 4, :, HD * c:HD * (c + 1), :]
                            act.dma_start(dst.rearrange("g i d s -> (g i) d s"),
                                          parts[:, b % 2, 1, K_PART[c], :]).then_inc(parts_out[b % 2], 16)

        with att:
            vb = asb("v_group", [P, 2, KB, GH, 32])
            probs = asb("probs", [P, 3, GH, CW])
            junk = asb("junk", [P, 2, S], BF16)
            mx = asb("row_max", [P, 2, KB * GH])
            mrest = asb("max_rest", [P, QC, 2, CH * GH])
            mparts = asb("max_parts", [P, QC, CH, GH, 3], BF16)
            mrows = asb("max_rows_sb", [CH * GH * 3, QC, P], BF16)
            osum = asb("osum", [P, QC, CW])

            a_in = [sem(f"a_in{i}") for i in range(2)]
            b_in = [sem(f"b_in{i}") for i in range(2)]
            m_in = [[sem(f"m_in{i}{j}") for j in range(QC)] for i in range(2)]
            m_out = [sem(f"m_out{j}") for j in range(QC)]
            o_out = [sem(f"o_out{j}") for j in range(QC)]
            a_scores, a_max, cut_chain, mparts_ready = sem("a_scores"), sem("a_max"), sem("cut_chain"), sem("mparts_ready")
            mt_psum, mrows_ready = sem("mt_psum"), sem("mrows_ready")
            s_scores, exp_ready, masked, pv_done, o_ready = sem("s_scores"), sem("exp_ready"), sem("masked"), sem("pv_done"), sem("o_ready")

            dve_turns, pe_turns, pool_turns, sp_turns = sem("dve_turns"), sem("pe_turns"), sem("pool_turns"), sem("sp_turns")

            psA = [bank2[0][:, :], bank2[1][:, :]]
            psS = [b0, b1_]
            psO = b2_
            psM = b3
            qn = q_dram.rearrange("n i c s -> n c i s")
            kn = k_dram.rearrange("n i c s -> n c i s")
            mb = MAXROWS
            block = att.enter_context(nc.Block())

            def load_max_operands(sp, n, par, half_n, late):
                if late:
                    sp.wait_ge(a_scores, (n - 1) * NM)
                sp.dma_start(qa[0:ROWS, par, :, :], qn[bass.ds(n, 1)].rearrange("n c i s -> (n c) i s")).then_inc(a_in[par], 16)
                sp.dma_start(ka[CROWS:ROWS, par, :, :], kn[bass.ds(n, 1)].rearrange("n c i s -> (n c) i s")).then_inc(a_in[par], 16)

            def load_exp_operands(sp, n, par, half_n, late):
                if late:
                    sp.wait_ge(s_scores, (n - 1) * NU * GH)
                sp.dma_start(qb[mb:ROWS, par, :, :], qn[bass.ds(n, 1), mb:ROWS].rearrange("n c i s -> (n c) i s")).then_inc(b_in[par], 16)
                sp.dma_start(kb_[CROWS:ROWS, par, :, :], kn[bass.ds(n, 1)].rearrange("n c i s -> (n c) i s")).then_inc(b_in[par], 16)
                if late:
                    sp.wait_ge(pv_done, (n - 1) * NU)
                sp.dma_start(vb[:, par, :, :, :].rearrange("p k i c -> p (k i c)"),
                             v_all[:, bass.ds(n, 1)].rearrange("p n k i c -> p (n k i c)")).then_inc(b_in[par], 16)

            @block.sync
            def _(sp):
                sp.wait_ge(rows_in, 16 * B)
                for i in range(2):
                    sp.wait_ge(parts_out[i], 16 * NPROD * 2 * 2)
                sp.wait_ge(v_ready, CHUNKS)

                def rows_of_maxima(n, par, half_n, slot, late):
                    c = QC - 1 - slot
                    sp.wait_ge(m_out[slot], 16 * n + 16)
                    if late:
                        sp.wait_ge(s_scores, (n - 1) * NU * GH)
                    src = m_dram[slot].rearrange("(t i m) q -> m i t q", t=CH, i=GH)
                    for i in range(GH):
                        dst = qb[0:mb, par, i, CW * c:CW * c + CW]
                        sp.dma_start(dst.rearrange("m (t q) -> m t q", t=CH), src[:, i]).then_inc(m_in[par][slot], 16)

                def step(n, half_n, par, first, with_a, load2, late):
                    if load2:
                        load_max_operands(sp, n + 2, par, half_n, True)
                    if with_a and n is not None:
                        load_exp_operands(sp, n + 1, 1 - par, half_n, late)
                    for item in step_order(True, with_a):
                        if item[0] == "O":
                            slot = item[1]
                            c = QC - 1 - slot
                            sp.wait_ge(o_ready, n * QC + slot + 1)
                            sp.sem_inc(sp_turns, 1)
                            for i in range(GH):
                                sp.dma_start(o_dram[bass.ds(n, 1), i, :, CW * c:CW * c + CW].rearrange("n r s -> (n r) s"),
                                             osum[32 * i:32 * i + HD + 1, slot, :]).then_inc(o_out[slot], 16)
                        elif item[0] == "T":
                            rows_of_maxima(n + 1, 1 - par, None, item[1], late)
                        elif item[0] == "L":
                            rows_of_maxima(n, par, None, item[1], not first)

                load_max_operands(sp, 0, 0, 0, False)
                load_exp_operands(sp, 0, 0, 0, False)
                load_max_operands(sp, 1, 1, 0, False)
                for item in step_order(False, True):
                    if item[0] == "T":
                        rows_of_maxima(0, 0, None, item[1], False)
                step(0, 0, 0, True, True, True, False)
                step(1, 0, 1, True, True, True, True)
                with sp.Fori(1, NG // 2 - 1) as it:
                    step(2 * it, it, 0, False, True, True, True)
                    step(2 * it + 1, it, 1, False, True, True, True)
                step(NG - 2, NG // 2 - 1, 0, False, True, False, True)
                step(NG - 1, NG // 2 - 1, 1, False, False, False, True)
                for slot in range(QC):
                    sp.wait_ge(o_out[slot], 16 * GH * NG)

            @block.tensor
            def _(pe):
                pe.wait_ge(v_ready, CHUNKS)
                pe.wait_ge(hi_ready, 2 * CHUNKS)
                pe.wait_ge(krows_in, 16 * 16)
                pe.wait_ge(const_in, 16 * NCONST)

                def max_scores(n, par, half_n, k, ready):
                    slot, t, i = MAXUNITS[k]
                    if k == 0:
                        pe.wait_ge(a_in[par], 32 * (half_n + 1))
                    if not ready or k >= 2:
                        pe.wait_ge(a_max, n * NM + k - 1)
                    w = P * (t + 1)
                    for f in range(0, w, CW):
                        e = min(w, f + CW)
                        last = nc.tensor.matmul(psA[k % 2][:, f:e], qa[:, par, i, P * t:P * t + P],
                                                ka[:, par, i, f:e], start=True, stop=True)
                    last.then_inc(a_scores, 1)

                def turn_maxima(n, slot, first):
                    pe.wait_ge(mparts_ready, n * QC + slot + 1)
                    if not (first and slot == 0):
                        pe.wait_ge(mrows_ready, n * QC + slot)
                    pe.sem_inc(pe_turns, 1)
                    nc.tensor.transpose(psM[0:CH * GH * 3, :].bitcast(BF16)[:, 0:P],
                                        mparts[:, slot, :, :, :].rearrange("p t i m -> p (t i m)"),
                                        identb[:, :]).then_inc(mt_psum, 1)

                def scores(n, par, half_n, u, i, first):
                    slot, c, kb, q0, w, diag = UNITS[u]
                    k = GH * u + i
                    if k == 0:
                        pe.wait_ge(b_in[par], 48 * (half_n + 1))
                    if u in FIRST and i == 0:
                        pe.wait_ge(m_in[par][slot], 64 * (half_n + 1))
                    if not first or k >= 2:
                        pe.wait_ge(exp_ready, n * NU * GH + k - 1)
                    guard = diag and steep(par, i)
                    last = nc.tensor.matmul(psS[k % 2][:, 0:w], kb_[:, par, i, P * kb:P * kb + P],
                                            qb[:, par, i, CW * c + q0:CW * c + q0 + w], start=True, stop=not guard)
                    if guard:
                        last = nc.tensor.matmul(psS[k % 2][:, 0:P], identb[:, :], guards[:, :],
                                                start=False, stop=True)
                    last.then_inc(s_scores, 1)

                def weighted_sums(n, par, u, first):
                    slot, c, kb, q0, w, diag = UNITS[u]
                    pe.wait_ge(exp_ready, (n * NU + u + 1) * GH)
                    if diag:
                        pe.wait_ge(masked, n * len(DIAG) + DIAG.index(u) + 1)
                    if u in FIRST and not (first and slot == 0):
                        pe.wait_ge(o_ready, n * QC + slot)
                    for i in range(GH):
                        last = nc.tensor.matmul(psO[32 * i:32 * i + 32, q0:q0 + w], vb[:, par, kb, i, :],
                                                probs[:, u % 3, i, 0:w], start=u in FIRST, stop=u in LAST,
                                                tile_position=(0, 32 * i))
                    last.then_inc(pv_done, 1)

                def step(n, half_n, par, first, with_a, half_next=None):
                    for item in step_order(True, with_a):
                        if item[0] == "A":
                            max_scores(n + 1, 1 - par, half_next, item[1], False)
                        elif item[0] == "T":
                            turn_maxima(n + 1, item[1], False)
                        elif item[0] == "L":
                            turn_maxima(n, item[1], False)
                        elif item[0] == "S":
                            scores(n, par, half_n, item[1], item[2], first)
                        elif item[0] == "V":
                            weighted_sums(n, par, item[1], first)

                for item in step_order(False, True):
                    if item[0] == "A":
                        max_scores(0, 0, 0, item[1], True)
                    elif item[0] == "T":
                        turn_maxima(0, item[1], True)
                step(0, 0, 0, True, True, 0)
                step(1, 0, 1, False, True, 1)
                with pe.Fori(1, NG // 2 - 1) as it:
                    step(2 * it, it, 0, False, True, it)
                    step(2 * it + 1, it, 1, False, True, it + 1)
                step(NG - 2, NG // 2 - 1, 0, False, True, NG // 2 - 1)
                step(NG - 1, NG // 2 - 1, 1, False, False)

            @block.vector
            def _(dve):
                dve.wait_ge(const_in, 16 * NCONST)

                def row_max(n, par, k):
                    slot, t, i = MAXUNITS[k]
                    w = P * (t + 1)
                    dve.wait_ge(a_scores, n * NM + k + 1)
                    dve.sem_inc(dve_turns, 1)
                    nc.vector.tensor_tensor_reduce(
                        out=junk[:, k % 2, 0:w], in0=psA[k % 2][:, 0:w], in1=cmask[:, S - w:S], scale=1.0, scalar=FILL,
                        op0=ALU.add, op1=ALU.max, accum_out=mx[:, par, t * GH + i:t * GH + i + 1]).then_inc(a_max, 1)

                def cut_maxima(n, par, slot, first):
                    c = QC - 1 - slot
                    done = (n * QC + slot) * 3
                    m = mx[:, par, CH * GH * c:CH * GH * (c + 1)]
                    part = mparts[:, slot, :, :, :].rearrange("p t i m -> p (t i) m")
                    dve.wait_ge(a_max, n * NM + NM // 2 * (slot + 1))
                    if not first:
                        dve.wait_ge(mt_psum, (n - 1) * QC + slot + 1)
                    nc.vector.tensor_scalar_mul(part[:, :, 0], m, -1.0).then_inc(cut_chain, 1)
                    dve.wait_ge(cut_chain, done + 1)
                    nc.vector.scalar_tensor_tensor(mrest[:, slot, 0, :], m, -1.0, part[:, :, 0],
                                                   ALU.mult, ALU.subtract).then_inc(cut_chain, 1)
                    dve.wait_ge(cut_chain, done + 2)
                    nc.vector.tensor_copy(part[:, :, 1], mrest[:, slot, 0, :]).then_inc(cut_chain, 1)
                    dve.wait_ge(cut_chain, done + 3)
                    nc.vector.tensor_tensor(part[:, :, 2], mrest[:, slot, 0, :], part[:, :, 1],
                                            ALU.subtract).then_inc(mparts_ready, 1)

                def step(n, par, first, order):
                    for item in order:
                        if item[0] == "A":
                            row_max(n, par, item[1])
                        elif item[0] == "F":
                            cut_maxima(n, par, item[1], first)

                step(0, 0, True, step_order(False, True))
                step(1, 1, False, step_order(True, True))
                step(2, 0, False, step_order(True, True))
                with dve.Fori(1, NG // 2 - 1) as it:
                    step(2 * it + 1, 1, False, step_order(True, True))
                    step(2 * it + 2, 0, False, step_order(True, True))
                step(NG - 1, 1, False, step_order(True, True))

            @block.scalar
            def _(act):
                def exps(n, u, i, first):
                    slot, c, kb, q0, w, diag = UNITS[u]
                    k = GH * u + i
                    if i == 0 and (not first or u >= 3):
                        act.wait_ge(pv_done, n * NU + u - 2)
                    act.wait_ge(s_scores, n * NU * GH + k + 1)
                    nc.scalar.activation(probs[:, u % 3, i, 0:w], psS[k % 2][:, 0:w], ACT.Exp).then_inc(exp_ready, 1)

                def maxima_rows(n, par, half_last, slot, first):
                    act.wait_ge(mt_psum, n * QC + slot + 1)
                    if not first:
                        act.wait_ge(m_out[slot], 16 * n)
                    nc.scalar.copy(mrows[:, slot, :], psM[0:CH * GH * 3, :].bitcast(BF16)[:, 0:P]).then_inc(mrows_ready, 1)
                    act.wait_ge(mrows_ready, n * QC + slot + 1)
                    if not first:
                        act.wait_ge(m_in[1 - par][slot], 64 * (half_last + 1))
                    act.dma_start(m_dram[slot], mrows[:, slot, :]).then_inc(m_out[slot], 16)

                def sums_out(n, slot, first):
                    act.wait_ge(pv_done, n * NU + LAST[slot] + 1)
                    if not first:
                        act.wait_ge(o_out[slot], 16 * GH * n)
                    nc.scalar.copy(osum[:, slot, :], psO).then_inc(o_ready, 1)

                def step(n, par, half_n, first, with_a):
                    for item in step_order(True, with_a):
                        if item[0] == "S":
                            exps(n, item[1], item[2], first)
                        elif item[0] == "T":
                            maxima_rows(n + 1, 1 - par, half_n, item[1], False)
                        elif item[0] == "L":
                            maxima_rows(n, par, half_n - 1 + par, item[1], first)
                        elif item[0] == "O":
                            sums_out(n, item[1], first)

                for item in step_order(False, True):
                    if item[0] == "T":
                        maxima_rows(0, 0, 0, item[1], True)
                step(0, 0, 0, True, True)
                step(1, 1, 0, False, True)
                with act.Fori(1, NG // 2 - 1) as it:
                    step(2 * it, 0, it, False, True)
                    step(2 * it + 1, 1, it, False, True)
                step(NG - 2, 0, NG // 2 - 1, False, True)
                step(NG - 1, 1, NG // 2 - 1, False, False)

            @block.gpsimd
            def _(pool):
                def mask(n, u):
                    pool.wait_ge(exp_ready, (n * NU + u + 1) * GH)
                    pool.sem_inc(pool_turns, 1)
                    tri = probs[:, u % 3, :, 0:P]
                    nc.gpsimd.affine_select(out=tri, in_=tri, compare_op=ALU.is_ge, fill=0.0, base=0,
                                            pattern=[[0, GH], [1, P]], channel_multiplier=-1).then_inc(masked, 1)

                for u in DIAG:
                    mask(0, u)
                with pool.Fori(1, NG) as n:
                    for u in DIAG:
                        mask(n, u)

        later_stages(nc, ctx, sb, sem, dict(
            x_res=x_res, xres_in=xres_in, o_dram=o_dram, ident=ident, identb=identb, half_pow=half_pow, half=half,
            banks=[b0, b1_, b2_, b3]), Wo, bo, Wr, br, W1, b1, W2, b2, W1q, W1k, Wf, disha, consts, out)


def later_stages(nc, ctx, sb, sem, sh, Wo, bo, Wr, br, W1, b1, W2, b2, W1q, W1k, Wf, disha, consts, out):
    x_res, ident, identb, half_pow, half, banks = (sh[k] for k in ("x_res", "ident", "identb", "half_pow", "half", "banks"))
    o_dram = sh["o_dram"]
    R = 64

    wo = sb("wo", [P, D])
    bob = sb("bob", [P, D])
    wr = sb("wr", [P, E])
    brb = sb("brb", [P, E])
    rank = sb("rank", [P, E])
    sel = sb("sel", [H, P])
    incl, same, less = (sb(n, [P, P], BF16) for n in ("incl", "same", "less"))
    big = sb("big", [E, E, P], BF16)
    samet = sb("samet", [P, P])
    w1 = sb("w1", [P, E, D])
    w2 = sb("w2", [P, E, D])
    b1c = sb("b1c", [P, E])
    b2r = sb("b2r", [E, D])
    w1q, w1k, wf = sb("w1q", [P, D]), sb("w1k", [P, D]), sb("wf", [P, D])
    dis = sb("dis", [P, D])
    aqk = sb("aqk", [P, D])
    wft = sb("wft", [P, D])

    ot = sb("ot", [P, B, S])
    den = sb("den", [H, B, S])
    at = sb("at", [P, 2, CH, P])
    xn2 = sb("xn2", [P, TILES, D])
    xt2 = sb("xt2", [P, 2, CW])
    stats = sb("stats1", [P, CH, 6])
    mv = sb("mv1", [P, CH, 2])
    ve, rs = sb("ve1", [P, CH]), sb("rs1", [P, CH])
    nt = sb("nt1", [P, 3, CH])
    lg = sb("lg", [P, TILES, E])
    ex = sb("ex", [P, TILES, E])
    hot = sb("hot", [P, TILES, E])
    hotb = sb("hotb", [P, TILES, E], BF16)
    cnt = sb("cnt", [P, 2, TILES, E])
    pos = sb("pos", [P, TILES, E])
    col = sb("col", [P, 4, TILES])
    tot = sb("tot", [P, E])
    gate = sb("gate", [P, TILES])
    hott = sb("hott", [E, 2, CW])
    noth = sb("noth", [E, 2, CW], BF16)
    xg = sb("xg", [P, 2, CH, D])
    xgt = sb("xgt", [P, 2, CW])
    hid = sb("hid", [P, 3, CW])
    xe = sb("xe", [P, 2, CH, D + 4])
    xt3 = sb("xt3", [P, CW])
    ut = sb("ut", [P, CW])
    th = sb("th", [P, CH, P])
    ee = sb("ee", [P, CH, P])
    inv = sb("inv", [P, CH])
    xn4 = sb("xn4", [P, CH, D])
    xt4 = sb("xt4", [P, CW])
    res = sb("res", [P, 2, CH, D])

    o_in, wts_in, res_out = sem("o_in"), sem("wts_in"), [sem(f"res_out{i}") for i in range(2)]
    NO = HD + 1
    p_chain, v_chain = sem("p_chain"), sem("v_chain")
    xb_ready = sem("xb_ready")
    rden_ready, rb_psum, at_ready, proj_psum, x1_ready = (sem(n) for n in ("rden_ready", "rb_psum", "at_ready", "proj_psum", "x1_ready"))
    ve_ready, pw_ready, norm_ready = sem("ve_ready"), sem("pw_ready"), sem("norm_ready")
    t2_psum, xt2_ready, lg_psum, lg_ready, ex_ready = (sem(n) for n in ("t2_psum", "xt2_ready", "lg_psum", "lg_ready", "ex_ready"))
    mx_ready, hot_ready, cnt_psum, gate_ready = sem("mx_ready"), sem("hot_ready"), sem("cnt_psum"), sem("gate_ready")
    xg_ready, g_psum, xgt_ready, hott_ready = (sem(n) for n in ("xg_ready", "g_psum", "xgt_ready", "hott_ready"))
    ht_psum = sem("ht_psum")
    z_psum, hid_ready, y_psum, x2_ready = (sem(n) for n in ("z_psum", "hid_ready", "y_psum", "x2_ready"))
    fold_psum, fold_ready = sem("fold_psum"), sem("fold_ready")
    xe_ready, t3_psum, xt3_ready, u_psum, ut_ready = (sem(n) for n in ("xe_ready", "t3_psum", "xt3_ready", "u_psum", "ut_ready"))
    s_psum, th_ready, ee_ready, em_ready, mix_psum, x3_ready = (sem(n) for n in ("s_psum", "th_ready", "ee_ready", "em_ready", "mix_psum", "x3_ready"))
    xn4_ready, t4_psum, xt4_ready, f_psum, res_ready = (sem(n) for n in ("xn4_ready", "t4_psum", "xt4_ready", "f_psum", "res_ready"))

    psRb, psProj, psT2, psLg = half[0], half[1], half[2], half[3]
    psFold = banks[3]
    psZ = [banks[0], banks[1]]
    psY = banks[2]
    psG = banks[3]
    psT3, psU, psS = half[0], half[1], half[0]
    psMix = [half[2], half[3]]
    WEIGHTS = 24

    SLOTS = {"t3": 2, "u": 3, "s": 4, "mix": 5, "t4": 7, "f": 8}

    def slots():
        for n in range((CHUNKS + 2) * E):
            due = [(name, (n - E - at) // E) for name, at in SLOTS.items()
                   if n >= E + at and (n - E - at) % E == 0 and (n - E - at) // E < CHUNKS]
            yield (n // E, n % E) if n < CHUNKS * E else None, due

    block = ctx.enter_context(nc.Block())

    @block.sync
    def _(sp):
        for s in range(1):
            sp.dma_start(bob[:, :], bo.partition_broadcast(P)).then_inc(wts_in, 16)
        for d in range(HD):
            sp.dma_start(wo[H * d:H * d + H, :], Wo.rearrange("(h d) n -> d h n", d=HD)[d]).then_inc(wts_in, 16)
        sp.dma_start(wr[:, :], Wr).then_inc(wts_in, 16)
        sp.dma_start(brb[:, :], br.partition_broadcast(P)).then_inc(wts_in, 16)
        sp.dma_start(rank[:, :], consts["c_rank"]).then_inc(wts_in, 16)
        sp.dma_start(sel[:, :], consts["c_sel"]).then_inc(wts_in, 16)
        sp.dma_start(incl[:, :], consts["c_incl"].bitcast(BF16)).then_inc(wts_in, 16)
        sp.dma_start(same[:, :], consts["c_same"].bitcast(BF16)).then_inc(wts_in, 16)
        sp.dma_start(less[:, :], consts["c_less"].bitcast(BF16)).then_inc(wts_in, 16)
        sp.dma_start(big[:, :, :].rearrange("k e f -> k (e f)"), consts["c_big"].bitcast(BF16)).then_inc(wts_in, 16)
        sp.dma_start(samet[:, :], consts["c_samet"]).then_inc(wts_in, 16)
        sp.dma_start(b2r[:, :], b2).then_inc(wts_in, 16)
        for r in range(NO):
            dst = ot[H * r:H * r + H, :, :] if r < HD else den[:, :, :]
            sp.dma_start(dst, o_dram.rearrange("(b g) i r s -> r (g i) b s", b=B)[r]).then_inc(o_in, 16)
        sp.dma_start(w1[:, :, :], W1.rearrange("e d f -> d e f")).then_inc(wts_in, 16)
        sp.dma_start(w2[:, :, :], W2.rearrange("e f d -> f e d")).then_inc(wts_in, 16)
        sp.dma_start(b1c[:, :], b1.rearrange("e f -> f e"), allow_slow_non_contiguous=True).then_inc(wts_in, 16)
        sp.dma_start(w1q[:, :], W1q).then_inc(wts_in, 16)
        sp.dma_start(w1k[:, :], W1k).then_inc(wts_in, 16)
        sp.dma_start(wf[:, :], Wf).then_inc(wts_in, 16)
        for r in range(2):
            sp.dma_start(dis[R * r:R * r + R, :], disha).then_inc(wts_in, 16)
        for j in range(CHUNKS):
            sp.wait_ge(res_ready, j + 1)
            for s in range(B):
                dst = out[s].rearrange("(u t) d -> t u d", t=32)[:, CH * j:CH * j + CH, :]
                sp.dma_start(dst, res[32 * s:32 * s + 32, j % 2, :, :]).then_inc(res_out[j % 2], 16)
        for i in range(2):
            sp.wait_ge(res_out[i], 16 * B * CHUNKS // 2)

    NW = 1 + HD + 6 + 3 + 1 + 3 + 3 + 2

    @block.gpsimd
    def _(pool):
        pool.wait_ge(sh["xres_in"], 16 * B)
        pool.wait_ge(wts_in, 16 * NW)
        for j in range(CHUNKS):
            for i in range(CH):
                last = nc.gpsimd.tensor_tensor(x_res[:, CH * j + i, :], x_res[:, CH * j + i, :], bob[:, :], ALU.add)
            last.then_inc(xb_ready, 1)
        for k in range(3 * CHUNKS):
            pool.wait_ge(ve_ready, k + 1)
            nc.gpsimd.tensor_tensor(rs[:, :], ve[:, :], half_pow[:, :], ALU.pow).then_inc(pw_ready, 1)

    @block.vector
    def _(dve):
        chain = [0]
        norms = [0]

        def link(ins):
            chain[0] += 1
            ins.then_inc(v_chain, 1)
            dve.wait_ge(v_chain, chain[0])

        def norm(src, dst):
            for i in range(CH):
                last = nc.vector.bn_stats(stats[:, i, :], src(i))
            link(last)
            for i in range(CH):
                last = nc.vector.bn_aggr(mv[:, i, :], stats[:, i, :])
            link(last)
            nc.vector.tensor_scalar_add(ve[:, :], mv[:, :, 1], EPS).then_inc(ve_ready, 1)
            norms[0] += 1
            dve.wait_ge(pw_ready, norms[0])
            link(nc.vector.tensor_tensor(nt[:, 0, :], ve[:, :], rs[:, :], ALU.mult))
            link(nc.vector.tensor_tensor(nt[:, 1, :], nt[:, 0, :], rs[:, :], ALU.mult))
            link(nc.vector.tensor_scalar(nt[:, 2, :], nt[:, 1, :], -0.5, 1.5, ALU.mult, ALU.add))
            link(nc.vector.tensor_tensor(nt[:, 0, :], rs[:, :], nt[:, 2, :], ALU.mult))
            for i in range(CH):
                last = nc.vector.tensor_scalar(dst(i), src(i), mv[:, i, 0:1], nt[:, 0, i:i + 1], ALU.subtract, ALU.mult)
            return last

        dve.wait_ge(wts_in, 16 * NW)
        dve.wait_ge(o_in, 16 * NO)
        link(nc.vector.tensor_tensor(wft[:, :], wf[:, :], wf[:, :], ALU.max))
        for s in range(B):
            last = nc.vector.reciprocal(den[:, s, :], den[:, s, :])
        last.then_inc(rden_ready, 1)
        for j in range(CHUNKS):
            dve.wait_ge(rb_psum, j + 1)
            if j >= 2:
                dve.wait_ge(proj_psum, j - 1)
            for i in range(CH):
                cols = slice(P * j + 32 * i, P * j + 32 * i + 32)
                last = nc.vector.tensor_tensor(at[:, j % 2, i, :].rearrange("p (s t) -> p s t", s=B), ot[:, :, cols],
                                               psRb.rearrange("p (s t) -> p s t", s=B)[:, :, 32 * i:32 * i + 32], ALU.mult)
            last.then_inc(at_ready, 1)
            dve.wait_ge(proj_psum, j + 1)
            dve.wait_ge(xb_ready, j + 1)
            rows = x_res[:, CH * j:CH * j + CH, :]
            link(nc.vector.tensor_tensor(rows, rows, psProj.rearrange("p (i d) -> p i d", i=CH), ALU.add))
            norm(lambda i: x_res[:, CH * j + i, :], lambda i: xn2[:, CH * j + i, :]).then_inc(norm_ready, 1)

        dve.wait_ge(lg_psum, CHUNKS)
        bc = lambda a: a.unsqueeze(2).to_broadcast([P, TILES, E])
        link(nc.vector.tensor_tensor(lg[:, :, :], psLg.rearrange("p (u e) -> p u e", e=E)[:, 0:TILES, :],
                                     brb[:, :].unsqueeze(1).to_broadcast([P, TILES, E]), ALU.add))
        link(nc.vector.tensor_reduce(col[:, 0, :], lg[:, :, :], AX.X, ALU.max))
        nc.vector.tensor_tensor(lg[:, :, :], lg[:, :, :], bc(col[:, 0, :]), ALU.subtract).then_inc(mx_ready, 1)
        dve.wait_ge(mx_ready, 1)
        link(nc.vector.tensor_scalar(hot[:, :, :], lg[:, :, :], 0.0, None, ALU.is_equal))
        link(nc.vector.tensor_tensor(hot[:, :, :], hot[:, :, :], rank[:, :].unsqueeze(1).to_broadcast([P, TILES, E]), ALU.mult))
        link(nc.vector.tensor_reduce(col[:, 1, :], hot[:, :, :], AX.X, ALU.max))
        link(nc.vector.tensor_tensor(hot[:, :, :], hot[:, :, :], bc(col[:, 1, :]), ALU.is_equal))
        nc.vector.tensor_copy(hotb[:, :, :], hot[:, :, :]).then_inc(hot_ready, 1)
        dve.wait_ge(ex_ready, 1)
        link(nc.vector.tensor_reduce(col[:, 2, :], ex[:, :, :], AX.X, ALU.add))
        link(nc.vector.reciprocal(col[:, 3, :], col[:, 2, :]))
        dve.wait_ge(cnt_psum, 1)
        cview = psZ[0].rearrange("p (k u e) -> p k u e", k=2, e=E)
        link(nc.vector.tensor_copy(cnt[:, 0, :, :], cview[:, 1]))
        link(nc.vector.tensor_tensor(pos[:, :, :], cview[:, 0], cnt[:, 0, :, :], ALU.subtract))
        cur, step = 0, 1
        while step < TILES:
            nc.vector.tensor_copy(cnt[:, 1 - cur, 0:step, :], cnt[:, cur, 0:step, :])
            link(nc.vector.tensor_tensor(cnt[:, 1 - cur, step:, :], cnt[:, cur, step:, :], cnt[:, cur, 0:TILES - step, :], ALU.add))
            cur, step = 1 - cur, 2 * step
        link(nc.vector.tensor_tensor(pos[:, :, :], pos[:, :, :], cnt[:, cur, :, :], ALU.add))
        link(nc.vector.tensor_reduce(tot[:, :], psY.rearrange("p (k u e) -> p k e u", k=2, e=E)[:, 0], AX.X, ALU.add))
        link(nc.vector.tensor_tensor(pos[:, :, :], pos[:, :, :], tot[:, :].unsqueeze(1).to_broadcast([P, TILES, E]), ALU.add))
        link(nc.vector.tensor_scalar(pos[:, :, :], pos[:, :, :], float(CAP), None, ALU.is_lt))
        link(nc.vector.tensor_tensor(pos[:, :, :], pos[:, :, :], hot[:, :, :], ALU.mult))
        link(nc.vector.tensor_reduce(col[:, 0, :], pos[:, :, :], AX.X, ALU.max))
        nc.vector.tensor_tensor(gate[:, :], col[:, 0, :], col[:, 3, :], ALU.mult).then_inc(gate_ready, 1)
        dve.wait_ge(gate_ready, 1)
        dve.wait_ge(fold_psum, 1)
        nc.vector.tensor_copy(aqk[:, :], psFold[:, 0:P])
        nc.vector.tensor_tensor(wft[:, :], psFold[:, P:2 * P], dis[:, :], ALU.add).then_inc(fold_ready, 1)

        def gated(j):
            if j >= 2:
                dve.wait_ge(g_psum, j - 1)
            for i in range(CH):
                last = nc.vector.tensor_scalar(xg[:, j % 2, i, :], xn2[:, CH * j + i, :], gate[:, CH * j + i:CH * j + i + 1],
                                               None, ALU.mult)
            last.then_inc(xg_ready, 1)

        def moe_out(j):
            dve.wait_ge(y_psum, j + 1)
            for i in range(CH):
                u = CH * j + i
                last = nc.vector.scalar_tensor_tensor(x_res[:, u, :], psY[:, P * i:P * i + P], gate[:, u:u + 1],
                                                      x_res[:, u, :], ALU.mult, ALU.add)
            link(last)
            last = norm(lambda i: x_res[:, CH * j + i, :], lambda i: xe[:, j % 2, i, 0:D])
            last.then_inc(xe_ready, 1)

        nc.vector.memset(xe[:, :, :, D:D + 1], 1.0)
        gated(0)
        gated(1)
        for expert, due in slots():
            for name, j in due:
                if name == "t3":
                    pass
                if name == "mix":
                    dve.wait_ge(ee_ready, j + 1)
                    nc.vector.tensor_tensor(ee[:, :, :], ee[:, :, :], samet[:, :].unsqueeze(1).to_broadcast([P, CH, P]),
                                            ALU.mult).then_inc(em_ready, 1)
                    dve.wait_ge(mix_psum, j + 1)
                    for k in range(2):
                        v = psMix[k].rearrange("p (i c) -> p i c", i=2)
                        last = nc.vector.reciprocal(inv[:, 2 * k:2 * k + 2], v[:, :, D])
                    link(last)
                    for i in range(CH):
                        u = CH * j + i
                        c0 = (i % 2) * (CW // 2)
                        last = nc.vector.scalar_tensor_tensor(x_res[:, u, :], psMix[i // 2][:, c0:c0 + D], inv[:, i:i + 1],
                                                              x_res[:, u, :], ALU.mult, ALU.add)
                    last.then_inc(x3_ready, 1)
                    dve.wait_ge(x3_ready, j + 1)
                    if j >= 1:
                        dve.wait_ge(t4_psum, j)
                    norm(lambda i: x_res[:, CH * j + i, :], lambda i: xn4[:, i, :]).then_inc(xn4_ready, 1)
                if name == "f":
                    dve.wait_ge(f_psum, j + 1)
                    if j >= 2:
                        dve.wait_ge(res_out[j % 2], 16 * B * (j // 2))
                    nc.vector.tensor_tensor(res[:, j % 2, :, :], x_res[:, CH * j:CH * j + CH, :],
                                            psU.rearrange("p (i d) -> p i d", i=CH), ALU.add).then_inc(res_ready, 1)
            if expert and expert[1] == E - 1:
                j = expert[0]
                moe_out(j)
                if j + 2 < CHUNKS:
                    gated(j + 2)

    @block.tensor
    def _(pe):
        pe.wait_ge(wts_in, 16 * NW)
        pe.wait_ge(rden_ready, 1)

        def turned(j):
            pe.wait_ge(norm_ready, j + 1)
            if j >= 1:
                pe.wait_ge(xt2_ready, j)
            for i in range(CH):
                last = nc.tensor.transpose(psT2[:, P * i:P * i + P], xn2[:, CH * j + i, :], ident[:, :])
            last.then_inc(t2_psum, 1)

        def logits(j):
            pe.wait_ge(xt2_ready, j + 1)
            for i in range(CH):
                u = CH * j + i
                last = nc.tensor.matmul(psLg[:, E * u:E * u + E], xt2[:, j % 2, P * i:P * i + P], wr[:, :], start=True, stop=True)
            last.then_inc(lg_psum, 1)

        nc.tensor.matmul(psFold[:, 0:P], w1q[:, :], w1k[:, :], start=True, stop=True)
        nc.tensor.transpose(psFold[:, P:2 * P], wf[:, :], ident[:, :]).then_inc(fold_psum, 1)

        for j in range(CHUNKS):
            if j >= 1:
                pe.wait_ge(at_ready, j)
            nc.tensor.matmul(psRb.rearrange("p (s t) -> p s t", s=B), sel[:, :], den[:, :, P * j:P * j + P],
                             start=True, stop=True).then_inc(rb_psum, 1)
            if j >= 1:
                turned(j - 1)
            pe.wait_ge(at_ready, j + 1)
            if j >= 1:
                pe.wait_ge(norm_ready, j)
            for i in range(CH):
                last = nc.tensor.matmul(psProj[:, P * i:P * i + P], at[:, j % 2, i, :], wo[:, :], start=True, stop=True)
            last.then_inc(proj_psum, 1)
            if j >= 1:
                logits(j - 1)
        turned(CHUNKS - 1)
        logits(CHUNKS - 1)

        pe.wait_ge(hot_ready, 1)
        flat = hotb[:, :, :].rearrange("p u e -> p (u e)")
        nc.tensor.matmul(psZ[0][:, 0:TILES * E], incl[:, :], flat, start=True, stop=True)
        nc.tensor.matmul(psZ[0][:, TILES * E:2 * TILES * E], same[:, :], flat, start=True, stop=True)
        nc.tensor.matmul(psY[:, 0:TILES * E], less[:, :], flat, start=True, stop=True).then_inc(cnt_psum, 1)

        def gated_columns(j):
            pe.wait_ge(xg_ready, j + 1)
            pe.wait_ge(fold_ready, 1)
            if j >= 1:
                pe.wait_ge(hott_ready, 2 * j)
            for i in range(CH):
                last = nc.tensor.transpose(psG[:, P * i:P * i + P], xg[:, j % 2, i, :], ident[:, :])
            last.then_inc(g_psum, 1)
            pe.wait_ge(xgt_ready, j + 1)
            for i in range(CH):
                last = nc.tensor.matmul(psG[0:E, P * i:P * i + P], hot[:, CH * j + i, :], ident[:, :], start=True, stop=True)
            last.then_inc(ht_psum, 1)

        def expert_in(n):
            j, e = n // E, n % E
            if n >= 2:
                pe.wait_ge(hid_ready, n - 1)
            pe.wait_ge(xgt_ready, j + 1)
            pe.wait_ge(hott_ready, 2 * j + 2)
            nc.tensor.matmul(psZ[n % 2], w1[:, e, :], xgt[:, j % 2, :], start=True, stop=False)
            nc.tensor.matmul(psZ[n % 2], big[:, e, :], noth[:, j % 2, :], start=False, stop=True).then_inc(z_psum, 1)

        def expert_out(n):
            j, e = n // E, n % E
            if e == 0 and j >= 1:
                pe.wait_ge(xe_ready, j)
            pe.wait_ge(hid_ready, n + 1)
            for i in range(CH):
                nc.tensor.matmul(psY[:, P * i:P * i + P], hid[:, n % 3, P * i:P * i + P], w2[:, e, :],
                                 start=(e == 0 and i == 0), stop=False, skip_group_check=True)
            if e == E - 1:
                for i in range(CH):
                    last = nc.tensor.matmul(psY[:, P * i:P * i + P], hott[:, j % 2, P * i:P * i + P], b2r[:, :],
                                            start=False, stop=(i == CH - 1), skip_group_check=True)
                last.then_inc(y_psum, 1)

        pe.wait_ge(gate_ready, 1)
        gated_columns(0)
        expert_in(0)
        for n, (expert, due) in enumerate(slots()):
            for name, j in due:
                if name == "t3":
                    pe.wait_ge(xe_ready, j + 1)
                    if j >= 1:
                        pe.wait_ge(th_ready, j)
                    for i in range(CH):
                        last = nc.tensor.transpose(psT3[:, P * i:P * i + P], xe[:, j % 2, i, 0:D], ident[:, :])
                    last.then_inc(t3_psum, 1)
                if name == "u":
                    pe.wait_ge(xt3_ready, j + 1)
                    if j >= 1:
                        pe.wait_ge(res_ready, j)
                    nc.tensor.matmul(psU, aqk[:, :], xt3[:, :], start=True, stop=True).then_inc(u_psum, 1)
                if name == "s":
                    pe.wait_ge(ut_ready, j + 1)
                    for i in range(CH):
                        last = nc.tensor.matmul(psS[:, P * i:P * i + P], xt3[:, P * i:P * i + P], ut[:, P * i:P * i + P],
                                                start=True, stop=True)
                    last.then_inc(s_psum, 1)
                if name == "mix":
                    pe.wait_ge(em_ready, j + 1)
                    if j >= 1:
                        pe.wait_ge(xt4_ready, j)
                    for i in range(CH):
                        c0 = (i % 2) * (CW // 2)
                        last = nc.tensor.matmul(psMix[i // 2][:, c0:c0 + D + 1], ee[:, i, :], xe[:, j % 2, i, 0:D + 1],
                                                start=True, stop=True)
                    last.then_inc(mix_psum, 1)
                if name == "t4":
                    pe.wait_ge(xn4_ready, j + 1)
                    for i in range(CH):
                        last = nc.tensor.transpose(psMix[0][:, P * i:P * i + P], xn4[:, i, :], ident[:, :])
                    last.then_inc(t4_psum, 1)
                if name == "f":
                    pe.wait_ge(xt4_ready, j + 1)
                    for i in range(CH):
                        last = nc.tensor.matmul(psU[:, P * i:P * i + P], xt4[:, P * i:P * i + P], wft[:, :], start=True, stop=True)
                    last.then_inc(f_psum, 1)
            if expert:
                j, e = expert
                if e == 4 and j + 1 < CHUNKS:
                    gated_columns(j + 1)
                if n + 1 < CHUNKS * E:
                    expert_in(n + 1)
                expert_out(n)

    @block.scalar
    def _(act):
        def columns(j):
            act.wait_ge(t2_psum, j + 1)
            if j >= 2:
                act.wait_ge(lg_psum, j - 1)
            nc.scalar.copy(xt2[:, j % 2, :], psT2).then_inc(xt2_ready, 1)

        for j in range(CHUNKS):
            columns(j)
        act.wait_ge(mx_ready, 1)
        nc.scalar.activation(ex[:, :, :], lg[:, :, :], ACT.Exp).then_inc(ex_ready, 1)
        act.wait_ge(wts_in, 16 * NW)

        def gated_columns(j):
            act.wait_ge(g_psum, j + 1)
            if j >= 2:
                act.wait_ge(z_psum, E * (j - 1))
                act.wait_ge(y_psum, j - 1)
            nc.scalar.copy(xgt[:, j % 2, :], psG).then_inc(xgt_ready, 1)
            act.wait_ge(ht_psum, j + 1)
            nc.scalar.copy(hott[:, j % 2, :], psG[0:E, :]).then_inc(hott_ready, 1)
            nc.scalar.activation(noth[:, j % 2, :], psG[0:E, :], ACT.Copy, bias=1.0, scale=-1.0).then_inc(hott_ready, 1)

        def hidden(n):
            act.wait_ge(z_psum, n + 1)
            if n >= 3:
                j, e = (n - 2) // E, (n - 2) % E
                act.wait_ge(hid_ready, n - 2)
            e = n % E
            nc.scalar.activation(hid[:, n % 3, :], psZ[n % 2], ACT.Relu, bias=b1c[:, e:e + 1]).then_inc(hid_ready, 1)

        gated_columns(0)
        hidden(0)
        for n, (expert, due) in enumerate(slots()):
            for name, j in due:
                if name == "t3":
                    act.wait_ge(t3_psum, j + 1)
                    if j >= 1:
                        act.wait_ge(s_psum, j)
                    nc.scalar.copy(xt3[:, :], psT3).then_inc(xt3_ready, 1)
                if name == "u":
                    act.wait_ge(u_psum, j + 1)
                    nc.scalar.copy(ut[:, :], psU).then_inc(ut_ready, 1)
                if name == "s":
                    act.wait_ge(s_psum, j + 1)
                    nc.scalar.activation(th[:, :, :].rearrange("p i t -> p (i t)"), psS, ACT.Tanh,
                                         scale=1.0 / float(np.sqrt(np.float32(D)))).then_inc(th_ready, 1)
                    act.wait_ge(th_ready, j + 1)
                    if j >= 1:
                        act.wait_ge(mix_psum, j)
                    nc.scalar.activation(ee[:, :, :], th[:, :, :], ACT.Exp).then_inc(ee_ready, 1)
                if name == "t4":
                    act.wait_ge(t4_psum, j + 1)
                    if j >= 1:
                        act.wait_ge(f_psum, j)
                    nc.scalar.copy(xt4[:, :], psMix[0]).then_inc(xt4_ready, 1)
            if expert:
                j, e = expert
                if e == 4 and j + 1 < CHUNKS:
                    gated_columns(j + 1)
                if n + 1 < CHUNKS * E:
                    hidden(n + 1)


_INS = ["L0_attn_x", "L0_attn_Wq", "L0_attn_bq", "L0_attn_Wk", "L0_attn_bk", "L0_attn_Wv", "L0_attn_bv", "L0_attn_Wo",
        "L0_attn_bo", "L0_ffn_Wr", "L0_ffn_br", "L0_ffn_W1", "L0_ffn_b1", "L0_ffn_W2", "L0_ffn_b2", "L1_attn_Wq",
        "L1_attn_Wk", "L1_ffn_weight", "L1_ffn_disha"]


def kernel(**inputs):
    import concourse.bacc as _bacc
    from concourse.bass_utils import run_bass_kernel_spmd as _run

    nc = _bacc.Bacc("TRN2", target_bir_lowering=False, num_devices=1)
    arrays, args, consts = {}, [], {}
    for name in _INS:
        a = np.ascontiguousarray(inputs[name])
        arrays[f"in_{name}"] = a
        args.append(nc.dram_tensor(f"in_{name}", a.shape, mybir.dt.from_np(a.dtype), kind="ExternalInput").ap())
    for name, a in constants().items():
        arrays[name] = a
        consts[name] = nc.dram_tensor(name, a.shape, mybir.dt.from_np(a.dtype), kind="ExternalInput").ap()
    result = nc.dram_tensor("out_0", (B, S, D), F32, kind="ExternalOutput").ap()
    build(nc, *args, consts, result)
    return _run(nc, [arrays], core_ids=[0]).results[0]["out_0"]
```

```python
from contextlib import ExitStack

import numpy as np
import concourse.bass as bass
from concourse import mybir

F32 = mybir.dt.float32
BF16 = mybir.dt.bfloat16
ALU = mybir.AluOpType
ACT = mybir.ActivationFunctionType
AX = mybir.AxisListType

P = 128
B, S, D = 4, 1024, 128
H, HD = 16, 8
E, CAP = 8, B * S // 8
TILES = B * S // P
CH = 4
CW = CH * P
CHUNKS = TILES // CH
EPS = 1e-5
GH = 4
NG = B * H // GH
KB = S // P
QC = S // CW

MAXROWS, BIASROWS = 3, 6
RUNS = ((0, 3), (3, 2), (5, 1))
NPROD = 6
CROWS = MAXROWS + BIASROWS
ROWS = CROWS + NPROD * HD
FILL = -3.0e38
BIG = -1.0e30


def bf16_bits(a):
    return (np.ascontiguousarray(a, np.float32).view(np.uint32) >> 16).astype(np.uint16)


def top(a):
    return (np.ascontiguousarray(a, np.float32).view(np.uint32) & np.uint32(0xFFFF0000)).view(np.float32)


def constants():
    pos = np.arange(S)
    slopes = np.power(np.float32(2.0 ** (-8.0 / H)), np.arange(1, H + 1, dtype=np.float32)).astype(np.float32)
    s0 = top(slopes)
    s1 = top(slopes - s0)
    s2 = top(slopes - s0 - s1)
    krows = np.zeros((CROWS, S), np.float32)
    krows[:MAXROWS] = 1.0
    qrows = np.zeros((H, CROWS, S), np.float32)
    for part, s in enumerate((s0, s1, s2)):
        krows[MAXROWS + 2 * part] = pos // P * P
        krows[MAXROWS + 2 * part + 1] = pos % P
        qrows[:, MAXROWS + 2 * part] = s[:, None]
        qrows[:, MAXROWS + 2 * part + 1] = s[:, None]
    q, k = np.arange(P)[:, None], np.arange(P)[None, :]
    cmask = np.zeros((P, S), np.float32)
    cmask[:, S - P:] = np.where(k <= q, 0.0, FILL)
    seq, at = np.arange(P) // 32, np.arange(P) % 32
    same = seq[:, None] == seq[None, :]
    sel = np.zeros((H, CHUNKS, CHUNKS, P), np.float32)
    for j in range(CHUNKS):
        sel[np.arange(P) % H, j, j, np.arange(P)] = 1.0
    big = np.zeros((E, E, P), np.float32)
    big[np.arange(E), np.arange(E)] = BIG
    return {
        "c_qrows": bf16_bits(np.tile(qrows.reshape(H // GH, GH, CROWS, S), (B, 1, 1, 1))),
        "c_krows": bf16_bits(krows),
        "c_cmask": bf16_bits(cmask),
        "c_identb": bf16_bits(np.eye(P)),
        "c_guard": bf16_bits(np.where(q > k, FILL, 0.0)),
        "c_ident": np.eye(P, dtype=np.float32),
        "c_sel": sel.reshape(P, CHUNKS * P),
        "c_incl": bf16_bits(same & (at[:, None] <= at[None, :])),
        "c_same": bf16_bits(same),
        "c_less": bf16_bits(seq[:, None] < seq[None, :]),
        "c_big": bf16_bits(big.reshape(E, E * P)),
        "c_samet": (at[:, None] == at[None, :]).astype(np.float32),
        "c_rank": np.tile((E - np.arange(E)).astype(np.float32), (P, 1)),
    }


W_S, W_SF, W_V, W_VF, W_AF = 1.5, 0.0, 2.0, 0.0, 0.0


def attention_units():
    out = []
    for slot, c in enumerate(range(QC - 1, -1, -1)):
        last = CH * (c + 1)
        mixed = [kb for pair in zip(range(last // 2), range(last - 1, last // 2 - 1, -1)) for kb in pair]
        for kb in mixed:
            d = kb - CH * c
            q0 = P * max(d, 0)
            out.append((slot, c, kb, q0, CW - q0, d >= 0))
    return out


def steep(par, i):
    return any(2.0 ** (-8.0 / H * (GH * g + i + 1)) * (P - 1) > 40 for g in range(par, H // GH, 2))


UNITS = attention_units()
NU = len(UNITS)
MAXUNITS = [(slot, t, tuple(range(i, i + (1 if t >= CH else 2))))
            for slot, c in enumerate(range(QC - 1, -1, -1))
            for t in range(CH * c, CH * c + CH) for i in range(0, GH, 1 if t >= CH else 2)]
NM = len(MAXUNITS)
NM_SLOT = [sum(1 for m in MAXUNITS if m[0] <= slot) for slot in range(QC)]
EXPS = [(u, i, min(GH, CW // UNITS[u][4])) for u in range(NU)
        for i in range(0, GH, min(GH, CW // UNITS[u][4]))]
NE = len(EXPS)
EXPS_TO = [sum(1 for e in EXPS if e[0] <= u) for u in range(NU)]
RING = 3
FIRST = [min(u for u in range(NU) if UNITS[u][0] == s) for s in range(QC)]
LAST = [max(u for u in range(NU) if UNITS[u][0] == s) for s in range(QC)]
DIAG = [u for u in range(NU) if UNITS[u][5]]


def step_order(with_b, with_a):
    b, a = [], []
    if with_b:
        for u in range(NU + 2):
            items = [k for k in range(NE) if EXPS[k][0] == u]
            cut = (len(items) + 1) // 2
            b += [(("S", k), W_S * EXPS[k][2] * UNITS[u][4] + W_SF) for k in items[:cut]]
            if u > 1:
                b.append((("V", u - 2), W_V * UNITS[u - 2][4] + W_VF))
                if u - 2 in LAST:
                    b.append((("O", LAST.index(u - 2)), 0))
            b += [(("S", k), W_S * EXPS[k][2] * UNITS[u][4] + W_SF) for k in items[cut:]]
            if u == 1:
                b.append((("L", QC - 1), 100))
    if with_a:
        for k, (slot, t, heads) in enumerate(MAXUNITS):
            a.append((("A", k), len(heads) * (P * (t + 1) + W_AF)))
            if k + 1 == NM_SLOT[0]:
                a.append((("F", 0), 0))
            if k == NM_SLOT[0] + 2:
                a.append((("T", 0), 100))
        a.append((("F", 1), 0))
    out, done_a, done_b = [], 0.0, 0.0
    tot_a = sum(w for _, w in a) or 1
    tot_b = sum(w for _, w in b) or 1
    while a or b:
        if b and (not a or done_b / tot_b <= done_a / tot_a):
            item, w = b.pop(0)
            done_b += w
        else:
            item, w = a.pop(0)
            done_a += w
        out.append(item)
    return out


def banks_of(order, before):
    def uses(items):
        return [it for it in items if it[0] in "STL"]
    out = {}
    old, new = uses(before), uses(order)
    for j, item in enumerate(new):
        if j >= RING:
            out[item] = (j % RING, new[j - RING], False)
        else:
            last = [it for k, it in enumerate(old) if k % RING == j]
            out[item] = (j, last[-1] if last else None, True)
    return out


def build(nc, x, Wq, bq, Wk, bk, Wv, bv, Wo, bo, Wr, br, W1, b1, W2, b2, W1q, W1k, Wf, disha, consts, out):
    ctx = ExitStack()
    with ctx:
        def sb(name, shape, dt=F32):
            return ctx.enter_context(nc.sbuf_tensor(name, shape, dt))

        def sem(name):
            return ctx.enter_context(nc.semaphore(name))

        bank2 = [ctx.enter_context(nc.psum_tensor(f"bank2_{i}", [P, 2 * CW], F32)) for i in range(2)]
        bank = [ctx.enter_context(nc.psum_tensor(f"bank{i}", [P, CW], F32)) for i in range(4)]
        half = [bank2[0][:, 0:CW], bank2[0][:, CW:2 * CW], bank2[1][:, 0:CW], bank2[1][:, CW:2 * CW]]
        b0, b1_, b2_, b3 = (t[:, :] for t in bank)

        qk_dram = nc.dram_tensor("qk_rows", (NG, 2, 3, HD, GH, S), BF16).ap()
        m_dram = nc.dram_tensor("max_rows", (QC, CH * GH * 3, P), BF16).ap()
        o_dram = nc.dram_tensor("weighted_sums", (NG, GH, HD + 1, S), F32).ap()

        ident = sb("ident", [P, P])
        identb = sb("identb", [P, P], BF16)
        cmask = sb("cmask", [P, S], BF16)
        guards = sb("guards", [P, P], BF16)
        half_pow = sb("half_pow", [P, TILES // 2])
        wq, wk, wv = sb("wq", [P, D]), sb("wk", [P, D]), sb("wv", [P, D])
        bqc, bkc = sb("bqc", [P, 1]), sb("bkc", [P, 1])
        bvb = sb("bvb", [P, D])
        v_all = sb("v_all", [P, NG, KB, GH, HD + 1])
        x_res = sb("x_res", [P, TILES, D])

        w = dict(
            wo=sb("wo", [P, D]), bob=sb("bob", [P, D]), wr=sb("wr", [P, E]), brb=sb("brb", [P, E]), rank=sb("rank", [P, E]),
            sel=sb("sel", [P, CHUNKS, P]), incl=sb("incl", [P, P], BF16), same=sb("same", [P, P], BF16),
            less=sb("less", [P, P], BF16), big=sb("big", [E, E, P], BF16), samet=sb("samet", [P, P]),
            w1=sb("w1", [P, E, D]), w2=sb("w2", [P, E, D]), b1c=sb("b1c", [P, E]), b2r=sb("b2r", [E, D]),
            w1q=sb("w1q", [P, D]), w1k=sb("w1k", [P, D]), wf=sb("wf", [P, D]), dis=sb("dis", [P, D]))
        ot = sb("sums_in", [P, B, S])
        den = sb("denominators", [P, B, P])
        wts_in, o_in, xb_ready, bob_in = sem("wts_in"), sem("o_in"), sem("xb_ready"), sem("bob_in")

        def load_later_weights(queue):
            loads = [(w["wo"][H * d:H * d + H, :], Wo.rearrange("(h d) n -> d h n", d=HD)[d]) for d in range(HD)]
            loads += [(w["wr"][:, :], Wr), (w["brb"][:, :], br.partition_broadcast(P)), (w["rank"][:, :], consts["c_rank"]),
                      (w["sel"][:, :, :].rearrange("p c m -> p (c m)"), consts["c_sel"]),
                      (w["incl"][:, :], consts["c_incl"].bitcast(BF16)), (w["same"][:, :], consts["c_same"].bitcast(BF16)),
                      (w["less"][:, :], consts["c_less"].bitcast(BF16)),
                      (w["big"][:, :, :].rearrange("k e f -> k (e f)"), consts["c_big"].bitcast(BF16)),
                      (w["samet"][:, :], consts["c_samet"]), (w["b2r"][:, :], b2),
                      (w["w1"][:, :, :], W1.rearrange("e d f -> d e f")), (w["w2"][:, :, :], W2.rearrange("e f d -> f e d")),
                      (w["w1q"][:, :], W1q), (w["w1k"][:, :], W1k), (w["wf"][:, :], Wf)]
            rd = disha.shape[0]
            loads += [(w["dis"][rd * i:rd * i + rd, :], disha) for i in range(D // rd)]
            for dst, src in loads:
                queue.dma_start(dst, src).then_inc(wts_in, 16)
            queue.dma_start(w["b1c"][:, :], b1.rearrange("e f -> f e"), allow_slow_non_contiguous=True).then_inc(wts_in, 16)

        NLATER = HD + 15 + D // disha.shape[0] + 1

        def load_sums(sp, b):
            groups = slice(b * H // GH, (b + 1) * H // GH)
            sp.dma_start(ot[:, b, :], o_dram[groups, :, 0:HD].rearrange("g i r s -> r (g i) s")).then_inc(o_in, 16)
            sp.dma_start(den[:, b, :],
                         o_dram[groups, :, HD].rearrange("g i (j q) -> (g i) j q", q=P)).then_inc(o_in, 16)

        const_in = sem("const_in")
        w_in = sem("w_in")
        x_in = [sem(f"x_in{b}") for b in range(B)]
        xres_in = sem("xres_in")

        scale = 1.0 / float(np.sqrt(np.float32(HD)))

        att = ExitStack()
        ctx.enter_context(att)

        def asb(name, shape, dt=F32):
            return att.enter_context(nc.sbuf_tensor(name, shape, dt))

        qa, ka = asb("q_for_max", [P, 2, GH, S], BF16), asb("k_for_max", [P, 2, GH, S], BF16)
        qb, kb_ = asb("q_for_exp", [P, 2, GH, S], BF16), asb("k_for_exp", [P, 2, GH, S], BF16)
        pad_zero, krows_in = sem("pad_zero"), sem("krows_in")
        parts_out = [sem(f"parts_out{i}") for i in range(2)]
        a_in = [sem(f"a_in{i}") for i in range(2)]
        b_in = [sem(f"b_in{i}") for i in range(2)]
        a_scores, s_scores, sp_turns = sem("a_scores"), sem("s_scores"), sem("sp_turns")
        const_rows = consts["c_qrows"].bitcast(BF16).rearrange("n i c s -> n c i s")
        mb = MAXROWS
        NA = 1 + 2 * len(RUNS)

        def load_max_operands(sp, n, par, late):
            if late:
                sp.wait_ge(a_scores, (n - 1) * NM)
                sp.sem_inc(sp_turns, 1)
            sp.dma_start(qa[0:CROWS, par, :, :], const_rows[bass.ds(n, 1)].rearrange("n c i s -> (n c) i s")).then_inc(a_in[par], 16)
            for m, (p0, count) in enumerate(RUNS):
                r0, r1 = CROWS + HD * p0, CROWS + HD * (p0 + count)
                sp.dma_start(qa[r0:r1, par, :, :].rearrange("r i s -> r (i s)"),
                             qk_dram[bass.ds(n, 1), 0, 0:count].rearrange("n m d i s -> (n m d) (i s)")).then_inc(a_in[par], 16)
                sp.dma_start(ka[r0:r1, par, :, :].rearrange("r i s -> r (i s)"),
                             qk_dram[bass.ds(n, 1), 1, m].rearrange("n d i s -> n d (i s)")
                             .to_broadcast([count, HD, GH * S])).then_inc(a_in[par], 16)

        def copy_exp_operands(sp, n, half, par, late):
            sp.wait_ge(a_in[par], 16 * NA * (half + 1))
            sp.sem_inc(sp_turns, 1)
            if late:
                sp.wait_ge(s_scores, (n - 1) * NE)
            sp.sem_inc(sp_turns, 1)
            sp.dma_start(qb[mb:ROWS, par, :, :], qa[mb:ROWS, par, :, :]).then_inc(b_in[par], 16)
            sp.dma_start(kb_[0:ROWS, par, :, :], ka[0:ROWS, par, :, :]).then_inc(b_in[par], 16)

        pre = ExitStack()
        with pre:
            def tsb(name, shape, dt=F32):
                return pre.enter_context(nc.sbuf_tensor(name, shape, dt))

            xn = tsb("xn", [P, TILES, D])
            stats = tsb("stats0", [P, 2, KB, 6])
            mv = tsb("mv0", [P, 2, KB, 2])
            ve = tsb("ve0", [P, 2, KB])
            rs = tsb("rs0", [P, 2, KB])
            nt = tsb("nt0", [P, 3, KB])
            xt = tsb("xt0", [P, 2, CW])
            full = tsb("qk_full", [P, 2, 2, CW])
            rest = tsb("qk_rest", [P, 2, 2, CW])
            parts = tsb("qk_parts", [P, 2, 2, 3, S], BF16)
            bsc = tsb("bsc", [P, 2])
            wqk = tsb("wqk", [P, 2, D])

            norm_in, var_ready, pow_ready, xn_ready = sem("norm_chain"), sem("var_ready"), sem("pow_ready"), sem("xn_ready")
            xt_psum, xt_ready, qk_psum, v_psum = sem("xt_psum"), sem("xt_ready"), sem("qk_psum"), sem("v_psum")
            bias_ready, hi_ready, rest_ready, parts_ready = sem("bias_ready"), sem("hi_ready"), sem("rest_ready"), sem("parts_ready")
            mid_ready, v_ready, ones_ready = sem("mid_ready"), sem("v_ready"), sem("ones_ready")
            half_ready = sem("half_ready")
            NCONST = 3
            NW = 5 + 2 * (H // GH)

            psT = [half[0], half[1]]
            psQ = [b0, b1_]
            psK = [b2_, b3]
            psV = [half[2], half[3]]
            block = pre.enter_context(nc.Block())

            @block.sync
            def _(sp):
                for b in range(B):
                    sp.dma_start(xn[:, b * KB:(b + 1) * KB, :],
                                 x[b].rearrange("(u p) d -> p u d", p=P)).then_inc(x_in[b], 16)
                sp.dma_start(cmask[:, :], consts["c_cmask"].bitcast(BF16)).then_inc(const_in, 16)
                sp.dma_start(identb[:, :], consts["c_identb"].bitcast(BF16)).then_inc(const_in, 16)
                sp.dma_start(guards[:, :], consts["c_guard"].bitcast(BF16)).then_inc(const_in, 16)
                sp.wait_ge(pad_zero, 4)
                for par in range(2):
                    for i in range(GH):
                        sp.dma_start(ka[0:CROWS, par, i, :], consts["c_krows"].bitcast(BF16)).then_inc(krows_in, 16)
                for s in range(B):
                    sp.dma_start(x_res[32 * s:32 * s + 32, :, :],
                                 x[s].rearrange("(u t) d -> t u d", t=32)).then_inc(xres_in, 16)
                for b in range(B):
                    sp.wait_ge(parts_ready, 2 * 2 * (b + 1))
                    sp.wait_ge(mid_ready, 2 * 2 * (b + 1))
                    sp.wait_ge(hi_ready, 2 * 2 * (b + 1))
                    for z in range(2):
                        for m in range(3):
                            dst = qk_dram[4 * b:4 * b + 4, z, m]
                            sp.dma_start(dst.rearrange("g d i s -> g (d i) s"),
                                         parts[:, b % 2, z, m, :]).then_inc(parts_out[b % 2], 16)
                    if b == 0:
                        sp.wait_ge(krows_in, 16 * 2 * GH)
                        sp.wait_ge(parts_out[0], 16 * 6)
                        load_max_operands(sp, 0, 0, False)
                        load_max_operands(sp, 1, 1, False)

            @block.gpsimd
            def _(pool):
                nc.gpsimd.memset(half_pow[:, :], -0.5).then_inc(half_ready, 1)
                nc.gpsimd.memset(v_all[:, :, :, :, HD:HD + 1], 1.0).then_inc(ones_ready, 1)
                pool.wait_ge(half_ready, 1)

                def power(b):
                    pool.wait_ge(var_ready, b + 1)
                    nc.gpsimd.tensor_tensor(rs[:, b % 2, :], ve[:, b % 2, :], half_pow[:, 0:KB], ALU.pow).then_inc(pow_ready, 1)

                nc.gpsimd.memset(qa[:, :, :, :].bitcast(F32), 0.0).then_inc(pad_zero, 1)
                power(0)
                power(1)
                nc.gpsimd.memset(ka[:, :, :, :].bitcast(F32), 0.0).then_inc(pad_zero, 1)
                nc.gpsimd.memset(kb_[:, :, :, :].bitcast(F32), 0.0).then_inc(pad_zero, 1)
                for k in range(CHUNKS):
                    if k == 1 or k == 3:
                        power(k // 2 + 2)
                    for z in range(2):
                        pool.wait_ge(mid_ready, 2 * k + z + 1)
                        to = slice(CW * (k % 2), CW * (k % 2) + CW)
                        nc.gpsimd.tensor_tensor(parts[:, k // 2 % 2, z, 2, to], rest[:, k % 2, z, :],
                                                parts[:, k // 2 % 2, z, 1, to], ALU.subtract).then_inc(parts_ready, 1)

            @block.vector
            def _(dve):
                chain = [0]

                def link(ins):
                    chain[0] += 1
                    ins.then_inc(norm_in, 1)
                    dve.wait_ge(norm_in, chain[0])

                def norm(b):
                    dve.wait_ge(x_in[b], 16)
                    for i in range(KB):
                        last = nc.vector.bn_stats(stats[:, b % 2, i, :], xn[:, KB * b + i, :])
                    link(last)
                    for i in range(KB):
                        last = nc.vector.bn_aggr(mv[:, b % 2, i, :], stats[:, b % 2, i, :])
                    link(last)
                    nc.vector.tensor_scalar_add(ve[:, b % 2, :], mv[:, b % 2, :, 1], EPS).then_inc(var_ready, 1)
                    dve.wait_ge(pow_ready, b + 1)
                    link(nc.vector.tensor_tensor(nt[:, 0, :], ve[:, b % 2, :], rs[:, b % 2, :], ALU.mult))
                    link(nc.vector.tensor_tensor(nt[:, 1, :], nt[:, 0, :], rs[:, b % 2, :], ALU.mult))
                    link(nc.vector.tensor_scalar(nt[:, 2, :], nt[:, 1, :], -0.5, 1.5, ALU.mult, ALU.add))
                    link(nc.vector.tensor_tensor(rs[:, b % 2, :], rs[:, b % 2, :], nt[:, 2, :], ALU.mult))
                    for i in range(KB):
                        u = KB * b + i
                        last = nc.vector.tensor_scalar(xn[:, u, :], xn[:, u, :], mv[:, b % 2, i, 0:1],
                                                       rs[:, b % 2, i:i + 1], ALU.subtract, ALU.mult)
                        if i % CH == CH - 1:
                            last.then_inc(xn_ready, 1)

                def cut(k):
                    for z in range(2):
                        dve.wait_ge(hi_ready, 2 * k + z + 1)
                        if k >= 2:
                            dve.wait_ge(parts_ready, 2 * (k - 2) + z + 1)
                        if k >= 4:
                            dve.wait_ge(parts_out[k // 2 % 2], 16 * 6 * (k // 4))
                        to = slice(CW * (k % 2), CW * (k % 2) + CW)
                        link(nc.vector.tensor_tensor(rest[:, k % 2, z, :], full[:, k % 2, z, :],
                                                     parts[:, k // 2 % 2, z, 0, to], ALU.subtract))
                        nc.vector.tensor_copy(parts[:, k // 2 % 2, z, 1, to], rest[:, k % 2, z, :]).then_inc(mid_ready, 1)
                    dve.wait_ge(v_psum, k + 1)
                    dve.wait_ge(ones_ready, 1)
                    for i in range(CH):
                        t = CH * k + i
                        dst = v_all[:, 4 * (t // KB):4 * (t // KB) + 4, t % KB, :, 0:HD]
                        last = nc.vector.tensor_tensor(
                            dst, psV[k % 2][:, P * i:P * i + P].rearrange("p (g i d) -> p g i d", g=4, i=GH),
                            bvb[:, :].rearrange("p (g i d) -> p g i d", g=4, i=GH), ALU.add)
                    last.then_inc(v_ready, 1)

                nc.vector.memset(qb[:, :, :, :].bitcast(F32), 0.0).then_inc(pad_zero, 1)
                norm(0)
                norm(1)
                dve.wait_ge(w_in, 16 * NW)
                for k in range(CHUNKS):
                    if k == 1 or k == 3:
                        norm(k // 2 + 2)
                    cut(k)

            @block.tensor
            def _(pe):
                pe.wait_ge(w_in, 16 * NW)

                def turn(k):
                    pe.wait_ge(xn_ready, k + 1)
                    if k >= 2:
                        pe.wait_ge(xt_ready, k - 1)
                    for i in range(CH):
                        last = nc.tensor.transpose(psT[k % 2][:, P * i:P * i + P], xn[:, CH * k + i, :], ident[:, :])
                    last.then_inc(xt_psum, 1)

                def project(k):
                    pe.wait_ge(xt_ready, k + 1)
                    if k >= 2:
                        pe.wait_ge(hi_ready, 2 * (k - 1))
                        pe.wait_ge(v_ready, k - 1)
                    nc.tensor.matmul(psQ[k % 2], wqk[:, 0, :], xt[:, k % 2, :], start=True, stop=True).then_inc(qk_psum, 1)
                    nc.tensor.matmul(psK[k % 2], wqk[:, 1, :], xt[:, k % 2, :], start=True, stop=True).then_inc(qk_psum, 1)
                    for i in range(CH):
                        last = nc.tensor.matmul(psV[k % 2][:, P * i:P * i + P], xt[:, k % 2, P * i:P * i + P], wv[:, :],
                                                start=True, stop=True)
                    last.then_inc(v_psum, 1)

                turn(0)
                pe.wait_ge(bias_ready, 4)
                for k in range(CHUNKS):
                    if k + 1 < CHUNKS:
                        turn(k + 1)
                    project(k)

            @block.scalar
            def _(act):
                act.dma_start(ident[:, :], consts["c_ident"]).then_inc(w_in, 16)
                act.dma_start(wq[:, :], Wq).then_inc(w_in, 16)
                act.dma_start(wk[:, :], Wk).then_inc(w_in, 16)
                for g in range(H // GH):
                    for dst, src in ((bqc, bq), (bkc, bk)):
                        act.dma_start(dst[32 * g:32 * g + 32, :], src.rearrange("(g i d o) -> g d i o", g=4, i=GH, o=1)[g],
                                      allow_slow_non_contiguous=True).then_inc(w_in, 16)
                act.dma_start(wv[:, :], Wv).then_inc(w_in, 16)
                act.dma_start(bvb[:, :], bv.partition_broadcast(P)).then_inc(w_in, 16)
                act.wait_ge(w_in, 16 * NW)
                nc.scalar.mul(bsc[:, 0:1], bqc[:, :], scale).then_inc(bias_ready, 1)
                nc.scalar.copy(bsc[:, 1:2], bkc[:, :]).then_inc(bias_ready, 1)
                for i, w in enumerate((wq, wk)):
                    nc.scalar.copy(wqk[:, i, :].rearrange("p (g d i) -> p g d i", g=4, d=HD),
                                   w[:, :].rearrange("p (g i d) -> p g d i", g=4, i=GH)).then_inc(bias_ready, 1)
                act.wait_ge(bias_ready, 4)

                def take(k):
                    act.wait_ge(xt_psum, k + 1)
                    if k >= 2:
                        act.wait_ge(v_psum, k - 1)
                    nc.scalar.copy(xt[:, k % 2, :], psT[k % 2]).then_inc(xt_ready, 1)

                take(0)
                for k in range(CHUNKS):
                    if k + 1 < CHUNKS:
                        take(k + 1)
                    for z, ps in enumerate((psQ, psK)):
                        act.wait_ge(qk_psum, 2 * k + z + 1)
                        if k >= 2:
                            act.wait_ge(mid_ready, 2 * (k - 2) + z + 1)
                        if k >= 4:
                            act.wait_ge(parts_out[k // 2 % 2], 16 * 6 * (k // 4))
                        to = slice(CW * (k % 2), CW * (k % 2) + CW)
                        sc = scale if z == 0 else 1.0
                        nc.scalar.activation(full[:, k % 2, z, :], ps[k % 2], ACT.Identity, bias=bsc[:, z:z + 1], scale=sc)
                        nc.scalar.activation(parts[:, k // 2 % 2, z, 0, to], ps[k % 2], ACT.Identity,
                                             bias=bsc[:, z:z + 1], scale=sc).then_inc(hi_ready, 1)

        with att:
            vb = asb("v_group", [P, 2, KB, GH, HD + 1])
            probs = asb("probs", [P, 3, GH, CW])
            junk = asb("junk", [P, 2, S], BF16)
            mx = asb("row_max", [P, 2, KB * GH])
            mrest = asb("max_rest", [P, QC, 2, CH * GH])
            mparts = asb("max_parts", [P, QC, CH, GH, 3], BF16)
            mrows = asb("max_rows_sb", [CH * GH * 3, QC, P], BF16)
            osum = asb("osum", [P, QC, CW])

            m_in = [[sem(f"m_in{i}{j}") for j in range(QC)] for i in range(2)]
            m_out = [sem(f"m_out{j}") for j in range(QC)]
            o_out = [sem(f"o_out{j}") for j in range(QC)]
            a_max, cut_chain, mparts_ready = sem("a_max"), sem("cut_chain"), sem("mparts_ready")
            mt_psum, mrows_ready = sem("mt_psum"), sem("mrows_ready")
            o_clear = sem("o_clear")
            exp_ready, masked, pv_done, o_ready = sem("exp_ready"), sem("masked"), sem("pv_done"), sem("o_ready")

            dve_turns, pe_turns, pool_turns = sem("dve_turns"), sem("pe_turns"), sem("pool_turns")

            psA = [bank2[0][:, :], bank2[1][:, :]]
            psS = [b0, b1_, b2_]
            psO = b3
            block = att.enter_context(nc.Block())

            def load_values(sp, n, par, late):
                if late:
                    sp.wait_ge(pv_done, (n - 1) * NU)
                    sp.sem_inc(sp_turns, 1)
                sp.dma_start(vb[:, par, :, :, :].rearrange("p k i c -> p (k i c)"),
                             v_all[:, bass.ds(n, 1)].rearrange("p n k i c -> p (n k i c)")).then_inc(b_in[par], 16)

            @block.sync
            def _(sp):
                for i in range(2):
                    sp.wait_ge(parts_out[i], 16 * 6 * 2)
                sp.wait_ge(v_ready, CHUNKS)

                def rows_of_maxima(n, par, half_n, slot, late):
                    c = QC - 1 - slot
                    sp.wait_ge(m_out[slot], 16 * n + 16)
                    if late:
                        sp.wait_ge(s_scores, (n - 1) * NE)
                    src = m_dram[slot].rearrange("(t i m) q -> m i t q", t=CH, i=GH)
                    for i in range(GH):
                        dst = qb[0:mb, par, i, CW * c:CW * c + CW]
                        sp.dma_start(dst.rearrange("m (t q) -> m t q", t=CH), src[:, i]).then_inc(m_in[par][slot], 16)

                def step(n, half_n, par, first, with_a, load2, late):
                    if load2:
                        sp.wait_ge(b_in[par], 48 * (half_n + 1))
                        sp.sem_inc(sp_turns, 1)
                        load_max_operands(sp, n + 2, par, True)
                    if with_a:
                        copy_exp_operands(sp, n + 1, half_n + par, 1 - par, late)
                        load_values(sp, n + 1, 1 - par, late)
                    for item in step_order(True, with_a):
                        if item[0] == "O":
                            slot = item[1]
                            c = QC - 1 - slot
                            sp.wait_ge(o_ready, n * QC + slot + 1)
                            sp.sem_inc(sp_turns, 1)
                            for i in range(GH):
                                sp.dma_start(o_dram[bass.ds(n, 1), i, :, CW * c:CW * c + CW].rearrange("n r s -> (n r) s"),
                                             osum[32 * i:32 * i + HD + 1, slot, :]).then_inc(o_out[slot], 16)
                        elif item[0] == "T":
                            rows_of_maxima(n + 1, 1 - par, None, item[1], late)
                        elif item[0] == "L":
                            rows_of_maxima(n, par, None, item[1], not first)

                copy_exp_operands(sp, 0, 0, 0, False)
                load_values(sp, 0, 0, False)
                sp.dma_start(w["bob"][:, :], bo.partition_broadcast(P)).then_inc(bob_in, 16)
                for item in step_order(False, True):
                    if item[0] == "T":
                        rows_of_maxima(0, 0, None, item[1], False)
                step(0, 0, 0, True, True, True, False)
                step(1, 0, 1, True, True, True, True)
                with sp.Fori(1, NG // 2 - 1) as it:
                    step(2 * it, it, 0, False, True, True, True)
                    step(2 * it + 1, it, 1, False, True, True, True)
                for slot in range(QC):
                    sp.wait_ge(o_out[slot], 16 * GH * (NG - GH))
                for b in range(B - 1):
                    load_sums(sp, b)
                step(NG - 2, NG // 2 - 1, 0, False, True, False, True)
                step(NG - 1, NG // 2 - 1, 1, False, False, False, True)
                for slot in range(QC):
                    sp.wait_ge(o_out[slot], 16 * GH * NG)
                load_sums(sp, B - 1)

            @block.tensor
            def _(pe):
                pe.wait_ge(v_ready, CHUNKS)
                pe.wait_ge(hi_ready, 2 * CHUNKS)
                pe.wait_ge(krows_in, 16 * 2 * GH)
                pe.wait_ge(const_in, 16 * NCONST)

                def max_scores(n, par, half_n, k, ready):
                    slot, t, heads = MAXUNITS[k]
                    if k == 0:
                        pe.wait_ge(a_in[par], 16 * NA * (half_n + 1))
                    if not ready or k >= 2:
                        pe.wait_ge(a_max, n * NM + k - 1)
                    w = P * (t + 1)
                    for j, i in enumerate(heads):
                        for f in range(0, w, CW):
                            e = min(w, f + CW)
                            last = nc.tensor.matmul(psA[k % 2][:, CW * j + f:CW * j + e], qa[:, par, i, P * t:P * t + P],
                                                    ka[:, par, i, f:e], start=True, stop=True)
                    last.then_inc(a_scores, 1)

                def bank_free(n, use):
                    bank, user, in_last = use
                    if user is None:
                        return
                    group = n - 1 if in_last else n
                    if user[0] == "S":
                        pe.wait_ge(exp_ready, group * NE + user[1] + 1)
                    else:
                        pe.wait_ge(mrows_ready, (group + (user[0] == "T")) * QC + user[1] + 1)

                def turn_maxima(n, slot, use, group):
                    bank_free(group, use)
                    pe.wait_ge(mparts_ready, n * QC + slot + 1)
                    pe.sem_inc(pe_turns, 1)
                    nc.tensor.transpose(psS[use[0]][0:CH * GH * 3, :].bitcast(BF16)[:, 0:P],
                                        mparts[:, slot, :, :, :].rearrange("p t i m -> p (t i m)"),
                                        identb[:, :]).then_inc(mt_psum, 1)

                def scores(n, par, half_n, k, use):
                    u, i0, nh = EXPS[k]
                    slot, c, kb, q0, w, diag = UNITS[u]
                    if k == 0:
                        pe.wait_ge(b_in[par], 48 * (half_n + 1))
                    if u in FIRST and i0 == 0:
                        pe.wait_ge(m_in[par][slot], 64 * (half_n + 1))
                    bank_free(n, use)
                    for j in range(nh):
                        i = i0 + j
                        guard = diag and steep(par, i)
                        last = nc.tensor.matmul(psS[use[0]][:, w * j:w * j + w], kb_[:, par, i, P * kb:P * kb + P],
                                                qb[:, par, i, CW * c + q0:CW * c + q0 + w], start=True, stop=not guard)
                        if guard:
                            last = nc.tensor.matmul(psS[use[0]][:, w * j:w * j + P], identb[:, :], guards[:, :],
                                                    start=False, stop=True)
                    last.then_inc(s_scores, 1)

                def weighted_sums(n, par, u, first):
                    slot, c, kb, q0, w, diag = UNITS[u]
                    pe.wait_ge(exp_ready, n * NE + EXPS_TO[u])
                    if diag:
                        pe.wait_ge(masked, n * len(DIAG) + DIAG.index(u) + 1)
                    if first and u == 0:
                        pe.wait_ge(o_clear, 1)
                    if u in FIRST and not (first and slot == 0):
                        pe.wait_ge(o_ready, n * QC + slot)
                    for i in range(GH):
                        last = nc.tensor.matmul(psO[32 * i:32 * i + HD + 1, q0:q0 + w], vb[:, par, kb, i, :],
                                                probs[:, u % 3, i, 0:w], start=u in FIRST, stop=u in LAST,
                                                tile_position=(0, 32 * i))
                    last.then_inc(pv_done, 1)

                def step(n, half_n, par, first, with_a, half_next=None):
                    order = step_order(True, with_a)
                    use = banks_of(order, step_order(not first, True))
                    for item in order:
                        if item[0] == "A":
                            max_scores(n + 1, 1 - par, half_next, item[1], False)
                        elif item[0] == "T":
                            turn_maxima(n + 1, item[1], use[item], n)
                        elif item[0] == "L":
                            turn_maxima(n, item[1], use[item], n)
                        elif item[0] == "S":
                            scores(n, par, half_n, item[1], use[item])
                        elif item[0] == "V":
                            weighted_sums(n, par, item[1], first)

                order = step_order(False, True)
                use = banks_of(order, [])
                for item in order:
                    if item[0] == "A":
                        max_scores(0, 0, 0, item[1], True)
                    elif item[0] == "T":
                        turn_maxima(0, item[1], use[item], 0)
                step(0, 0, 0, True, True, 0)
                step(1, 0, 1, False, True, 1)
                with pe.Fori(1, NG // 2 - 1) as it:
                    step(2 * it, it, 0, False, True, it)
                    step(2 * it + 1, it, 1, False, True, it + 1)
                step(NG - 2, NG // 2 - 1, 0, False, True, NG // 2 - 1)
                step(NG - 1, NG // 2 - 1, 1, False, False)

            @block.vector
            def _(dve):
                dve.wait_ge(const_in, 16 * NCONST)
                dve.wait_ge(hi_ready, 2 * CHUNKS)
                nc.vector.memset(psO, 0.0).then_inc(o_clear, 1)

                def row_max(n, par, k):
                    slot, t, heads = MAXUNITS[k]
                    w = P * (t + 1)
                    dve.wait_ge(a_scores, n * NM + k + 1)
                    dve.sem_inc(dve_turns, 1)
                    for j, i in enumerate(heads):
                        last = nc.vector.tensor_tensor_reduce(
                            out=junk[:, k % 2, CW * j:CW * j + w], in0=psA[k % 2][:, CW * j:CW * j + w],
                            in1=cmask[:, S - w:S], scale=1.0, scalar=FILL, op0=ALU.add, op1=ALU.max,
                            accum_out=mx[:, par, t * GH + i:t * GH + i + 1])
                    last.then_inc(a_max, 1)

                def cut_maxima(n, par, slot, first):
                    c = QC - 1 - slot
                    done = (n * QC + slot) * 3
                    m = mx[:, par, CH * GH * c:CH * GH * (c + 1)]
                    part = mparts[:, slot, :, :, :].rearrange("p t i m -> p (t i) m")
                    dve.wait_ge(a_max, n * NM + NM_SLOT[slot])
                    if not first:
                        dve.wait_ge(mt_psum, (n - 1) * QC + slot + 1)
                    nc.vector.tensor_scalar_mul(part[:, :, 0], m, -1.0).then_inc(cut_chain, 1)
                    dve.wait_ge(cut_chain, done + 1)
                    nc.vector.scalar_tensor_tensor(mrest[:, slot, 0, :], m, -1.0, part[:, :, 0],
                                                   ALU.mult, ALU.subtract).then_inc(cut_chain, 1)
                    dve.wait_ge(cut_chain, done + 2)
                    nc.vector.tensor_copy(part[:, :, 1], mrest[:, slot, 0, :]).then_inc(cut_chain, 1)
                    dve.wait_ge(cut_chain, done + 3)
                    nc.vector.tensor_tensor(part[:, :, 2], mrest[:, slot, 0, :], part[:, :, 1],
                                            ALU.subtract).then_inc(mparts_ready, 1)

                def step(n, par, first, order):
                    for item in order:
                        if item[0] == "A":
                            row_max(n, par, item[1])
                        elif item[0] == "F":
                            cut_maxima(n, par, item[1], first)

                step(0, 0, True, step_order(False, True))
                step(1, 1, False, step_order(True, True))
                step(2, 0, False, step_order(True, True))
                with dve.Fori(1, NG // 2 - 1) as it:
                    step(2 * it + 1, 1, False, step_order(True, True))
                    step(2 * it + 2, 0, False, step_order(True, True))
                step(NG - 1, 1, False, step_order(True, True))

            @block.scalar
            def _(act):
                def exps(n, k, bank, first):
                    u, i0, nh = EXPS[k]
                    w = UNITS[u][4]
                    if i0 == 0 and (not first or u >= 3):
                        act.wait_ge(pv_done, n * NU + u - 2)
                    act.wait_ge(s_scores, n * NE + k + 1)
                    nc.scalar.activation(probs[:, u % 3, i0:i0 + nh, 0:w],
                                         psS[bank][:, 0:nh * w].rearrange("p (i q) -> p i q", i=nh),
                                         ACT.Exp).then_inc(exp_ready, 1)

                def maxima_rows(n, par, half_last, slot, bank, first):
                    act.wait_ge(mt_psum, n * QC + slot + 1)
                    if not first:
                        act.wait_ge(m_out[slot], 16 * n)
                    nc.scalar.copy(mrows[:, slot, :], psS[bank][0:CH * GH * 3, :].bitcast(BF16)[:, 0:P]).then_inc(mrows_ready, 1)
                    act.wait_ge(mrows_ready, n * QC + slot + 1)
                    if not first:
                        act.wait_ge(m_in[1 - par][slot], 64 * (half_last + 1))
                    act.dma_start(m_dram[slot], mrows[:, slot, :]).then_inc(m_out[slot], 16)

                def sums_out(n, slot, first):
                    act.wait_ge(pv_done, n * NU + LAST[slot] + 1)
                    if not first:
                        act.wait_ge(o_out[slot], 16 * GH * n)
                    nc.scalar.copy(osum[:, slot, :], psO).then_inc(o_ready, 1)

                def step(n, par, half_n, first, with_a):
                    order = step_order(True, with_a)
                    use = banks_of(order, [])
                    for item in order:
                        if item[0] == "S":
                            exps(n, item[1], use[item][0], first)
                        elif item[0] == "T":
                            maxima_rows(n + 1, 1 - par, half_n, item[1], use[item][0], False)
                        elif item[0] == "L":
                            maxima_rows(n, par, half_n - 1 + par, item[1], use[item][0], first)
                        elif item[0] == "O":
                            sums_out(n, item[1], first)

                load_later_weights(act)
                for item, use in banks_of(step_order(False, True), []).items():
                    maxima_rows(0, 0, 0, item[1], use[0], True)
                step(0, 0, 0, True, True)
                step(1, 1, 0, False, True)
                with act.Fori(1, NG // 2 - 1) as it:
                    step(2 * it, 0, it, False, True)
                    step(2 * it + 1, 1, it, False, True)
                step(NG - 2, 0, NG // 2 - 1, False, True)
                step(NG - 1, 1, NG // 2 - 1, False, False)

            @block.gpsimd
            def _(pool):
                def mask(n, u):
                    pool.wait_ge(exp_ready, n * NE + EXPS_TO[u])
                    pool.sem_inc(pool_turns, 1)
                    tri = probs[:, u % 3, :, 0:P]
                    nc.gpsimd.affine_select(out=tri, in_=tri, compare_op=ALU.is_ge, fill=0.0, base=0,
                                            pattern=[[0, GH], [1, P]], channel_multiplier=-1).then_inc(masked, 1)

                pool.wait_ge(xres_in, 16 * B)
                pool.wait_ge(bob_in, 16)
                for j in range(CHUNKS):
                    rows = x_res[:, CH * j:CH * j + CH, :]
                    nc.gpsimd.tensor_tensor(rows, rows, w["bob"][:, :].unsqueeze(1).to_broadcast([P, CH, D]),
                                            ALU.add).then_inc(xb_ready, 1)
                for u in DIAG:
                    mask(0, u)
                with pool.Fori(1, NG) as n:
                    for u in DIAG:
                        mask(n, u)

        later_stages(nc, ctx, sb, sem, w, dict(
            x_res=x_res, ot=ot, den=den, ident=ident, half_pow=half_pow, half=half, banks=[b0, b1_, b2_, b3],
            wts_in=wts_in, o_in=o_in, xb_ready=xb_ready, n_later=NLATER), out)


def later_stages(nc, ctx, sb, sem, w, shared, out):
    x_res, ot, den, ident, half_pow, half, banks = (
        shared[k] for k in ("x_res", "ot", "den", "ident", "half_pow", "half", "banks"))
    wts_in, o_in, xb_ready, n_later = (shared[k] for k in ("wts_in", "o_in", "xb_ready", "n_later"))
    wo, wr, brb, rank, sel, incl, same, less = (
        w[k] for k in ("wo", "wr", "brb", "rank", "sel", "incl", "same", "less"))
    big, samet, w1, w2, b1c, b2r, w1q, w1k, wf, dis = (
        w[k] for k in ("big", "samet", "w1", "w2", "b1c", "b2r", "w1q", "w1k", "wf", "dis"))
    aqk = sb("aqk", [P, D])
    wft = sb("wft", [P, D])

    at = sb("at", [P, 2, CH, P])
    xn2 = sb("xn2", [P, TILES, D])
    xt2 = sb("xt2", [P, 2, CW])
    stats = sb("stats1", [P, CH, 6])
    HT = TILES // 2
    stats2, mv2 = sb("stats2", [P, TILES, 6]), sb("mv2", [P, TILES, 2])
    ve2, rs2, nt2 = sb("ve2", [P, TILES]), sb("rs2", [P, TILES]), sb("nt2", [P, 4, TILES])
    mv = sb("mv1", [P, CH, 2])
    ve, rs = sb("ve1", [P, CH]), sb("rs1", [P, CH])
    nt = sb("nt1", [P, 3, CH])
    lg = sb("lg", [P, TILES, E])
    ex = sb("ex", [P, TILES, E])
    hot = sb("hot", [P, TILES, E])
    hotb = sb("hotb", [P, TILES, E], BF16)
    cnt = sb("cnt", [P, 2, TILES, E])
    pos = sb("pos", [P, TILES, E])
    col = sb("col", [P, 4, TILES])
    tot = sb("tot", [P, E])
    gate = sb("gate", [P, TILES])
    hott = sb("hott", [E, 2, CW])
    noth = sb("noth", [E, 2, CW], BF16)
    xg = sb("xg", [P, 2, CH, D])
    xgt = sb("xgt", [P, 2, CW])
    hid = sb("hid", [P, 3, CW])
    xe = sb("xe", [P, 2, CH, D + 4])
    xt3 = sb("xt3", [P, CW])
    ut = sb("ut", [P, CW])
    th = sb("th", [P, CH, P])
    ee = sb("ee", [P, CH, P])
    inv = sb("inv", [P, CH])
    xn4 = sb("xn4", [P, CH, D])
    xt4 = sb("xt4", [P, CW])
    res = sb("res", [P, 2, CH, D])

    res_out = [sem(f"res_out{i}") for i in range(2)]
    v_chain = sem("v_chain")
    ve2_ready, pw2_ready, stats_ready, scales_ready = (sem(n) for n in ("ve2_ready", "pw2_ready", "stats_ready", "scales_ready"))
    rden_ready, rb_psum, at_ready, proj_psum, x1_ready = (sem(n) for n in ("rden_ready", "rb_psum", "at_ready", "proj_psum", "x1_ready"))
    ve_ready, pw_ready = sem("ve_ready"), sem("pw_ready")
    t2_psum, xt2_ready, lg_psum, lg_ready, ex_ready = (sem(n) for n in ("t2_psum", "xt2_ready", "lg_psum", "lg_ready", "ex_ready"))
    mx_ready, hot_ready, cnt_psum, gate_ready = sem("mx_ready"), sem("hot_ready"), sem("cnt_psum"), sem("gate_ready")
    xg_ready, g_psum, xgt_ready, hott_ready = (sem(n) for n in ("xg_ready", "g_psum", "xgt_ready", "hott_ready"))
    ht_psum = sem("ht_psum")
    z_psum, hid_ready, y_psum, x2_ready = (sem(n) for n in ("z_psum", "hid_ready", "y_psum", "x2_ready"))
    fold_psum, fold_ready = sem("fold_psum"), sem("fold_ready")
    xe_ready, t3_psum, xt3_ready, u_psum, ut_ready = (sem(n) for n in ("xe_ready", "t3_psum", "xt3_ready", "u_psum", "ut_ready"))
    s_psum, th_ready, ee_ready, em_ready, mix_psum, x3_ready = (sem(n) for n in ("s_psum", "th_ready", "ee_ready", "em_ready", "mix_psum", "x3_ready"))
    xn4_ready, t4_psum, xt4_ready, f_psum, res_ready = (sem(n) for n in ("xn4_ready", "t4_psum", "xt4_ready", "f_psum", "res_ready"))

    psRb, psProj, psT2, psLg = [half[0], half[1]], [banks[0], banks[1]], [half[2], banks[2]], half[3]
    psFold = banks[3]
    psZ = [banks[0], banks[1]]
    psY = banks[2]
    psG = banks[3]
    psT3, psU, psS = half[0], half[1], half[0]
    psMix = [half[2], half[3]]
    psOut = half[3]

    BY_DVE = [j for j in range(CHUNKS) if j % 4 >= 2]
    BY_ACT = [j for j in range(CHUNKS) if j % 4 < 2]
    xn2_by_dve, xn2_by_act = sem("xn2_by_dve"), sem("xn2_by_act")

    SLOTS = {"t3": 4, "u": 5, "s": 6, "mask": 10, "mix": 11, "t4": 14, "f": 15}

    def slots():
        for n in range((CHUNKS + 1) * E + max(SLOTS.values())):
            due = [(name, (n - E - at) // E) for name, at in SLOTS.items()
                   if n >= E + at and (n - E - at) % E == 0 and (n - E - at) // E < CHUNKS]
            yield (n // E, n % E) if n < CHUNKS * E else None, due

    block = ctx.enter_context(nc.Block())

    @block.sync
    def _(sp):
        for j in range(CHUNKS):
            sp.wait_ge(res_ready, j + 1)
            for s in range(B):
                dst = out[s].rearrange("(u t) d -> t u d", t=32)[:, CH * j:CH * j + CH, :]
                sp.dma_start(dst, res[32 * s:32 * s + 32, j % 2, :, :]).then_inc(res_out[j % 2], 16)
        for i in range(2):
            sp.wait_ge(res_out[i], 16 * B * CHUNKS // 2)

    @block.gpsimd
    def _(pool):
        for h in range(2):
            pool.wait_ge(ve2_ready, h + 1)
            nc.gpsimd.tensor_tensor(rs2[:, HT * h:HT * h + HT], ve2[:, HT * h:HT * h + HT], half_pow[:, :],
                                    ALU.pow).then_inc(pw2_ready, 1)
        for k in range(2 * CHUNKS):
            pool.wait_ge(ve_ready, k + 1)
            nc.gpsimd.tensor_tensor(rs[:, :], ve[:, :], half_pow[:, 0:CH], ALU.pow).then_inc(pw_ready, 1)

    @block.vector
    def _(dve):
        chain = [0]
        norms = [0]

        def link(ins):
            chain[0] += 1
            ins.then_inc(v_chain, 1)
            dve.wait_ge(v_chain, chain[0])

        def norm(src, dst):
            for i in range(CH):
                last = nc.vector.bn_stats(stats[:, i, :], src(i))
            link(last)
            for i in range(CH):
                last = nc.vector.bn_aggr(mv[:, i, :], stats[:, i, :])
            link(last)
            nc.vector.tensor_scalar_add(ve[:, :], mv[:, :, 1], EPS).then_inc(ve_ready, 1)
            norms[0] += 1
            dve.wait_ge(pw_ready, norms[0])
            link(nc.vector.tensor_tensor(nt[:, 0, :], ve[:, :], rs[:, :], ALU.mult))
            link(nc.vector.tensor_tensor(nt[:, 1, :], nt[:, 0, :], rs[:, :], ALU.mult))
            link(nc.vector.tensor_scalar(nt[:, 2, :], nt[:, 1, :], -0.5, 1.5, ALU.mult, ALU.add))
            link(nc.vector.tensor_tensor(nt[:, 0, :], rs[:, :], nt[:, 2, :], ALU.mult))
            for i in range(CH):
                last = nc.vector.tensor_scalar(dst(i), src(i), mv[:, i, 0:1], nt[:, 0, i:i + 1], ALU.subtract, ALU.mult)
            return last

        dve.wait_ge(o_in, 16 * 2 * B)
        nc.vector.reciprocal(den[:, :, :], den[:, :, :]).then_inc(rden_ready, 1)

        def divide(j):
            dve.wait_ge(rb_psum, j + 1)
            if j >= 2:
                dve.wait_ge(proj_psum, j - 1)
            nc.vector.tensor_tensor(at[:, j % 2, :, :].rearrange("p i (s t) -> p s i t", s=B),
                                    ot[:, :, P * j:P * j + P].rearrange("p s (i t) -> p s i t", t=32),
                                    psRb[j % 2].rearrange("p (s i t) -> p s i t", s=B, i=CH), ALU.mult).then_inc(at_ready, 1)

        def add(j):
            dve.wait_ge(proj_psum, j + 1)
            if j == 0:
                dve.wait_ge(xb_ready, CHUNKS)
            rows = x_res[:, CH * j:CH * j + CH, :]
            nc.vector.tensor_tensor(rows, rows, psProj[j % 2].rearrange("p (i d) -> p i d", i=CH), ALU.add).then_inc(x1_ready, 1)
            dve.wait_ge(x1_ready, j + 1)
            for i in range(CH):
                last = nc.vector.bn_stats(stats2[:, CH * j + i, :], x_res[:, CH * j + i, :])
            last.then_inc(stats_ready, 1)

        def variance(h):
            dve.wait_ge(stats_ready, CHUNKS // 2 * (h + 1))
            for u in range(HT * h, HT * h + HT):
                last = nc.vector.bn_aggr(mv2[:, u, :], stats2[:, u, :])
            link(last)
            nc.vector.tensor_scalar_add(ve2[:, HT * h:HT * h + HT], mv2[:, HT * h:HT * h + HT, 1], EPS).then_inc(ve2_ready, 1)

        def scales(h):
            c = slice(HT * h, HT * h + HT)
            dve.wait_ge(pw2_ready, h + 1)
            link(nc.vector.tensor_tensor(nt2[:, 0, c], ve2[:, c], rs2[:, c], ALU.mult))
            link(nc.vector.tensor_tensor(nt2[:, 1, c], nt2[:, 0, c], rs2[:, c], ALU.mult))
            link(nc.vector.tensor_scalar(nt2[:, 2, c], nt2[:, 1, c], -0.5, 1.5, ALU.mult, ALU.add))
            link(nc.vector.tensor_tensor(rs2[:, c], rs2[:, c], nt2[:, 2, c], ALU.mult))
            nc.vector.scalar_tensor_tensor(nt2[:, 3, c], mv2[:, c, 0], -1.0, rs2[:, c],
                                           ALU.mult, ALU.mult).then_inc(scales_ready, 1)

        def apply(j):
            dve.wait_ge(scales_ready, j // (CHUNKS // 2) + 1)
            for u in range(CH * j, CH * j + CH):
                last = nc.vector.tensor_scalar(xn2[:, u, :], x_res[:, u, :], rs2[:, u:u + 1], nt2[:, 3, u:u + 1],
                                               ALU.mult, ALU.add)
            last.then_inc(xn2_by_dve, 1)

        divide(0)
        for j in range(CHUNKS):
            if j + 1 < CHUNKS:
                divide(j + 1)
            add(j)
            if j == CHUNKS // 2 - 1:
                variance(0)
            if j == CHUNKS // 2:
                scales(0)
        variance(1)
        for j in BY_DVE[:len(BY_DVE) // 2]:
            apply(j)
        scales(1)
        for j in BY_DVE[len(BY_DVE) // 2:]:
            apply(j)

        dve.wait_ge(lg_psum, CHUNKS)
        dve.wait_ge(wts_in, 16 * n_later)
        bc = lambda a: a.unsqueeze(2).to_broadcast([P, TILES, E])
        link(nc.vector.tensor_tensor(lg[:, :, :], psLg.rearrange("p (u e) -> p u e", e=E)[:, 0:TILES, :],
                                     brb[:, :].unsqueeze(1).to_broadcast([P, TILES, E]), ALU.add))
        link(nc.vector.tensor_reduce(col[:, 0, :], lg[:, :, :], AX.X, ALU.max))
        nc.vector.tensor_tensor(lg[:, :, :], lg[:, :, :], bc(col[:, 0, :]), ALU.subtract).then_inc(mx_ready, 1)
        dve.wait_ge(mx_ready, 1)
        link(nc.vector.tensor_scalar(hot[:, :, :], lg[:, :, :], 0.0, None, ALU.is_equal))
        link(nc.vector.tensor_tensor(hot[:, :, :], hot[:, :, :], rank[:, :].unsqueeze(1).to_broadcast([P, TILES, E]), ALU.mult))
        link(nc.vector.tensor_reduce(col[:, 1, :], hot[:, :, :], AX.X, ALU.max))
        link(nc.vector.tensor_tensor(hot[:, :, :], hot[:, :, :], bc(col[:, 1, :]), ALU.is_equal))
        nc.vector.tensor_copy(hotb[:, :, :], hot[:, :, :]).then_inc(hot_ready, 1)
        dve.wait_ge(ex_ready, 1)
        link(nc.vector.tensor_reduce(col[:, 2, :], ex[:, :, :], AX.X, ALU.add))
        link(nc.vector.reciprocal(col[:, 3, :], col[:, 2, :]))
        dve.wait_ge(cnt_psum, 1)
        cview = psZ[0].rearrange("p (k u e) -> p k u e", k=2, e=E)
        link(nc.vector.tensor_copy(cnt[:, 0, :, :], cview[:, 1]))
        link(nc.vector.tensor_tensor(pos[:, :, :], cview[:, 0], cnt[:, 0, :, :], ALU.subtract))
        cur, step = 0, 1
        while step < TILES:
            nc.vector.tensor_copy(cnt[:, 1 - cur, 0:step, :], cnt[:, cur, 0:step, :])
            link(nc.vector.tensor_tensor(cnt[:, 1 - cur, step:, :], cnt[:, cur, step:, :], cnt[:, cur, 0:TILES - step, :], ALU.add))
            cur, step = 1 - cur, 2 * step
        link(nc.vector.tensor_tensor(pos[:, :, :], pos[:, :, :], cnt[:, cur, :, :], ALU.add))
        link(nc.vector.tensor_reduce(tot[:, :], psY.rearrange("p (k u e) -> p k e u", k=2, e=E)[:, 0], AX.X, ALU.add))
        link(nc.vector.tensor_tensor(pos[:, :, :], pos[:, :, :], tot[:, :].unsqueeze(1).to_broadcast([P, TILES, E]), ALU.add))
        link(nc.vector.tensor_scalar(pos[:, :, :], pos[:, :, :], float(CAP), None, ALU.is_lt))
        link(nc.vector.tensor_tensor(pos[:, :, :], pos[:, :, :], hot[:, :, :], ALU.mult))
        link(nc.vector.tensor_reduce(col[:, 0, :], pos[:, :, :], AX.X, ALU.max))
        nc.vector.tensor_tensor(gate[:, :], col[:, 0, :], col[:, 3, :], ALU.mult).then_inc(gate_ready, 1)
        dve.wait_ge(gate_ready, 1)
        dve.wait_ge(fold_psum, 1)
        nc.vector.tensor_copy(aqk[:, :], psFold[:, 0:P])
        nc.vector.tensor_tensor(wft[:, :], psFold[:, P:2 * P], dis[:, :], ALU.add).then_inc(fold_ready, 1)

        def gated(j):
            if j >= 2:
                dve.wait_ge(g_psum, j - 1)
            for i in range(CH):
                last = nc.vector.tensor_scalar(xg[:, j % 2, i, :], xn2[:, CH * j + i, :], gate[:, CH * j + i:CH * j + i + 1],
                                               None, ALU.mult)
            last.then_inc(xg_ready, 1)

        def moe_out(j):
            dve.wait_ge(y_psum, j + 1)
            for i in range(CH):
                u = CH * j + i
                last = nc.vector.scalar_tensor_tensor(x_res[:, u, :], psY[:, P * i:P * i + P], gate[:, u:u + 1],
                                                      x_res[:, u, :], ALU.mult, ALU.add)
            last.then_inc(x2_ready, 1)
            dve.wait_ge(x2_ready, j + 1)
            last = norm(lambda i: x_res[:, CH * j + i, :], lambda i: xe[:, j % 2, i, 0:D])
            last.then_inc(xe_ready, 1)

        nc.vector.memset(xe[:, :, :, D:D + 1], 1.0)
        gated(0)
        gated(1)
        for expert, due in slots():
            for name, j in due:
                if name == "mask":
                    dve.wait_ge(ee_ready, j + 1)
                    nc.vector.tensor_tensor(ee[:, :, :], ee[:, :, :], samet[:, :].unsqueeze(1).to_broadcast([P, CH, P]),
                                            ALU.mult).then_inc(em_ready, 1)
                if name == "mix":
                    dve.wait_ge(mix_psum, j + 1)
                    for k in range(2):
                        v = psMix[k].rearrange("p (i c) -> p i c", i=2)
                        last = nc.vector.reciprocal(inv[:, 2 * k:2 * k + 2], v[:, :, D])
                    link(last)
                    for i in range(CH):
                        u = CH * j + i
                        c0 = (i % 2) * (CW // 2)
                        last = nc.vector.scalar_tensor_tensor(x_res[:, u, :], psMix[i // 2][:, c0:c0 + D], inv[:, i:i + 1],
                                                              x_res[:, u, :], ALU.mult, ALU.add)
                    last.then_inc(x3_ready, 1)
                    dve.wait_ge(x3_ready, j + 1)
                    if j >= 1:
                        dve.wait_ge(t4_psum, j)
                    norm(lambda i: x_res[:, CH * j + i, :], lambda i: xn4[:, i, :]).then_inc(xn4_ready, 1)
                if name == "f":
                    dve.wait_ge(f_psum, j + 1)
                    if j >= 2:
                        dve.wait_ge(res_out[j % 2], 16 * B * (j // 2))
                    nc.vector.tensor_tensor(res[:, j % 2, :, :], x_res[:, CH * j:CH * j + CH, :],
                                            psOut.rearrange("p (i d) -> p i d", i=CH), ALU.add).then_inc(res_ready, 1)
            if expert and expert[1] == E - 1:
                j = expert[0]
                moe_out(j)
                if j + 2 < CHUNKS:
                    gated(j + 2)

    @block.tensor
    def _(pe):
        pe.wait_ge(wts_in, 16 * n_later)

        def reciprocals(j):
            if j >= 2:
                pe.wait_ge(at_ready, j - 1)
            nc.tensor.matmul(psRb[j % 2], sel[:, j, :], den[:, :, :].rearrange("p s q -> p (s q)"),
                             start=True, stop=True).then_inc(rb_psum, 1)

        def project(j):
            pe.wait_ge(at_ready, j + 1)
            if j >= 2:
                pe.wait_ge(x1_ready, j - 1)
            for i in range(CH):
                last = nc.tensor.matmul(psProj[j % 2][:, P * i:P * i + P], at[:, j % 2, i, :], wo[:, :], start=True, stop=True)
            last.then_inc(proj_psum, 1)

        def turned(j):
            if j in BY_DVE:
                pe.wait_ge(xn2_by_dve, BY_DVE.index(j) + 1)
            else:
                pe.wait_ge(xn2_by_act, BY_ACT.index(j) + 1)
            if j >= 2:
                pe.wait_ge(xt2_ready, j - 1)
            for i in range(CH):
                last = nc.tensor.transpose(psT2[j % 2][:, P * i:P * i + P], xn2[:, CH * j + i, :], ident[:, :])
            last.then_inc(t2_psum, 1)

        def logits(j):
            pe.wait_ge(xt2_ready, j + 1)
            for i in range(CH):
                u = CH * j + i
                last = nc.tensor.matmul(psLg[:, E * u:E * u + E], xt2[:, j % 2, P * i:P * i + P], wr[:, :], start=True, stop=True)
            last.then_inc(lg_psum, 1)

        nc.tensor.matmul(psFold[:, 0:P], w1q[:, :], w1k[:, :], start=True, stop=True)
        nc.tensor.transpose(psFold[:, P:2 * P], wf[:, :], ident[:, :]).then_inc(fold_psum, 1)

        pe.wait_ge(rden_ready, 1)
        reciprocals(0)
        for j in range(CHUNKS):
            if j + 1 < CHUNKS:
                reciprocals(j + 1)
            project(j)
        turned(0)
        for j in range(CHUNKS):
            if j + 1 < CHUNKS:
                turned(j + 1)
            logits(j)

        pe.wait_ge(hot_ready, 1)
        flat = hotb[:, :, :].rearrange("p u e -> p (u e)")
        nc.tensor.matmul(psZ[0][:, 0:TILES * E], incl[:, :], flat, start=True, stop=True)
        nc.tensor.matmul(psZ[0][:, TILES * E:2 * TILES * E], same[:, :], flat, start=True, stop=True)
        nc.tensor.matmul(psY[:, 0:TILES * E], less[:, :], flat, start=True, stop=True).then_inc(cnt_psum, 1)

        def gated_columns(j):
            pe.wait_ge(xg_ready, j + 1)
            pe.wait_ge(fold_ready, 1)
            if j >= 1:
                pe.wait_ge(hott_ready, 2 * j)
            for i in range(CH):
                last = nc.tensor.transpose(psG[:, P * i:P * i + P], xg[:, j % 2, i, :], ident[:, :])
            last.then_inc(g_psum, 1)
            pe.wait_ge(xgt_ready, j + 1)
            for i in range(CH):
                last = nc.tensor.matmul(psG[0:E, P * i:P * i + P], hot[:, CH * j + i, :], ident[:, :], start=True, stop=True)
            last.then_inc(ht_psum, 1)

        def expert_in(n):
            j, e = n // E, n % E
            if n >= 2:
                pe.wait_ge(hid_ready, n - 1)
            pe.wait_ge(xgt_ready, j + 1)
            pe.wait_ge(hott_ready, 2 * j + 2)
            nc.tensor.matmul(psZ[n % 2], w1[:, e, :], xgt[:, j % 2, :], start=True, stop=False)
            nc.tensor.matmul(psZ[n % 2], big[:, e, :], noth[:, j % 2, :], start=False, stop=True).then_inc(z_psum, 1)

        def expert_out(n):
            j, e = n // E, n % E
            if e == 0 and j >= 1:
                pe.wait_ge(x2_ready, j)
            pe.wait_ge(hid_ready, n + 1)
            for i in range(CH):
                nc.tensor.matmul(psY[:, P * i:P * i + P], hid[:, n % 3, P * i:P * i + P], w2[:, e, :],
                                 start=(e == 0 and i == 0), stop=False, skip_group_check=True)
            if e == E - 1:
                for i in range(CH):
                    last = nc.tensor.matmul(psY[:, P * i:P * i + P], hott[:, j % 2, P * i:P * i + P], b2r[:, :],
                                            start=False, stop=(i == CH - 1), skip_group_check=True)
                last.then_inc(y_psum, 1)

        pe.wait_ge(gate_ready, 1)
        gated_columns(0)
        expert_in(0)
        for n, (expert, due) in enumerate(slots()):
            for name, j in due:
                if name == "t3":
                    pe.wait_ge(xe_ready, j + 1)
                    if j >= 1:
                        pe.wait_ge(th_ready, j)
                    for i in range(CH):
                        last = nc.tensor.transpose(psT3[:, P * i:P * i + P], xe[:, j % 2, i, 0:D], ident[:, :])
                    last.then_inc(t3_psum, 1)
                if name == "u":
                    pe.wait_ge(xt3_ready, j + 1)
                    nc.tensor.matmul(psU, aqk[:, :], xt3[:, :], start=True, stop=True).then_inc(u_psum, 1)
                if name == "s":
                    pe.wait_ge(ut_ready, j + 1)
                    for i in range(CH):
                        last = nc.tensor.matmul(psS[:, P * i:P * i + P], xt3[:, P * i:P * i + P], ut[:, P * i:P * i + P],
                                                start=True, stop=True)
                    last.then_inc(s_psum, 1)
                if name == "mix":
                    pe.wait_ge(em_ready, j + 1)
                    if j >= 1:
                        pe.wait_ge(xt4_ready, j)
                        pe.wait_ge(res_ready, j)
                    for i in range(CH):
                        c0 = (i % 2) * (CW // 2)
                        last = nc.tensor.matmul(psMix[i // 2][:, c0:c0 + D + 1], ee[:, i, :], xe[:, j % 2, i, 0:D + 1],
                                                start=True, stop=True)
                    last.then_inc(mix_psum, 1)
                if name == "t4":
                    pe.wait_ge(xn4_ready, j + 1)
                    for i in range(CH):
                        last = nc.tensor.transpose(psMix[0][:, P * i:P * i + P], xn4[:, i, :], ident[:, :])
                    last.then_inc(t4_psum, 1)
                if name == "f":
                    pe.wait_ge(xt4_ready, j + 1)
                    for i in range(CH):
                        last = nc.tensor.matmul(psOut[:, P * i:P * i + P], xt4[:, P * i:P * i + P], wft[:, :], start=True, stop=True)
                    last.then_inc(f_psum, 1)
            if expert:
                j, e = expert
                if e == 4 and j + 1 < CHUNKS:
                    gated_columns(j + 1)
                if n + 1 < CHUNKS * E:
                    expert_in(n + 1)
                expert_out(n)

    @block.scalar
    def _(act):
        def columns(j):
            act.wait_ge(t2_psum, j + 1)
            if j >= 2:
                act.wait_ge(lg_psum, j - 1)
            nc.scalar.copy(xt2[:, j % 2, :], psT2[j % 2]).then_inc(xt2_ready, 1)

        def apply(j):
            act.wait_ge(scales_ready, j // (CHUNKS // 2) + 1)
            for u in range(CH * j, CH * j + CH):
                last = nc.scalar.activation(xn2[:, u, :], x_res[:, u, :], ACT.Identity, bias=nt2[:, 3, u:u + 1],
                                            scale=rs2[:, u:u + 1])
            last.then_inc(xn2_by_act, 1)

        for j in BY_ACT[:len(BY_ACT) // 2]:
            apply(j)
        for j in range(CHUNKS // 2):
            columns(j)
        for j in BY_ACT[len(BY_ACT) // 2:]:
            apply(j)
        for j in range(CHUNKS // 2, CHUNKS):
            columns(j)
        act.wait_ge(mx_ready, 1)
        nc.scalar.activation(ex[:, :, :], lg[:, :, :], ACT.Exp).then_inc(ex_ready, 1)
        act.wait_ge(wts_in, 16 * n_later)

        def gated_columns(j):
            act.wait_ge(g_psum, j + 1)
            if j >= 2:
                act.wait_ge(z_psum, E * (j - 1))
                act.wait_ge(y_psum, j - 1)
            nc.scalar.copy(xgt[:, j % 2, :], psG).then_inc(xgt_ready, 1)
            act.wait_ge(ht_psum, j + 1)
            nc.scalar.copy(hott[:, j % 2, :], psG[0:E, :]).then_inc(hott_ready, 1)
            nc.scalar.activation(noth[:, j % 2, :], psG[0:E, :], ACT.Copy, bias=1.0, scale=-1.0).then_inc(hott_ready, 1)

        def hidden(n):
            act.wait_ge(z_psum, n + 1)
            if n >= 3:
                j, e = (n - 2) // E, (n - 2) % E
                act.wait_ge(hid_ready, n - 2)
            e = n % E
            nc.scalar.activation(hid[:, n % 3, :], psZ[n % 2], ACT.Relu, bias=b1c[:, e:e + 1]).then_inc(hid_ready, 1)

        gated_columns(0)
        hidden(0)
        for n, (expert, due) in enumerate(slots()):
            for name, j in due:
                if name == "t3":
                    act.wait_ge(t3_psum, j + 1)
                    if j >= 1:
                        act.wait_ge(s_psum, j)
                    nc.scalar.copy(xt3[:, :], psT3).then_inc(xt3_ready, 1)
                if name == "u":
                    act.wait_ge(u_psum, j + 1)
                    nc.scalar.copy(ut[:, :], psU).then_inc(ut_ready, 1)
                if name == "s":
                    act.wait_ge(s_psum, j + 1)
                    nc.scalar.activation(th[:, :, :].rearrange("p i t -> p (i t)"), psS, ACT.Tanh,
                                         scale=1.0 / float(np.sqrt(np.float32(D)))).then_inc(th_ready, 1)
                    act.wait_ge(th_ready, j + 1)
                    if j >= 1:
                        act.wait_ge(mix_psum, j)
                    nc.scalar.activation(ee[:, :, :], th[:, :, :], ACT.Exp).then_inc(ee_ready, 1)
                if name == "t4":
                    act.wait_ge(t4_psum, j + 1)
                    if j >= 1:
                        act.wait_ge(f_psum, j)
                    nc.scalar.copy(xt4[:, :], psMix[0]).then_inc(xt4_ready, 1)
            if expert:
                j, e = expert
                if e == 4 and j + 1 < CHUNKS:
                    gated_columns(j + 1)
                if n + 1 < CHUNKS * E:
                    hidden(n + 1)


_INS = ["L0_attn_x", "L0_attn_Wq", "L0_attn_bq", "L0_attn_Wk", "L0_attn_bk", "L0_attn_Wv", "L0_attn_bv", "L0_attn_Wo",
        "L0_attn_bo", "L0_ffn_Wr", "L0_ffn_br", "L0_ffn_W1", "L0_ffn_b1", "L0_ffn_W2", "L0_ffn_b2", "L1_attn_Wq",
        "L1_attn_Wk", "L1_ffn_weight", "L1_ffn_disha"]


def kernel(**inputs):
    import concourse.bacc as _bacc
    from concourse.bass_utils import run_bass_kernel_spmd as _run

    nc = _bacc.Bacc("TRN2", target_bir_lowering=False, num_devices=1)
    arrays, args, consts = {}, [], {}
    for name in _INS:
        a = np.ascontiguousarray(inputs[name])
        arrays[f"in_{name}"] = a
        args.append(nc.dram_tensor(f"in_{name}", a.shape, mybir.dt.from_np(a.dtype), kind="ExternalInput").ap())
    for name, a in constants().items():
        arrays[name] = a
        consts[name] = nc.dram_tensor(name, a.shape, mybir.dt.from_np(a.dtype), kind="ExternalInput").ap()
    result = nc.dram_tensor("out_0", (B, S, D), F32, kind="ExternalOutput").ap()
    build(nc, *args, consts, result)
    return _run(nc, [arrays], core_ids=[0]).results[0]["out_0"]
```

```python
from contextlib import ExitStack

import numpy as np
import concourse.bass as bass
from concourse import mybir

F32 = mybir.dt.float32
BF16 = mybir.dt.bfloat16
ALU = mybir.AluOpType
ACT = mybir.ActivationFunctionType
AX = mybir.AxisListType

P = 128
B, S, D = 4, 1024, 128
H, HD = 16, 8
E, CAP = 8, B * S // 8
TILES = B * S // P
CH = 4
CW = CH * P
CHUNKS = TILES // CH
EPS = 1e-5
GH = 4
NG = B * H // GH
KB = S // P
QC = S // CW

MAXROWS, BIASROWS = 3, 6
RUNS = ((0, 3), (3, 2), (5, 1))
NPROD = 6
CROWS = MAXROWS + BIASROWS
ROWS = CROWS + NPROD * HD
FILL = -3.0e38
BIG = -1.0e30


def bf16_bits(a):
    return (np.ascontiguousarray(a, np.float32).view(np.uint32) >> 16).astype(np.uint16)


def top(a):
    return (np.ascontiguousarray(a, np.float32).view(np.uint32) & np.uint32(0xFFFF0000)).view(np.float32)


def constants():
    pos = np.arange(S)
    slopes = np.power(np.float32(2.0 ** (-8.0 / H)), np.arange(1, H + 1, dtype=np.float32)).astype(np.float32)
    s0 = top(slopes)
    s1 = top(slopes - s0)
    s2 = top(slopes - s0 - s1)
    krows = np.zeros((CROWS, S), np.float32)
    krows[:MAXROWS] = 1.0
    qrows = np.zeros((H, CROWS, S), np.float32)
    for part, s in enumerate((s0, s1, s2)):
        krows[MAXROWS + 2 * part] = pos // P * P
        krows[MAXROWS + 2 * part + 1] = pos % P
        qrows[:, MAXROWS + 2 * part] = s[:, None]
        qrows[:, MAXROWS + 2 * part + 1] = s[:, None]
    q, k = np.arange(P)[:, None], np.arange(P)[None, :]
    cmask = np.zeros((P, S), np.float32)
    cmask[:, S - P:] = np.where(k <= q, 0.0, FILL)
    seq, at = np.arange(P) // 32, np.arange(P) % 32
    same = seq[:, None] == seq[None, :]
    sel = np.zeros((H, CHUNKS, CHUNKS, P), np.float32)
    for j in range(CHUNKS):
        sel[np.arange(P) % H, j, j, np.arange(P)] = 1.0
    big = np.zeros((E, E, P), np.float32)
    big[np.arange(E), np.arange(E)] = BIG
    return {
        "c_qrows": bf16_bits(np.tile(qrows.reshape(H // GH, GH, CROWS, S), (B, 1, 1, 1))),
        "c_krows": bf16_bits(krows),
        "c_cmask": bf16_bits(cmask),
        "c_identb": bf16_bits(np.eye(P)),
        "c_guard": bf16_bits(np.where(q > k, FILL, 0.0)),
        "c_ident": np.eye(P, dtype=np.float32),
        "c_sel": sel.reshape(P, CHUNKS * P),
        "c_incl": bf16_bits(same & (at[:, None] <= at[None, :])),
        "c_same": bf16_bits(same),
        "c_less": bf16_bits(seq[:, None] < seq[None, :]),
        "c_big": bf16_bits(big.reshape(E, E * P)),
        "c_samet": (at[:, None] == at[None, :]).astype(np.float32),
        "c_rank": np.tile((E - np.arange(E)).astype(np.float32), (P, 1)),
    }


W_SCORES, W_SUMS = 1.5, 2.0


def attention_units():
    out = []
    for slot, c in enumerate(range(QC - 1, -1, -1)):
        last = CH * (c + 1)
        mixed = [kb for pair in zip(range(last // 2), range(last - 1, last // 2 - 1, -1)) for kb in pair]
        for kb in mixed:
            d = kb - CH * c
            q0 = P * max(d, 0)
            out.append((slot, c, kb, q0, CW - q0, d >= 0))
    return out


def steep(par, i):
    return any(2.0 ** (-8.0 / H * (GH * g + i + 1)) * (P - 1) > 40 for g in range(par, H // GH, 2))


UNITS = attention_units()
NU = len(UNITS)
MAXUNITS = [(slot, t, tuple(range(i, i + (1 if t >= CH else 2))))
            for slot, c in enumerate(range(QC - 1, -1, -1))
            for t in range(CH * c, CH * c + CH) for i in range(0, GH, 1 if t >= CH else 2)]
NM = len(MAXUNITS)
NM_SLOT = [sum(1 for m in MAXUNITS if m[0] <= slot) for slot in range(QC)]
EXPS = [(u, i, min(GH, CW // UNITS[u][4])) for u in range(NU)
        for i in range(0, GH, min(GH, CW // UNITS[u][4]))]
NE = len(EXPS)
EXPS_TO = [sum(1 for e in EXPS if e[0] <= u) for u in range(NU)]
RING = 3
FIRST = [min(u for u in range(NU) if UNITS[u][0] == s) for s in range(QC)]
LAST = [max(u for u in range(NU) if UNITS[u][0] == s) for s in range(QC)]
DIAG = [u for u in range(NU) if UNITS[u][5]]


def step_order(with_b, with_a):
    b, a = [], []
    if with_b:
        for u in range(NU + 2):
            items = [k for k in range(NE) if EXPS[k][0] == u]
            b += [(("S", k), W_SCORES * EXPS[k][2] * UNITS[u][4]) for k in items[:3]]
            if u > 1:
                b.append((("V", u - 2), W_SUMS * UNITS[u - 2][4]))
                if u - 2 in LAST:
                    b.append((("O", LAST.index(u - 2)), 0))
            b += [(("S", k), W_SCORES * EXPS[k][2] * UNITS[u][4]) for k in items[3:]]
            if u == 3:
                b.append((("L", QC - 1), 100))
    if with_a:
        for k, (slot, t, heads) in enumerate(MAXUNITS):
            a.append((("A", k), len(heads) * P * (t + 1)))
            if k + 1 == NM_SLOT[0]:
                a.append((("F", 0), 0))
            if k == NM_SLOT[0] + 1:
                a.append((("T", 0), 100))
        a.append((("F", 1), 0))
    out, done_a, done_b = [], 0.0, 0.0
    tot_a = sum(w for _, w in a) or 1
    tot_b = sum(w for _, w in b) or 1
    while a or b:
        if b and (not a or done_b / tot_b <= done_a / tot_a):
            item, w = b.pop(0)
            done_b += w
        else:
            item, w = a.pop(0)
            done_a += w
        out.append(item)
    return out


def banks_of(order, before):
    def uses(items):
        return [it for it in items if it[0] in "STL"]
    out = {}
    old, new = uses(before), uses(order)
    for j, item in enumerate(new):
        if j >= RING:
            out[item] = (j % RING, new[j - RING], False)
        else:
            last = [it for k, it in enumerate(old) if k % RING == j]
            out[item] = (j, last[-1] if last else None, True)
    return out


def build(nc, x, Wq, bq, Wk, bk, Wv, bv, Wo, bo, Wr, br, W1, b1, W2, b2, W1q, W1k, Wf, disha, consts, out):
    ctx = ExitStack()
    with ctx:
        def sb(name, shape, dt=F32):
            return ctx.enter_context(nc.sbuf_tensor(name, shape, dt))

        def sem(name):
            return ctx.enter_context(nc.semaphore(name))

        bank2 = [ctx.enter_context(nc.psum_tensor(f"bank2_{i}", [P, 2 * CW], F32)) for i in range(2)]
        bank = [ctx.enter_context(nc.psum_tensor(f"bank{i}", [P, CW], F32)) for i in range(4)]
        half = [bank2[0][:, 0:CW], bank2[0][:, CW:2 * CW], bank2[1][:, 0:CW], bank2[1][:, CW:2 * CW]]
        b0, b1_, b2_, b3 = (t[:, :] for t in bank)

        qk_dram = nc.dram_tensor("qk_rows", (NG, 2, 3, HD, GH, S), BF16).ap()
        m_dram = nc.dram_tensor("max_rows", (QC, CH * GH * 3, P), BF16).ap()
        o_dram = nc.dram_tensor("weighted_sums", (NG, GH, HD + 1, S), F32).ap()

        ident = sb("ident", [P, P])
        identb = sb("identb", [P, P], BF16)
        cmask = sb("cmask", [P, S], BF16)
        guards = sb("guards", [P, P], BF16)
        half_pow = sb("half_pow", [P, TILES // 2])
        wq, wk, wv = sb("wq", [P, D]), sb("wk", [P, D]), sb("wv", [P, D])
        bqc, bkc = sb("bqc", [P, 1]), sb("bkc", [P, 1])
        bvb = sb("bvb", [P, D])
        v_all = sb("v_all", [P, NG, KB, GH, HD + 1])
        x_res = sb("x_res", [P, TILES, D])

        w = dict(
            wo=sb("wo", [P, D]), bob=sb("bob", [P, D]), wr=sb("wr", [P, E]), brb=sb("brb", [P, E]), rank=sb("rank", [P, E]),
            sel=sb("sel", [P, CHUNKS, P]), incl=sb("incl", [P, P], BF16), same=sb("same", [P, P], BF16),
            less=sb("less", [P, P], BF16), big=sb("big", [E, E, P], BF16), samet=sb("samet", [P, P]),
            w1=sb("w1", [P, E, D]), w2=sb("w2", [P, E, D]), b1c=sb("b1c", [P, E]), b2r=sb("b2r", [E, D]),
            w1q=sb("w1q", [P, D]), w1k=sb("w1k", [P, D]), wf=sb("wf", [P, D]), dis=sb("dis", [P, D]))
        ot = sb("sums_in", [P, B, S])
        den = sb("denominators", [P, B, P])
        wts_in, xb_ready, bob_in = sem("wts_in"), sem("xb_ready"), sem("bob_in")
        o_in = [sem(f"o_in{b}") for b in range(B)]
        rden_ready = sem("rden_ready")

        def load_later_weights(queue):
            loads = [(w["wo"][H * d:H * d + H, :], Wo.rearrange("(h d) n -> d h n", d=HD)[d]) for d in range(HD)]
            loads += [(w["wr"][:, :], Wr), (w["brb"][:, :], br.partition_broadcast(P)), (w["rank"][:, :], consts["c_rank"]),
                      (w["sel"][:, :, :].rearrange("p c m -> p (c m)"), consts["c_sel"]),
                      (w["incl"][:, :], consts["c_incl"].bitcast(BF16)), (w["same"][:, :], consts["c_same"].bitcast(BF16)),
                      (w["less"][:, :], consts["c_less"].bitcast(BF16)),
                      (w["big"][:, :, :].rearrange("k e f -> k (e f)"), consts["c_big"].bitcast(BF16)),
                      (w["samet"][:, :], consts["c_samet"]), (w["b2r"][:, :], b2),
                      (w["w1"][:, :, :], W1.rearrange("e d f -> d e f")), (w["w2"][:, :, :], W2.rearrange("e f d -> f e d")),
                      (w["w1q"][:, :], W1q), (w["w1k"][:, :], W1k), (w["wf"][:, :], Wf)]
            rd = disha.shape[0]
            loads += [(w["dis"][rd * i:rd * i + rd, :], disha) for i in range(D // rd)]
            for dst, src in loads:
                queue.dma_start(dst, src).then_inc(wts_in, 16)
            queue.dma_start(w["b1c"][:, :], b1.rearrange("e f -> f e"), allow_slow_non_contiguous=True).then_inc(wts_in, 16)

        NLATER = HD + 15 + D // disha.shape[0] + 1

        def load_sums(sp, b):
            groups = slice(b * H // GH, (b + 1) * H // GH)
            sp.dma_start(ot[:, b, :], o_dram[groups, :, 0:HD].rearrange("g i r s -> r (g i) s")).then_inc(o_in[b], 16)
            sp.dma_start(den[:, b, :],
                         o_dram[groups, :, HD].rearrange("g i (j q) -> (g i) j q", q=P)).then_inc(o_in[b], 16)

        const_in = sem("const_in")
        w_in = sem("w_in")
        x_in = [sem(f"x_in{b}") for b in range(B)]
        xres_in = sem("xres_in")

        scale = 1.0 / float(np.sqrt(np.float32(HD)))

        att = ExitStack()
        ctx.enter_context(att)

        def asb(name, shape, dt=F32):
            return att.enter_context(nc.sbuf_tensor(name, shape, dt))

        qa, ka = asb("q_for_max", [P, 2, GH, S], BF16), asb("k_for_max", [P, 2, GH, S], BF16)
        qb, kb_ = asb("q_for_exp", [P, 2, GH, S], BF16), asb("k_for_exp", [P, 2, GH, S], BF16)
        pad_zero, krows_in = sem("pad_zero"), sem("krows_in")
        parts_out = [sem(f"parts_out{b}") for b in range(B)]
        DEEP = 3
        a_in = [sem(f"a_in{i}") for i in range(2)]
        b_in = [sem(f"b_in{i}") for i in range(2)]
        a_scores, s_scores, sp_turns = sem("a_scores"), sem("s_scores"), sem("sp_turns")
        const_rows = consts["c_qrows"].bitcast(BF16).rearrange("n i c s -> n c i s")
        mb = MAXROWS
        NA = 1 + 2 * len(RUNS)
        NBIN = 3

        def load_max_operands(sp, n, par, late):
            if late:
                sp.wait_ge(a_scores, (n - 1) * NM)
                sp.sem_inc(sp_turns, 1)
            sp.dma_start(qa[0:CROWS, par, :, :], const_rows[bass.ds(n, 1)].rearrange("n c i s -> (n c) i s")).then_inc(a_in[par], 16)
            for m, (p0, count) in enumerate(RUNS):
                r0, r1 = CROWS + HD * p0, CROWS + HD * (p0 + count)
                sp.dma_start(qa[r0:r1, par, :, :].rearrange("r i s -> r (i s)"),
                             qk_dram[bass.ds(n, 1), 0, 0:count].rearrange("n m d i s -> (n m d) (i s)")).then_inc(a_in[par], 16)
                sp.dma_start(ka[r0:r1, par, :, :].rearrange("r i s -> r (i s)"),
                             qk_dram[bass.ds(n, 1), 1, m].rearrange("n d i s -> n d (i s)")
                             .to_broadcast([count, HD, GH * S])).then_inc(a_in[par], 16)

        def copy_exp_operands(sp, n, half, par, late):
            sp.wait_ge(a_in[par], 16 * NA * (half + 1))
            sp.sem_inc(sp_turns, 1)
            if late:
                sp.wait_ge(s_scores, (n - 1) * NE)
            sp.sem_inc(sp_turns, 1)
            sp.dma_start(qb[mb:ROWS, par, :, :], qa[mb:ROWS, par, :, :]).then_inc(b_in[par], 16)
            sp.dma_start(kb_[0:ROWS, par, :, :], ka[0:ROWS, par, :, :]).then_inc(b_in[par], 16)

        pre = ExitStack()
        with pre:
            def tsb(name, shape, dt=F32):
                return pre.enter_context(nc.sbuf_tensor(name, shape, dt))

            xn = ot[:, :, :].rearrange("p b (u d) -> p (b u) d", d=D)
            stats = tsb("stats0", [P, B, KB, 6])
            mv = tsb("mv0", [P, B, KB, 2])
            ve = tsb("ve0", [P, B, KB])
            rs = tsb("rs0", [P, B, KB])
            nt = tsb("nt0", [P, 2, KB])
            nm = tsb("nm0", [P, B, KB])
            xt = tsb("xt0", [P, 2, CW])
            full = tsb("qk_full", [P, 2, 2, CW])
            rest = tsb("qk_rest", [P, 2, 2, CW])
            parts = tsb("qk_parts", [P, DEEP, 2, 3, S], BF16)
            bsc = tsb("bsc", [P, 2])
            wqk = tsb("wqk", [P, 2, D])

            norm_in, var_ready, pow_ready, xn_ready = sem("norm_chain"), sem("var_ready"), sem("pow_ready"), sem("xn_ready")
            xt_psum, xt_ready, qk_psum, v_psum = sem("xt_psum"), sem("xt_ready"), sem("qk_psum"), sem("v_psum")
            bias_ready, hi_ready, parts_ready = sem("bias_ready"), sem("hi_ready"), sem("parts_ready")
            mid_ready, v_ready, ones_ready = sem("mid_ready"), sem("v_ready"), sem("ones_ready")
            half_ready = sem("half_ready")
            NCONST = 3
            NW = 4
            NB = 1 + 2 * (H // GH)
            bias_in, wqk_ready, xn_by_act, moments_ready = (sem(n) for n in ("bias_in", "wqk_ready", "xn_by_act", "moments_ready"))
            ON_DVE = KB // CH

            psT = [half[0], half[1]]
            psQ = [b0, b1_]
            psK = [b2_, b3]
            psV = [half[2], half[3]]
            block = pre.enter_context(nc.Block())

            @block.sync
            def _(sp):
                for b in range(B):
                    sp.dma_start(xn[:, b * KB:(b + 1) * KB, :],
                                 x[b].rearrange("(u p) d -> p u d", p=P)).then_inc(x_in[b], 16)
                sp.dma_start(cmask[:, :], consts["c_cmask"].bitcast(BF16)).then_inc(const_in, 16)
                sp.dma_start(identb[:, :], consts["c_identb"].bitcast(BF16)).then_inc(const_in, 16)
                sp.dma_start(guards[:, :], consts["c_guard"].bitcast(BF16)).then_inc(const_in, 16)
                sp.wait_ge(pad_zero, 4)
                for par in range(2):
                    for i in range(GH):
                        sp.dma_start(ka[0:CROWS, par, i, :], consts["c_krows"].bitcast(BF16)).then_inc(krows_in, 16)
                for s in range(B):
                    sp.dma_start(x_res[32 * s:32 * s + 32, :, :],
                                 x[s].rearrange("(u t) d -> t u d", t=32)).then_inc(xres_in, 16)
                for b in range(B):
                    sp.wait_ge(parts_ready, 2 * 2 * (b + 1))
                    sp.wait_ge(mid_ready, 2 * 2 * (b + 1))
                    sp.wait_ge(hi_ready, 2 * 2 * (b + 1))
                    for z in range(2):
                        for m in range(3):
                            dst = qk_dram[4 * b:4 * b + 4, z, m]
                            sp.dma_start(dst.rearrange("g d i s -> g (d i) s"),
                                         parts[:, b % DEEP, z, m, :]).then_inc(parts_out[b], 16)
                    if b == 0:
                        sp.wait_ge(krows_in, 16 * 2 * GH)
                        sp.wait_ge(parts_out[0], 16 * 6)
                        load_max_operands(sp, 0, 0, False)

            @block.gpsimd
            def _(pool):
                nc.gpsimd.memset(half_pow[:, :], -0.5).then_inc(half_ready, 1)
                nc.gpsimd.memset(v_all[:, :, :, :, HD:HD + 1], 1.0).then_inc(ones_ready, 1)
                pool.wait_ge(half_ready, 1)

                def power(b):
                    pool.wait_ge(var_ready, b + 1)
                    nc.gpsimd.tensor_tensor(rs[:, b, :], ve[:, b, :], half_pow[:, 0:KB], ALU.pow).then_inc(pow_ready, 1)

                nc.gpsimd.memset(qa[:, :, :, :].bitcast(F32), 0.0).then_inc(pad_zero, 1)
                power(0)
                power(1)
                nc.gpsimd.memset(ka[:, :, :, :].bitcast(F32), 0.0).then_inc(pad_zero, 1)
                nc.gpsimd.memset(kb_[:, :, :, :].bitcast(F32), 0.0).then_inc(pad_zero, 1)
                for k in range(CHUNKS):
                    if k % 2 == 0 and k // 2 + 2 < B:
                        power(k // 2 + 2)
                    for z in range(2):
                        pool.wait_ge(mid_ready, 2 * k + z + 1)
                        to = slice(CW * (k % 2), CW * (k % 2) + CW)
                        nc.gpsimd.tensor_tensor(parts[:, k // 2 % DEEP, z, 2, to], rest[:, k % 2, z, :],
                                                parts[:, k // 2 % DEEP, z, 1, to], ALU.subtract).then_inc(parts_ready, 1)

            @block.vector
            def _(dve):
                chain = [0]

                def link(ins):
                    chain[0] += 1
                    ins.then_inc(norm_in, 1)
                    dve.wait_ge(norm_in, chain[0])

                def moments(b):
                    dve.wait_ge(x_in[b], 16)
                    for i in range(KB):
                        last = nc.vector.bn_stats(stats[:, b, i, :], xn[:, KB * b + i, :])
                    link(last)
                    for i in range(KB):
                        last = nc.vector.bn_aggr(mv[:, b, i, :], stats[:, b, i, :])
                    link(last)
                    nc.vector.tensor_scalar_add(ve[:, b, :], mv[:, b, :, 1], EPS).then_inc(var_ready, 1)

                def scales(b):
                    dve.wait_ge(pow_ready, b + 1)
                    v, r = ve[:, b, :], rs[:, b, :]
                    link(nc.vector.scalar_tensor_tensor(nt[:, 0, :], v, -0.5, r, ALU.mult, ALU.mult))
                    link(nc.vector.tensor_tensor(nt[:, 1, :], nt[:, 0, :], r, ALU.mult))
                    link(nc.vector.scalar_tensor_tensor(r, nt[:, 1, :], 1.5, r, ALU.add, ALU.mult))
                    nc.vector.scalar_tensor_tensor(nm[:, b, :], mv[:, b, :, 0], -1.0, r,
                                                   ALU.mult, ALU.mult).then_inc(moments_ready, 1)

                def norm_rows(k):
                    b = k // 2
                    dve.wait_ge(moments_ready, b + 1)
                    for u in range(CH * k, CH * k + CH):
                        last = nc.vector.tensor_scalar(xn[:, u, :], xn[:, u, :], rs[:, b, u % KB:u % KB + 1],
                                                       nm[:, b, u % KB:u % KB + 1], ALU.mult, ALU.add)
                    last.then_inc(xn_ready, 1)

                def cut(k):
                    for z in range(2):
                        dve.wait_ge(hi_ready, 2 * k + z + 1)
                        if k >= 2:
                            dve.wait_ge(parts_ready, 2 * (k - 2) + z + 1)
                        if k // 2 >= DEEP:
                            dve.wait_ge(parts_out[k // 2 - DEEP], 16 * 6)
                        to = slice(CW * (k % 2), CW * (k % 2) + CW)
                        link(nc.vector.tensor_tensor(rest[:, k % 2, z, :], full[:, k % 2, z, :],
                                                     parts[:, k // 2 % DEEP, z, 0, to], ALU.subtract))
                        nc.vector.tensor_copy(parts[:, k // 2 % DEEP, z, 1, to], rest[:, k % 2, z, :]).then_inc(mid_ready, 1)
                    dve.wait_ge(v_psum, k + 1)
                    dve.wait_ge(ones_ready, 1)
                    for i in range(CH):
                        t = CH * k + i
                        dst = v_all[:, 4 * (t // KB):4 * (t // KB) + 4, t % KB, :, 0:HD]
                        last = nc.vector.tensor_tensor(
                            dst, psV[k % 2][:, P * i:P * i + P].rearrange("p (g i d) -> p g i d", g=4, i=GH),
                            bvb[:, :].rearrange("p (g i d) -> p g i d", g=4, i=GH), ALU.add)
                    last.then_inc(v_ready, 1)

                nc.vector.memset(qb[:, :, :, :].bitcast(F32), 0.0).then_inc(pad_zero, 1)
                moments(0)
                scales(0)
                for k in range(ON_DVE):
                    norm_rows(k)
                moments(1)
                dve.wait_ge(bias_in, 16 * NB)
                scales(1)
                for k in range(CHUNKS):
                    if k % 2 == 0 and k // 2 + 2 < B:
                        moments(k // 2 + 2)
                    cut(k)
                    if k % 2 == 0 and k // 2 + 2 < B:
                        scales(k // 2 + 2)

            @block.tensor
            def _(pe):
                pe.wait_ge(w_in, 16 * NW)

                def turn(k):
                    if k < ON_DVE:
                        pe.wait_ge(xn_ready, k + 1)
                    else:
                        pe.wait_ge(xn_by_act, k - ON_DVE + 1)
                    if k >= 2:
                        pe.wait_ge(xt_ready, k - 1)
                    for i in range(CH):
                        last = nc.tensor.transpose(psT[k % 2][:, P * i:P * i + P], xn[:, CH * k + i, :], ident[:, :])
                    last.then_inc(xt_psum, 1)

                def project(k):
                    pe.wait_ge(xt_ready, k + 1)
                    if k >= 2:
                        pe.wait_ge(hi_ready, 2 * (k - 1))
                        pe.wait_ge(v_ready, k - 1)
                    nc.tensor.matmul(psQ[k % 2], wqk[:, 0, :], xt[:, k % 2, :], start=True, stop=True).then_inc(qk_psum, 1)
                    nc.tensor.matmul(psK[k % 2], wqk[:, 1, :], xt[:, k % 2, :], start=True, stop=True).then_inc(qk_psum, 1)
                    for i in range(CH):
                        last = nc.tensor.matmul(psV[k % 2][:, P * i:P * i + P], xt[:, k % 2, P * i:P * i + P], wv[:, :],
                                                start=True, stop=True)
                    last.then_inc(v_psum, 1)

                turn(0)
                pe.wait_ge(wqk_ready, 2)
                for k in range(CHUNKS):
                    if k + 1 < CHUNKS:
                        turn(k + 1)
                    project(k)

            @block.scalar
            def _(act):
                act.dma_start(ident[:, :], consts["c_ident"]).then_inc(w_in, 16)
                act.dma_start(wq[:, :], Wq).then_inc(w_in, 16)
                act.dma_start(wk[:, :], Wk).then_inc(w_in, 16)
                act.dma_start(wv[:, :], Wv).then_inc(w_in, 16)
                for g in range(H // GH):
                    for dst, src in ((bqc, bq), (bkc, bk)):
                        act.dma_start(dst[32 * g:32 * g + 32, :], src.rearrange("(g i d o) -> g d i o", g=4, i=GH, o=1)[g],
                                      allow_slow_non_contiguous=True).then_inc(bias_in, 16)
                act.dma_start(bvb[:, :], bv.partition_broadcast(P)).then_inc(bias_in, 16)
                act.wait_ge(w_in, 16 * NW)
                for i, w in enumerate((wq, wk)):
                    nc.scalar.copy(wqk[:, i, :].rearrange("p (g d i) -> p g d i", g=4, d=HD),
                                   w[:, :].rearrange("p (g i d) -> p g d i", g=4, i=GH)).then_inc(wqk_ready, 1)
                act.wait_ge(bias_in, 16 * NB)
                nc.scalar.mul(bsc[:, 0:1], bqc[:, :], scale).then_inc(bias_ready, 1)
                nc.scalar.copy(bsc[:, 1:2], bkc[:, :]).then_inc(bias_ready, 1)
                act.wait_ge(bias_ready, 2)

                def take(k):
                    act.wait_ge(xt_psum, k + 1)
                    if k >= 2:
                        act.wait_ge(v_psum, k - 1)
                    nc.scalar.copy(xt[:, k % 2, :], psT[k % 2]).then_inc(xt_ready, 1)

                def norm_rows(k):
                    b = k // 2
                    act.wait_ge(moments_ready, b + 1)
                    for u in range(CH * k, CH * k + CH):
                        last = nc.scalar.activation(xn[:, u, :], xn[:, u, :], ACT.Identity,
                                                    bias=nm[:, b, u % KB:u % KB + 1],
                                                    scale=rs[:, b, u % KB:u % KB + 1])
                    last.then_inc(xn_by_act, 1)

                take(0)
                for k in range(CHUNKS):
                    if ON_DVE <= k + 1 + 1 < CHUNKS or k == 0:
                        for kk in range(ON_DVE, 2 + 1) if k == 0 else (k + 1 + 1,):
                            norm_rows(kk)
                    if k + 1 < CHUNKS:
                        take(k + 1)
                    for z, ps in enumerate((psQ, psK)):
                        act.wait_ge(qk_psum, 2 * k + z + 1)
                        if k >= 2:
                            act.wait_ge(mid_ready, 2 * (k - 2) + z + 1)
                        if k // 2 >= DEEP:
                            act.wait_ge(parts_out[k // 2 - DEEP], 16 * 6)
                        to = slice(CW * (k % 2), CW * (k % 2) + CW)
                        sc = scale if z == 0 else 1.0
                        nc.scalar.activation(full[:, k % 2, z, :], ps[k % 2], ACT.Identity, bias=bsc[:, z:z + 1], scale=sc)
                        nc.scalar.activation(parts[:, k // 2 % DEEP, z, 0, to], ps[k % 2], ACT.Identity,
                                             bias=bsc[:, z:z + 1], scale=sc).then_inc(hi_ready, 1)

        with att:
            junk = asb("junk", [P, 2, S], BF16)
            mx = asb("row_max", [P, 2, KB * GH])
            mrest = asb("max_rest", [P, QC, 2, CH * GH])
            mparts = asb("max_parts", [P, QC, CH, GH, 3], BF16)
            mrows = asb("max_rows_sb", [CH * GH * 3, QC, P], BF16)
            osum = asb("osum", [P, QC, CW])
            vb = asb("v_group", [P, 2, KB, GH, HD + 1])
            probs = asb("probs", [P, 3, GH, CW])

            m_in = [[sem(f"m_in{i}{j}") for j in range(QC)] for i in range(2)]
            m_out = [sem(f"m_out{j}") for j in range(QC)]
            o_out = [sem(f"o_out{j}") for j in range(QC)]
            a_max, cut_chain, mparts_ready = sem("a_max"), sem("cut_chain"), sem("mparts_ready")
            mt_psum, mrows_ready = sem("mt_psum"), sem("mrows_ready")
            o_clear = sem("o_clear")
            exp_ready, masked, pv_done, o_ready = sem("exp_ready"), sem("masked"), sem("pv_done"), sem("o_ready")

            dve_turns, pe_turns, pool_turns = sem("dve_turns"), sem("pe_turns"), sem("pool_turns")

            psA = [bank2[0][:, :], bank2[1][:, :]]
            psS = [b0, b1_, b2_]
            psO = b3
            block = att.enter_context(nc.Block())

            def load_values(sp, n, par, late):
                if late:
                    sp.wait_ge(pv_done, (n - 1) * NU)
                    sp.sem_inc(sp_turns, 1)
                sp.dma_start(vb[:, par, :, :, :].rearrange("p k i c -> p (k i c)"),
                             v_all[:, bass.ds(n, 1)].rearrange("p n k i c -> p (n k i c)")).then_inc(b_in[par], 16)

            @block.sync
            def _(sp):
                for b in range(B):
                    sp.wait_ge(parts_out[b], 16 * 6)
                sp.wait_ge(v_ready, CHUNKS)

                def rows_of_maxima(n, par, slot, late):
                    c = QC - 1 - slot
                    sp.wait_ge(m_out[slot], 16 * n + 16)
                    if late:
                        sp.wait_ge(s_scores, (n - 1) * NE)
                    src = m_dram[slot].rearrange("(t i m) q -> m i t q", t=CH, i=GH)
                    for i in range(GH):
                        dst = qb[0:mb, par, i, CW * c:CW * c + CW]
                        sp.dma_start(dst.rearrange("m (t q) -> m t q", t=CH), src[:, i]).then_inc(m_in[par][slot], 16)

                def step(n, half_n, par, first, with_a, load2, late):
                    if load2:
                        sp.wait_ge(b_in[par], 16 * NBIN * (half_n + 1))
                        sp.sem_inc(sp_turns, 1)
                        load_max_operands(sp, n + 2, par, True)
                    if with_a:
                        copy_exp_operands(sp, n + 1, half_n + par, 1 - par, late)
                        load_values(sp, n + 1, 1 - par, late)
                    for item in step_order(True, with_a):
                        if item[0] == "O":
                            slot = item[1]
                            c = QC - 1 - slot
                            sp.wait_ge(o_ready, n * QC + slot + 1)
                            sp.sem_inc(sp_turns, 1)
                            for i in range(GH):
                                sp.dma_start(o_dram[bass.ds(n, 1), i, :, CW * c:CW * c + CW].rearrange("n r s -> (n r) s"),
                                             osum[32 * i:32 * i + HD + 1, slot, :]).then_inc(o_out[slot], 16)
                        elif item[0] == "T":
                            rows_of_maxima(n + 1, 1 - par, item[1], late)
                        elif item[0] == "L":
                            rows_of_maxima(n, par, item[1], not first)

                copy_exp_operands(sp, 0, 0, 0, False)
                load_values(sp, 0, 0, False)
                load_max_operands(sp, 1, 1, False)
                sp.dma_start(w["bob"][:, :], bo.partition_broadcast(P)).then_inc(bob_in, 16)
                for item in step_order(False, True):
                    if item[0] == "T":
                        rows_of_maxima(0, 0, item[1], False)
                step(0, 0, 0, True, True, True, False)
                step(1, 0, 1, True, True, True, True)
                with sp.Fori(1, NG // 2 - 1) as it:
                    step(2 * it, it, 0, False, True, True, True)
                    step(2 * it + 1, it, 1, False, True, True, True)
                for slot in range(QC):
                    sp.wait_ge(o_out[slot], 16 * GH * (NG - GH))
                for b in range(B - 1):
                    load_sums(sp, b)
                step(NG - 2, NG // 2 - 1, 0, False, True, False, True)
                step(NG - 1, NG // 2 - 1, 1, False, False, False, True)
                for slot in range(QC):
                    sp.wait_ge(o_out[slot], 16 * GH * NG)
                load_sums(sp, B - 1)

            @block.tensor
            def _(pe):
                pe.wait_ge(v_ready, CHUNKS)
                pe.wait_ge(hi_ready, 2 * CHUNKS)
                pe.wait_ge(krows_in, 16 * 2 * GH)
                pe.wait_ge(const_in, 16 * NCONST)

                def max_scores(n, par, half_n, k, ready):
                    slot, t, heads = MAXUNITS[k]
                    if k == 0:
                        pe.wait_ge(a_in[par], 16 * NA * (half_n + 1))
                    if not ready or k >= 2:
                        pe.wait_ge(a_max, n * NM + k - 1)
                    w = P * (t + 1)
                    for j, i in enumerate(heads):
                        for f in range(0, w, CW):
                            e = min(w, f + CW)
                            last = nc.tensor.matmul(psA[k % 2][:, CW * j + f:CW * j + e], qa[:, par, i, P * t:P * t + P],
                                                    ka[:, par, i, f:e], start=True, stop=True)
                    last.then_inc(a_scores, 1)

                def bank_free(n, use):
                    bank, user, in_last = use
                    if user is None:
                        return
                    group = n - 1 if in_last else n
                    if user[0] == "S":
                        pe.wait_ge(exp_ready, group * NE + user[1] + 1)
                    else:
                        pe.wait_ge(mrows_ready, (group + (user[0] == "T")) * QC + user[1] + 1)

                def turn_maxima(n, slot, use, group):
                    bank_free(group, use)
                    pe.wait_ge(mparts_ready, n * QC + slot + 1)
                    pe.sem_inc(pe_turns, 1)
                    nc.tensor.transpose(psS[use[0]][0:CH * GH * 3, :].bitcast(BF16)[:, 0:P],
                                        mparts[:, slot, :, :, :].rearrange("p t i m -> p (t i m)"),
                                        identb[:, :]).then_inc(mt_psum, 1)

                def scores(n, par, half_n, k, use):
                    u, i0, nh = EXPS[k]
                    slot, c, kb, q0, w, diag = UNITS[u]
                    if k == 0:
                        pe.wait_ge(b_in[par], 16 * NBIN * (half_n + 1))
                    if u in FIRST and i0 == 0:
                        pe.wait_ge(m_in[par][slot], 16 * GH * (half_n + 1))
                    bank_free(n, use)
                    for j in range(nh):
                        i = i0 + j
                        guard = diag and steep(par, i)
                        last = nc.tensor.matmul(psS[use[0]][:, w * j:w * j + w], kb_[:, par, i, P * kb:P * kb + P],
                                                qb[:, par, i, CW * c + q0:CW * c + q0 + w], start=True, stop=not guard)
                        if guard:
                            last = nc.tensor.matmul(psS[use[0]][:, w * j:w * j + P], identb[:, :], guards[:, :],
                                                    start=False, stop=True)
                    last.then_inc(s_scores, 1)

                def weighted_sums(n, par, u, first):
                    slot, c, kb, q0, w, diag = UNITS[u]
                    pe.wait_ge(exp_ready, n * NE + EXPS_TO[u])
                    if diag:
                        pe.wait_ge(masked, n * len(DIAG) + DIAG.index(u) + 1)
                    if first and u == 0:
                        pe.wait_ge(o_clear, 1)
                    if u in FIRST and not (first and slot == 0):
                        pe.wait_ge(o_ready, n * QC + slot)
                    for i in range(GH):
                        last = nc.tensor.matmul(psO[32 * i:32 * i + HD + 1, q0:q0 + w], vb[:, par, kb, i, :],
                                                probs[:, u % 3, i, 0:w], start=u in FIRST, stop=u in LAST,
                                                tile_position=(0, 32 * i))
                    last.then_inc(pv_done, 1)

                def step(n, half_n, par, first, with_a, half_next=None):
                    order = step_order(True, with_a)
                    use = banks_of(order, step_order(not first, True))
                    for item in order:
                        if item[0] == "A":
                            max_scores(n + 1, 1 - par, half_next, item[1], False)
                        elif item[0] == "T":
                            turn_maxima(n + 1, item[1], use[item], n)
                        elif item[0] == "L":
                            turn_maxima(n, item[1], use[item], n)
                        elif item[0] == "S":
                            scores(n, par, half_n, item[1], use[item])
                        elif item[0] == "V":
                            weighted_sums(n, par, item[1], first)

                order = step_order(False, True)
                use = banks_of(order, [])
                for item in order:
                    if item[0] == "A":
                        max_scores(0, 0, 0, item[1], True)
                    elif item[0] == "T":
                        turn_maxima(0, item[1], use[item], 0)
                step(0, 0, 0, True, True, 0)
                step(1, 0, 1, False, True, 1)
                with pe.Fori(1, NG // 2 - 1) as it:
                    step(2 * it, it, 0, False, True, it)
                    step(2 * it + 1, it, 1, False, True, it + 1)
                step(NG - 2, NG // 2 - 1, 0, False, True, NG // 2 - 1)
                step(NG - 1, NG // 2 - 1, 1, False, False)

            @block.vector
            def _(dve):
                dve.wait_ge(const_in, 16 * NCONST)
                dve.wait_ge(hi_ready, 2 * CHUNKS)
                nc.vector.memset(psO, 0.0).then_inc(o_clear, 1)

                def row_max(n, par, k):
                    slot, t, heads = MAXUNITS[k]
                    w = P * (t + 1)
                    dve.wait_ge(a_scores, n * NM + k + 1)
                    dve.sem_inc(dve_turns, 1)
                    for j, i in enumerate(heads):
                        last = nc.vector.tensor_tensor_reduce(
                            out=junk[:, k % 2, CW * j:CW * j + w], in0=psA[k % 2][:, CW * j:CW * j + w],
                            in1=cmask[:, S - w:S], scale=1.0, scalar=FILL, op0=ALU.add, op1=ALU.max,
                            accum_out=mx[:, par, t * GH + i:t * GH + i + 1])
                    last.then_inc(a_max, 1)

                def cut_maxima(n, par, slot, first):
                    c = QC - 1 - slot
                    done = (n * QC + slot) * 3
                    m = mx[:, par, CH * GH * c:CH * GH * (c + 1)]
                    part = mparts[:, slot, :, :, :].rearrange("p t i m -> p (t i) m")
                    dve.wait_ge(a_max, n * NM + NM_SLOT[slot])
                    if not first:
                        dve.wait_ge(mt_psum, (n - 1) * QC + slot + 1)
                    nc.vector.tensor_scalar_mul(part[:, :, 0], m, -1.0).then_inc(cut_chain, 1)
                    dve.wait_ge(cut_chain, done + 1)
                    nc.vector.scalar_tensor_tensor(mrest[:, slot, 0, :], m, -1.0, part[:, :, 0],
                                                   ALU.mult, ALU.subtract).then_inc(cut_chain, 1)
                    dve.wait_ge(cut_chain, done + 2)
                    nc.vector.tensor_copy(part[:, :, 1], mrest[:, slot, 0, :]).then_inc(cut_chain, 1)
                    dve.wait_ge(cut_chain, done + 3)
                    nc.vector.tensor_tensor(part[:, :, 2], mrest[:, slot, 0, :], part[:, :, 1],
                                            ALU.subtract).then_inc(mparts_ready, 1)

                def step(n, par, first, order):
                    for item in order:
                        if item[0] == "A":
                            row_max(n, par, item[1])
                        elif item[0] == "F":
                            cut_maxima(n, par, item[1], first)

                step(0, 0, True, step_order(False, True))
                step(1, 1, False, step_order(True, True))
                step(2, 0, False, step_order(True, True))
                with dve.Fori(1, NG // 2 - 1) as it:
                    step(2 * it + 1, 1, False, step_order(True, True))
                    step(2 * it + 2, 0, False, step_order(True, True))
                step(NG - 1, 1, False, step_order(True, True))
                for b in range(B - 1):
                    dve.wait_ge(o_in[b], 32)
                    nc.vector.reciprocal(den[:, b, :], den[:, b, :]).then_inc(rden_ready, 1)

            @block.scalar
            def _(act):
                def exps(n, k, bank, first):
                    u, i0, nh = EXPS[k]
                    w = UNITS[u][4]
                    if i0 == 0 and (not first or u >= 3):
                        act.wait_ge(pv_done, n * NU + u - 2)
                    act.wait_ge(s_scores, n * NE + k + 1)
                    nc.scalar.activation(probs[:, u % 3, i0:i0 + nh, 0:w],
                                         psS[bank][:, 0:nh * w].rearrange("p (i q) -> p i q", i=nh),
                                         ACT.Exp).then_inc(exp_ready, 1)

                def maxima_rows(n, par, half_last, slot, bank, first):
                    act.wait_ge(mt_psum, n * QC + slot + 1)
                    if not first:
                        act.wait_ge(m_out[slot], 16 * n)
                    nc.scalar.copy(mrows[:, slot, :], psS[bank][0:CH * GH * 3, :].bitcast(BF16)[:, 0:P]).then_inc(mrows_ready, 1)
                    act.wait_ge(mrows_ready, n * QC + slot + 1)
                    if not first:
                        act.wait_ge(m_in[1 - par][slot], 16 * GH * (half_last + 1))
                    act.dma_start(m_dram[slot], mrows[:, slot, :]).then_inc(m_out[slot], 16)

                def sums_out(n, slot, first):
                    act.wait_ge(pv_done, n * NU + LAST[slot] + 1)
                    if not first:
                        act.wait_ge(o_out[slot], 16 * GH * n)
                    nc.scalar.copy(osum[:, slot, :], psO).then_inc(o_ready, 1)

                def step(n, par, half_n, first, with_a):
                    order = step_order(True, with_a)
                    use = banks_of(order, [])
                    for item in order:
                        if item[0] == "S":
                            exps(n, item[1], use[item][0], first)
                        elif item[0] == "T":
                            maxima_rows(n + 1, 1 - par, half_n, item[1], use[item][0], False)
                        elif item[0] == "L":
                            maxima_rows(n, par, half_n - 1 + par, item[1], use[item][0], first)
                        elif item[0] == "O":
                            sums_out(n, item[1], first)

                load_later_weights(act)
                for item, use in banks_of(step_order(False, True), []).items():
                    maxima_rows(0, 0, 0, item[1], use[0], True)
                step(0, 0, 0, True, True)
                step(1, 1, 0, False, True)
                with act.Fori(1, NG // 2 - 1) as it:
                    step(2 * it, 0, it, False, True)
                    step(2 * it + 1, 1, it, False, True)
                step(NG - 2, 0, NG // 2 - 1, False, True)
                step(NG - 1, 1, NG // 2 - 1, False, False)

            @block.gpsimd
            def _(pool):
                def mask(n, u):
                    pool.wait_ge(exp_ready, n * NE + EXPS_TO[u])
                    pool.sem_inc(pool_turns, 1)
                    tri = probs[:, u % 3, :, 0:P]
                    nc.gpsimd.affine_select(out=tri, in_=tri, compare_op=ALU.is_ge, fill=0.0, base=0,
                                            pattern=[[0, GH], [1, P]], channel_multiplier=-1).then_inc(masked, 1)

                pool.wait_ge(xres_in, 16 * B)
                pool.wait_ge(bob_in, 16)
                for j in range(CHUNKS):
                    rows = x_res[:, CH * j:CH * j + CH, :]
                    nc.gpsimd.tensor_tensor(rows, rows, w["bob"][:, :].unsqueeze(1).to_broadcast([P, CH, D]),
                                            ALU.add).then_inc(xb_ready, 1)
                for u in DIAG:
                    mask(0, u)
                with pool.Fori(1, NG) as n:
                    for u in DIAG:
                        mask(n, u)

        later_stages(nc, ctx, sb, sem, w, dict(
            x_res=x_res, ot=ot, den=den, ident=ident, half_pow=half_pow, half=half, banks=[b0, b1_, b2_, b3],
            wts_in=wts_in, o_in=o_in, xb_ready=xb_ready, rden_ready=rden_ready, n_later=NLATER,
            identb=identb), out)


def later_stages(nc, ctx, sb, sem, w, shared, out):
    x_res, ot, den, ident, half_pow, half, banks = (
        shared[k] for k in ("x_res", "ot", "den", "ident", "half_pow", "half", "banks"))
    wts_in, o_in, xb_ready, rden_ready, n_later, identb = (
        shared[k] for k in ("wts_in", "o_in", "xb_ready", "rden_ready", "n_later", "identb"))
    wo, wr, brb, rank, sel, incl, same, less = (
        w[k] for k in ("wo", "wr", "brb", "rank", "sel", "incl", "same", "less"))
    big, samet, w1, w2, b1c, b2r, w1q, w1k, wf, dis = (
        w[k] for k in ("big", "samet", "w1", "w2", "b1c", "b2r", "w1q", "w1k", "wf", "dis"))
    aqk = sb("aqk", [P, D])
    wft = sb("wft", [P, D])

    at = sb("at", [P, 2, CH, P])
    xn2 = sb("xn2", [P, TILES, D])
    xt2 = sb("xt2", [P, 2, CW])
    stats = sb("stats1", [P, CH, 6])
    SPANS = [(0, 4), (4, 6), (6, 8)]
    span_of = {j: h for h, (a, z) in enumerate(SPANS) for j in range(a, z)}
    stats2, mv2 = sb("stats2", [P, TILES, 6]), sb("mv2", [P, TILES, 2])
    ve2, rs2, nt2 = sb("ve2", [P, TILES]), sb("rs2", [P, TILES]), sb("nt2", [P, 3, TILES])
    mv = sb("mv1", [P, CH, 2])
    ve, rs = sb("ve1", [P, CH]), sb("rs1", [P, CH])
    nt = sb("nt1", [P, 2, CH])
    lg = sb("lg", [P, TILES, E])
    ex = sb("ex", [P, TILES, E])
    hot = sb("hot", [P, TILES, E])
    hotb = sb("hotb", [P, TILES, E], BF16)
    cnt = sb("cnt", [P, 2, TILES, E])
    pos = sb("pos", [P, TILES, E])
    col = sb("col", [P, 4, TILES])
    tot = sb("tot", [P, E])
    gate = sb("gate", [P, TILES])
    hott = sb("hott", [E, 2, CW])
    noth = sb("noth", [E, 2, CW], BF16)
    xg = sb("xg", [P, 2, CH, D])
    xgt = sb("xgt", [P, 2, CW])
    hid = sb("hid", [P, 3, CW])
    xe = sb("xe", [P, 2, CH, D + 4])
    xt3 = sb("xt3", [P, CW])
    ut = sb("ut", [P, CW])
    th = sb("th", [P, CH, P])
    ee = sb("ee", [P, CH, P])
    inv = sb("inv", [P, CH])
    xn4 = sb("xn4", [P, CH, D])
    xt4 = sb("xt4", [P, CW])
    res = sb("res", [P, 2, CH, D])

    res_out = [sem(f"res_out{i}") for i in range(2)]
    v_chain = sem("v_chain")
    ve2_ready, pw2_ready, stats_ready, scales_ready = (sem(n) for n in ("ve2_ready", "pw2_ready", "stats_ready", "scales_ready"))
    rb_psum, at_ready, proj_psum, x1_ready = (sem(n) for n in ("rb_psum", "at_ready", "proj_psum", "x1_ready"))
    ve_ready, pw_ready = sem("ve_ready"), sem("pw_ready")
    t2_psum, xt2_ready, lg_psum, lg_ready, ex_ready = (sem(n) for n in ("t2_psum", "xt2_ready", "lg_psum", "lg_ready", "ex_ready"))
    mx_ready, hot_ready, cnt_psum, gate_ready = sem("mx_ready"), sem("hot_ready"), sem("cnt_psum"), sem("gate_ready")
    xg_ready, g_psum, xgt_ready, hott_ready = (sem(n) for n in ("xg_ready", "g_psum", "xgt_ready", "hott_ready"))
    ht_psum = sem("ht_psum")
    z_psum, hid_ready, y_psum, x2_ready = (sem(n) for n in ("z_psum", "hid_ready", "y_psum", "x2_ready"))
    fold_psum, fold_ready = sem("fold_psum"), sem("fold_ready")
    xe_ready, t3_psum, xt3_ready, u_psum, ut_ready = (sem(n) for n in ("xe_ready", "t3_psum", "xt3_ready", "u_psum", "ut_ready"))
    s_psum, th_ready, ee_ready, em_ready, mix_psum, x3_ready = (sem(n) for n in ("s_psum", "th_ready", "ee_ready", "em_ready", "mix_psum", "x3_ready"))
    xn4_ready, t4_psum, xt4_ready, f_psum, res_ready = (sem(n) for n in ("xn4_ready", "t4_psum", "xt4_ready", "f_psum", "res_ready"))

    psRb, psProj, psT2, psLg = [half[0], half[1]], [banks[0], banks[1]], [half[2], banks[2]], half[3]
    psFold = banks[3]
    psZ = [banks[0], banks[1]]
    psY = banks[2]
    psG = banks[3]
    psT3, psU, psS = half[0], half[1], half[0]
    psMix = [half[2], half[3]]
    psOut = half[3]

    BY_DVE = (2, 3, 5, 7)
    BY_ACT = (0, 1, 4, 6)
    xn2_by_dve, xn2_by_act = sem("xn2_by_dve"), sem("xn2_by_act")

    SLOTS = {"t3": 4, "u": 5, "s": 6, "mask": 10, "mix": 11, "t4": 14, "f": 15}

    def slots():
        for n in range((CHUNKS + 1) * E + max(SLOTS.values())):
            due = [(name, (n - E - at) // E) for name, at in SLOTS.items()
                   if n >= E + at and (n - E - at) % E == 0 and (n - E - at) // E < CHUNKS]
            yield (n // E, n % E) if n < CHUNKS * E else None, due

    block = ctx.enter_context(nc.Block())

    @block.sync
    def _(sp):
        for j in range(CHUNKS):
            sp.wait_ge(res_ready, j + 1)
            for s in range(B):
                dst = out[s].rearrange("(u t) d -> t u d", t=32)[:, CH * j:CH * j + CH, :]
                sp.dma_start(dst, res[32 * s:32 * s + 32, j % 2, :, :]).then_inc(res_out[j % 2], 16)
        for i in range(2):
            sp.wait_ge(res_out[i], 16 * B * CHUNKS // 2)

    @block.gpsimd
    def _(pool):
        for h, (a, z) in enumerate(SPANS):
            pool.wait_ge(ve2_ready, h + 1)
            c = slice(CH * a, CH * z)
            nc.gpsimd.tensor_tensor(rs2[:, c], ve2[:, c], half_pow[:, 0:CH * (z - a)], ALU.pow).then_inc(pw2_ready, 1)
        for k in range(2 * CHUNKS):
            pool.wait_ge(ve_ready, k + 1)
            nc.gpsimd.tensor_tensor(rs[:, :], ve[:, :], half_pow[:, 0:CH], ALU.pow).then_inc(pw_ready, 1)

    @block.vector
    def _(dve):
        chain = [0]
        norms = [0]

        def link(ins):
            chain[0] += 1
            ins.then_inc(v_chain, 1)
            dve.wait_ge(v_chain, chain[0])

        def norm(src, dst):
            for i in range(CH):
                last = nc.vector.bn_stats(stats[:, i, :], src(i))
            link(last)
            for i in range(CH):
                last = nc.vector.bn_aggr(mv[:, i, :], stats[:, i, :])
            link(last)
            nc.vector.tensor_scalar_add(ve[:, :], mv[:, :, 1], EPS).then_inc(ve_ready, 1)
            norms[0] += 1
            dve.wait_ge(pw_ready, norms[0])
            link(nc.vector.scalar_tensor_tensor(nt[:, 0, :], ve[:, :], -0.5, rs[:, :], ALU.mult, ALU.mult))
            link(nc.vector.tensor_tensor(nt[:, 1, :], nt[:, 0, :], rs[:, :], ALU.mult))
            link(nc.vector.scalar_tensor_tensor(nt[:, 0, :], nt[:, 1, :], 1.5, rs[:, :], ALU.add, ALU.mult))
            for i in range(CH):
                last = nc.vector.tensor_scalar(dst(i), src(i), mv[:, i, 0:1], nt[:, 0, i:i + 1], ALU.subtract, ALU.mult)
            return last

        dve.wait_ge(o_in[B - 1], 32)
        nc.vector.reciprocal(den[:, B - 1, :], den[:, B - 1, :]).then_inc(rden_ready, 1)

        def divide(j):
            dve.wait_ge(rb_psum, j + 1)
            if j >= 2:
                dve.wait_ge(proj_psum, j - 1)
            nc.vector.tensor_tensor(at[:, j % 2, :, :].rearrange("p i (s t) -> p s i t", s=B),
                                    ot[:, :, P * j:P * j + P].rearrange("p s (i t) -> p s i t", t=32),
                                    psRb[j % 2].rearrange("p (s i t) -> p s i t", s=B, i=CH), ALU.mult).then_inc(at_ready, 1)

        def add(j):
            dve.wait_ge(proj_psum, j + 1)
            if j == 0:
                dve.wait_ge(xb_ready, CHUNKS)
            rows = x_res[:, CH * j:CH * j + CH, :]
            nc.vector.tensor_tensor(rows, rows, psProj[j % 2].rearrange("p (i d) -> p i d", i=CH), ALU.add).then_inc(x1_ready, 1)
            dve.wait_ge(x1_ready, j + 1)
            for i in range(CH):
                last = nc.vector.bn_stats(stats2[:, CH * j + i, :], x_res[:, CH * j + i, :])
            last.then_inc(stats_ready, 1)

        def variance(h):
            a, z = SPANS[h]
            dve.wait_ge(stats_ready, z)
            for u in range(CH * a, CH * z):
                last = nc.vector.bn_aggr(mv2[:, u, :], stats2[:, u, :])
            link(last)
            nc.vector.tensor_scalar_add(ve2[:, CH * a:CH * z], mv2[:, CH * a:CH * z, 1], EPS).then_inc(ve2_ready, 1)

        def scales(h):
            c = slice(CH * SPANS[h][0], CH * SPANS[h][1])
            dve.wait_ge(pw2_ready, h + 1)
            link(nc.vector.scalar_tensor_tensor(nt2[:, 0, c], ve2[:, c], -0.5, rs2[:, c], ALU.mult, ALU.mult))
            link(nc.vector.tensor_tensor(nt2[:, 1, c], nt2[:, 0, c], rs2[:, c], ALU.mult))
            link(nc.vector.scalar_tensor_tensor(rs2[:, c], nt2[:, 1, c], 1.5, rs2[:, c], ALU.add, ALU.mult))
            nc.vector.scalar_tensor_tensor(nt2[:, 2, c], mv2[:, c, 0], -1.0, rs2[:, c],
                                           ALU.mult, ALU.mult).then_inc(scales_ready, 1)

        def apply(j):
            dve.wait_ge(scales_ready, span_of[j] + 1)
            for u in range(CH * j, CH * j + CH):
                last = nc.vector.tensor_scalar(xn2[:, u, :], x_res[:, u, :], rs2[:, u:u + 1], nt2[:, 2, u:u + 1],
                                               ALU.mult, ALU.add)
            last.then_inc(xn2_by_dve, 1)

        divide(0)
        for j in range(CHUNKS):
            if j + 1 < CHUNKS:
                divide(j + 1)
            add(j)
            if j == 3:
                variance(0)
            if j == 4:
                scales(0)
            if j == 5:
                apply(2)
                variance(1)
            if j == 6:
                scales(1)
        variance(2)
        apply(3)
        apply(5)
        scales(2)
        apply(7)

        dve.wait_ge(lg_psum, CHUNKS)
        dve.wait_ge(wts_in, 16 * n_later)
        bc = lambda a: a.unsqueeze(2).to_broadcast([P, TILES, E])
        link(nc.vector.tensor_tensor(lg[:, :, :], psLg.rearrange("p (u e) -> p u e", e=E)[:, 0:TILES, :],
                                     brb[:, :].unsqueeze(1).to_broadcast([P, TILES, E]), ALU.add))
        link(nc.vector.tensor_reduce(col[:, 0, :], lg[:, :, :], AX.X, ALU.max))
        nc.vector.tensor_tensor(lg[:, :, :], lg[:, :, :], bc(col[:, 0, :]), ALU.subtract).then_inc(mx_ready, 1)
        dve.wait_ge(mx_ready, 1)
        link(nc.vector.tensor_scalar(hot[:, :, :], lg[:, :, :], 0.0, None, ALU.is_equal))
        link(nc.vector.tensor_tensor(hot[:, :, :], hot[:, :, :], rank[:, :].unsqueeze(1).to_broadcast([P, TILES, E]), ALU.mult))
        link(nc.vector.tensor_reduce(col[:, 1, :], hot[:, :, :], AX.X, ALU.max))
        link(nc.vector.tensor_tensor(hot[:, :, :], hot[:, :, :], bc(col[:, 1, :]), ALU.is_equal))
        nc.vector.tensor_copy(hotb[:, :, :], hot[:, :, :]).then_inc(hot_ready, 1)
        dve.wait_ge(ex_ready, 1)
        link(nc.vector.tensor_reduce(col[:, 2, :], ex[:, :, :], AX.X, ALU.add))
        link(nc.vector.reciprocal(col[:, 3, :], col[:, 2, :]))
        dve.wait_ge(cnt_psum, 1)
        cview = psZ[0].rearrange("p (k u e) -> p k u e", k=2, e=E)
        link(nc.vector.tensor_copy(cnt[:, 0, :, :], cview[:, 1]))
        link(nc.vector.tensor_tensor(pos[:, :, :], cview[:, 0], cnt[:, 0, :, :], ALU.subtract))
        cur, step = 0, 1
        while step < TILES:
            nc.vector.tensor_copy(cnt[:, 1 - cur, 0:step, :], cnt[:, cur, 0:step, :])
            link(nc.vector.tensor_tensor(cnt[:, 1 - cur, step:, :], cnt[:, cur, step:, :], cnt[:, cur, 0:TILES - step, :], ALU.add))
            cur, step = 1 - cur, 2 * step
        link(nc.vector.tensor_tensor(pos[:, :, :], pos[:, :, :], cnt[:, cur, :, :], ALU.add))
        link(nc.vector.tensor_reduce(tot[:, :], psY.rearrange("p (k u e) -> p k e u", k=2, e=E)[:, 0], AX.X, ALU.add))
        link(nc.vector.tensor_tensor(pos[:, :, :], pos[:, :, :], tot[:, :].unsqueeze(1).to_broadcast([P, TILES, E]), ALU.add))
        link(nc.vector.tensor_scalar(pos[:, :, :], pos[:, :, :], float(CAP), None, ALU.is_lt))
        link(nc.vector.tensor_tensor(pos[:, :, :], pos[:, :, :], hot[:, :, :], ALU.mult))
        link(nc.vector.tensor_reduce(col[:, 0, :], pos[:, :, :], AX.X, ALU.max))
        nc.vector.tensor_tensor(gate[:, :], col[:, 0, :], col[:, 3, :], ALU.mult).then_inc(gate_ready, 1)
        dve.wait_ge(gate_ready, 1)
        dve.wait_ge(fold_psum, 1)
        nc.vector.tensor_copy(aqk[:, :], psFold[:, 0:P])
        nc.vector.tensor_tensor(wft[:, :], psFold[:, P:2 * P], dis[:, :], ALU.add).then_inc(fold_ready, 1)

        def gated(j):
            if j >= 2:
                dve.wait_ge(g_psum, j - 1)
            for i in range(CH):
                last = nc.vector.tensor_scalar(xg[:, j % 2, i, :], xn2[:, CH * j + i, :], gate[:, CH * j + i:CH * j + i + 1],
                                               None, ALU.mult)
            last.then_inc(xg_ready, 1)

        def moe_out(j):
            dve.wait_ge(y_psum, j + 1)
            for i in range(CH):
                u = CH * j + i
                last = nc.vector.scalar_tensor_tensor(x_res[:, u, :], psY[:, P * i:P * i + P], gate[:, u:u + 1],
                                                      x_res[:, u, :], ALU.mult, ALU.add)
            last.then_inc(x2_ready, 1)
            dve.wait_ge(x2_ready, j + 1)
            last = norm(lambda i: x_res[:, CH * j + i, :], lambda i: xe[:, j % 2, i, 0:D])
            last.then_inc(xe_ready, 1)

        nc.vector.memset(xe[:, :, :, D:D + 1], 1.0)
        gated(0)
        gated(1)
        for expert, due in slots():
            for name, j in due:
                if name == "mask":
                    dve.wait_ge(ee_ready, j + 1)
                    nc.vector.tensor_tensor(ee[:, :, :], ee[:, :, :], samet[:, :].unsqueeze(1).to_broadcast([P, CH, P]),
                                            ALU.mult).then_inc(em_ready, 1)
                if name == "mix":
                    dve.wait_ge(mix_psum, j + 1)
                    for k in range(2):
                        v = psMix[k].rearrange("p (i c) -> p i c", i=2)
                        last = nc.vector.reciprocal(inv[:, 2 * k:2 * k + 2], v[:, :, D])
                    link(last)
                    for i in range(CH):
                        u = CH * j + i
                        c0 = (i % 2) * (CW // 2)
                        last = nc.vector.scalar_tensor_tensor(x_res[:, u, :], psMix[i // 2][:, c0:c0 + D], inv[:, i:i + 1],
                                                              x_res[:, u, :], ALU.mult, ALU.add)
                    last.then_inc(x3_ready, 1)
                    dve.wait_ge(x3_ready, j + 1)
                    if j >= 1:
                        dve.wait_ge(t4_psum, j)
                    norm(lambda i: x_res[:, CH * j + i, :], lambda i: xn4[:, i, :]).then_inc(xn4_ready, 1)
                if name == "f":
                    dve.wait_ge(f_psum, j + 1)
                    if j >= 2:
                        dve.wait_ge(res_out[j % 2], 16 * B * (j // 2))
                    nc.vector.tensor_tensor(res[:, j % 2, :, :], x_res[:, CH * j:CH * j + CH, :],
                                            psOut.rearrange("p (i d) -> p i d", i=CH), ALU.add).then_inc(res_ready, 1)
            if expert and expert[1] == E - 1:
                j = expert[0]
                moe_out(j)
                if j + 2 < CHUNKS:
                    gated(j + 2)

    @block.tensor
    def _(pe):
        pe.wait_ge(wts_in, 16 * n_later)

        def reciprocals(j):
            if j >= 2:
                pe.wait_ge(at_ready, j - 1)
            nc.tensor.matmul(psRb[j % 2], sel[:, j, :], den[:, :, :].rearrange("p s q -> p (s q)"),
                             start=True, stop=True).then_inc(rb_psum, 1)

        def project(j):
            pe.wait_ge(at_ready, j + 1)
            if j >= 2:
                pe.wait_ge(x1_ready, j - 1)
            for i in range(CH):
                last = nc.tensor.matmul(psProj[j % 2][:, P * i:P * i + P], at[:, j % 2, i, :], wo[:, :], start=True, stop=True)
            last.then_inc(proj_psum, 1)

        def turned(j):
            if j in BY_DVE:
                pe.wait_ge(xn2_by_dve, BY_DVE.index(j) + 1)
            else:
                pe.wait_ge(xn2_by_act, BY_ACT.index(j) + 1)
            if j >= 2:
                pe.wait_ge(xt2_ready, j - 1)
            for i in range(CH):
                last = nc.tensor.transpose(psT2[j % 2][:, P * i:P * i + P], xn2[:, CH * j + i, :], ident[:, :])
            last.then_inc(t2_psum, 1)

        def logits(j):
            pe.wait_ge(xt2_ready, j + 1)
            for i in range(CH):
                u = CH * j + i
                last = nc.tensor.matmul(psLg[:, E * u:E * u + E], xt2[:, j % 2, P * i:P * i + P], wr[:, :], start=True, stop=True)
            last.then_inc(lg_psum, 1)

        nc.tensor.matmul(psFold[:, 0:P], w1q[:, :], w1k[:, :], start=True, stop=True)
        nc.tensor.transpose(psFold[:, P:2 * P], wf[:, :], ident[:, :]).then_inc(fold_psum, 1)

        pe.wait_ge(rden_ready, B)
        reciprocals(0)
        for j in range(CHUNKS):
            if j + 1 < CHUNKS:
                reciprocals(j + 1)
            project(j)
            if j == 5:
                turned(0)
            if j == 6:
                turned(1)
                logits(0)
        for j in range(1, CHUNKS):
            if j + 1 < CHUNKS:
                turned(j + 1)
            logits(j)

        pe.wait_ge(hot_ready, 1)
        flat = hotb[:, :, :].rearrange("p u e -> p (u e)")
        nc.tensor.matmul(psZ[0][:, 0:TILES * E], incl[:, :], flat, start=True, stop=True)
        nc.tensor.matmul(psZ[0][:, TILES * E:2 * TILES * E], same[:, :], flat, start=True, stop=True)
        nc.tensor.matmul(psY[:, 0:TILES * E], less[:, :], flat, start=True, stop=True).then_inc(cnt_psum, 1)

        def gated_columns(j):
            pe.wait_ge(xg_ready, j + 1)
            pe.wait_ge(fold_ready, 1)
            if j >= 1:
                pe.wait_ge(hott_ready, 2 * j)
            for i in range(CH):
                last = nc.tensor.transpose(psG[:, P * i:P * i + P], xg[:, j % 2, i, :], ident[:, :])
            last.then_inc(g_psum, 1)

        def one_hot_rows(j):
            pe.wait_ge(xgt_ready, j + 1)
            for i in range(CH):
                last = nc.tensor.matmul(psG[0:E, P * i:P * i + P], hotb[:, CH * j + i, :], identb[:, :], start=True, stop=True)
            last.then_inc(ht_psum, 1)

        def expert_in(n):
            j, e = n // E, n % E
            if n >= 2:
                pe.wait_ge(hid_ready, n - 1)
            pe.wait_ge(xgt_ready, j + 1)
            pe.wait_ge(hott_ready, 2 * j + 2)
            nc.tensor.matmul(psZ[n % 2], w1[:, e, :], xgt[:, j % 2, :], start=True, stop=False)
            nc.tensor.matmul(psZ[n % 2], big[:, e, :], noth[:, j % 2, :], start=False, stop=True).then_inc(z_psum, 1)

        def expert_out(n):
            j, e = n // E, n % E
            if e == 0 and j >= 1:
                pe.wait_ge(x2_ready, j)
            pe.wait_ge(hid_ready, n + 1)
            for i in range(CH):
                nc.tensor.matmul(psY[:, P * i:P * i + P], hid[:, n % 3, P * i:P * i + P], w2[:, e, :],
                                 start=(e == 0 and i == 0), stop=False, skip_group_check=True)
            if e == E - 1:
                for i in range(CH):
                    last = nc.tensor.matmul(psY[:, P * i:P * i + P], hott[:, j % 2, P * i:P * i + P], b2r[:, :],
                                            start=False, stop=(i == CH - 1), skip_group_check=True)
                last.then_inc(y_psum, 1)

        pe.wait_ge(gate_ready, 1)
        gated_columns(0)
        one_hot_rows(0)
        expert_in(0)
        for n, (expert, due) in enumerate(slots()):
            for name, j in due:
                if name == "t3":
                    pe.wait_ge(xe_ready, j + 1)
                    if j >= 1:
                        pe.wait_ge(th_ready, j)
                    for i in range(CH):
                        last = nc.tensor.transpose(psT3[:, P * i:P * i + P], xe[:, j % 2, i, 0:D], ident[:, :])
                    last.then_inc(t3_psum, 1)
                if name == "u":
                    pe.wait_ge(xt3_ready, j + 1)
                    nc.tensor.matmul(psU, aqk[:, :], xt3[:, :], start=True, stop=True).then_inc(u_psum, 1)
                if name == "s":
                    pe.wait_ge(ut_ready, j + 1)
                    for i in range(CH):
                        last = nc.tensor.matmul(psS[:, P * i:P * i + P], xt3[:, P * i:P * i + P], ut[:, P * i:P * i + P],
                                                start=True, stop=True)
                    last.then_inc(s_psum, 1)
                if name == "mix":
                    pe.wait_ge(em_ready, j + 1)
                    if j >= 1:
                        pe.wait_ge(xt4_ready, j)
                        pe.wait_ge(res_ready, j)
                    for i in range(CH):
                        c0 = (i % 2) * (CW // 2)
                        last = nc.tensor.matmul(psMix[i // 2][:, c0:c0 + D + 1], ee[:, i, :], xe[:, j % 2, i, 0:D + 1],
                                                start=True, stop=True)
                    last.then_inc(mix_psum, 1)
                if name == "t4":
                    pe.wait_ge(xn4_ready, j + 1)
                    for i in range(CH):
                        last = nc.tensor.transpose(psMix[0][:, P * i:P * i + P], xn4[:, i, :], ident[:, :])
                    last.then_inc(t4_psum, 1)
                if name == "f":
                    pe.wait_ge(xt4_ready, j + 1)
                    for i in range(CH):
                        last = nc.tensor.matmul(psOut[:, P * i:P * i + P], xt4[:, P * i:P * i + P], wft[:, :], start=True, stop=True)
                    last.then_inc(f_psum, 1)
            if expert:
                j, e = expert
                if e == 3 and j + 1 < CHUNKS:
                    gated_columns(j + 1)
                if e == 4 and j + 1 < CHUNKS:
                    one_hot_rows(j + 1)
                if n + 1 < CHUNKS * E:
                    expert_in(n + 1)
                expert_out(n)

    @block.scalar
    def _(act):
        def columns(j):
            act.wait_ge(t2_psum, j + 1)
            if j >= 2:
                act.wait_ge(lg_psum, j - 1)
            nc.scalar.copy(xt2[:, j % 2, :], psT2[j % 2]).then_inc(xt2_ready, 1)

        def apply(j):
            act.wait_ge(scales_ready, span_of[j] + 1)
            for u in range(CH * j, CH * j + CH):
                last = nc.scalar.activation(xn2[:, u, :], x_res[:, u, :], ACT.Identity, bias=nt2[:, 2, u:u + 1],
                                            scale=rs2[:, u:u + 1])
            last.then_inc(xn2_by_act, 1)

        apply(0)
        columns(0)
        apply(1)
        columns(1)
        columns(2)
        apply(4)
        for j in range(3, 6):
            columns(j)
        apply(6)
        for j in range(6, CHUNKS):
            columns(j)
        act.wait_ge(mx_ready, 1)
        nc.scalar.activation(ex[:, :, :], lg[:, :, :], ACT.Exp).then_inc(ex_ready, 1)
        act.wait_ge(wts_in, 16 * n_later)

        def gated_columns(j):
            act.wait_ge(g_psum, j + 1)
            if j >= 2:
                act.wait_ge(z_psum, E * (j - 1))
                act.wait_ge(y_psum, j - 1)
            nc.scalar.copy(xgt[:, j % 2, :], psG).then_inc(xgt_ready, 1)

        def one_hot_rows(j):
            act.wait_ge(ht_psum, j + 1)
            nc.scalar.copy(hott[:, j % 2, :], psG[0:E, :]).then_inc(hott_ready, 1)
            nc.scalar.activation(noth[:, j % 2, :], psG[0:E, :], ACT.Copy, bias=1.0, scale=-1.0).then_inc(hott_ready, 1)

        def hidden(n):
            act.wait_ge(z_psum, n + 1)
            if n >= 3:
                j, e = (n - 2) // E, (n - 2) % E
                act.wait_ge(hid_ready, n - 2)
            e = n % E
            nc.scalar.activation(hid[:, n % 3, :], psZ[n % 2], ACT.Relu, bias=b1c[:, e:e + 1]).then_inc(hid_ready, 1)

        gated_columns(0)
        one_hot_rows(0)
        hidden(0)
        for n, (expert, due) in enumerate(slots()):
            for name, j in due:
                if name == "t3":
                    act.wait_ge(t3_psum, j + 1)
                    if j >= 1:
                        act.wait_ge(s_psum, j)
                    nc.scalar.copy(xt3[:, :], psT3).then_inc(xt3_ready, 1)
                if name == "u":
                    act.wait_ge(u_psum, j + 1)
                    nc.scalar.copy(ut[:, :], psU).then_inc(ut_ready, 1)
                if name == "s":
                    act.wait_ge(s_psum, j + 1)
                    nc.scalar.activation(th[:, :, :].rearrange("p i t -> p (i t)"), psS, ACT.Tanh,
                                         scale=1.0 / float(np.sqrt(np.float32(D)))).then_inc(th_ready, 1)
                    act.wait_ge(th_ready, j + 1)
                    if j >= 1:
                        act.wait_ge(mix_psum, j)
                    nc.scalar.activation(ee[:, :, :], th[:, :, :], ACT.Exp).then_inc(ee_ready, 1)
                if name == "t4":
                    act.wait_ge(t4_psum, j + 1)
                    if j >= 1:
                        act.wait_ge(f_psum, j)
                    nc.scalar.copy(xt4[:, :], psMix[0]).then_inc(xt4_ready, 1)
            if expert:
                j, e = expert
                if e == 3 and j + 1 < CHUNKS:
                    gated_columns(j + 1)
                if e == 4 and j + 1 < CHUNKS:
                    one_hot_rows(j + 1)
                if n + 1 < CHUNKS * E:
                    hidden(n + 1)


_INS = ["L0_attn_x", "L0_attn_Wq", "L0_attn_bq", "L0_attn_Wk", "L0_attn_bk", "L0_attn_Wv", "L0_attn_bv", "L0_attn_Wo",
        "L0_attn_bo", "L0_ffn_Wr", "L0_ffn_br", "L0_ffn_W1", "L0_ffn_b1", "L0_ffn_W2", "L0_ffn_b2", "L1_attn_Wq",
        "L1_attn_Wk", "L1_ffn_weight", "L1_ffn_disha"]


def kernel(**inputs):
    import concourse.bacc as _bacc
    from concourse.bass_utils import run_bass_kernel_spmd as _run

    nc = _bacc.Bacc("TRN2", target_bir_lowering=False, num_devices=1)
    arrays, args, consts = {}, [], {}
    for name in _INS:
        a = np.ascontiguousarray(inputs[name])
        arrays[f"in_{name}"] = a
        args.append(nc.dram_tensor(f"in_{name}", a.shape, mybir.dt.from_np(a.dtype), kind="ExternalInput").ap())
    for name, a in constants().items():
        arrays[name] = a
        consts[name] = nc.dram_tensor(name, a.shape, mybir.dt.from_np(a.dtype), kind="ExternalInput").ap()
    result = nc.dram_tensor("out_0", (B, S, D), F32, kind="ExternalOutput").ap()
    build(nc, *args, consts, result)
    return _run(nc, [arrays], core_ids=[0]).results[0]["out_0"]
```
